# Optimizing a Trainium2 kernel written in Bass

```python
import numpy as np
import jax
import jax.numpy as jnp

def _softmax(x, axis=-1):
    return jax.nn.softmax(x, axis=axis)

def _gelu(x):
    return jax.nn.gelu(x, approximate=True)

def _silu(x):
    return jax.nn.silu(x)

def _sigmoid(x):
    return jax.nn.sigmoid(x)

def _layernorm(x, axis=-1, eps=1e-05):
    m = jnp.mean(x, axis=axis, keepdims=True)
    v = jnp.var(x, axis=axis, keepdims=True)
    return (x - m) / jnp.sqrt(v + eps)

def _scatter_add(tgt, idx, src, axis=0):
    return tgt.at[idx].add(src)

def _segment_sum(src, seg, n):
    return jax.ops.segment_sum(src, seg, n)
kernel_name = 'mk_prb_d2_jaxref_r8_78e25d'

def setup_inputs(seed: int=0):
    np.random.seed(seed)
    _w = jnp.asarray

    def _L0_attn_setup():
        import jax, jax.numpy as jnp
        import numpy as np
        D = 256
        key = jax.random.key(seed)
        ks = jax.random.split(key, 5)
        scale = 1.0 / np.sqrt(D)
        x = jax.random.normal(ks[0], (4, 512, D), dtype=jnp.float32)
        Wq = jax.random.normal(ks[1], (D, D), dtype=jnp.float32) * scale
        Wk = jax.random.normal(ks[2], (D, D), dtype=jnp.float32) * scale
        Wv = jax.random.normal(ks[3], (D, D), dtype=jnp.float32) * scale
        Wo = jax.random.normal(ks[4], (D, D), dtype=jnp.float32) * scale
        return {'x': x, 'Wq': Wq, 'Wk': Wk, 'Wv': Wv, 'Wo': Wo}
    _L0_attn_in = _L0_attn_setup()

    def _L0_ffn_setup():
        import jax, jax.numpy as jnp
        import numpy as np
        HIDDEN = 256
        N_EXPERTS = 8
        N_SHARED = 2
        TOP_K = 2
        MOE_FF = 176
        SHARED_FF = N_SHARED * MOE_FF
        SCALE = 2.5
        BATCH, SEQ = (2, 128)
        key = jax.random.key(seed)
        ks = jax.random.split(key, 8)
        s = 0.02
        return {'hidden_states': jax.random.normal(ks[0], (BATCH, SEQ, HIDDEN), jnp.float32), 'gate_w': jax.random.normal(ks[1], (N_EXPERTS, HIDDEN), jnp.float32) * s, 'shared_wg': jax.random.normal(ks[2], (SHARED_FF, HIDDEN), jnp.float32) * s, 'shared_wu': jax.random.normal(ks[3], (SHARED_FF, HIDDEN), jnp.float32) * s, 'shared_wd': jax.random.normal(ks[4], (HIDDEN, SHARED_FF), jnp.float32) * s, 'exp_wg': jax.random.normal(ks[5], (N_EXPERTS, MOE_FF, HIDDEN), jnp.float32) * s, 'exp_wu': jax.random.normal(ks[6], (N_EXPERTS, MOE_FF, HIDDEN), jnp.float32) * s, 'exp_wd': jax.random.normal(ks[7], (N_EXPERTS, HIDDEN, MOE_FF), jnp.float32) * s}
    _L0_ffn_in = _L0_ffn_setup()

    def _L1_attn_setup():
        import jax, jax.numpy as jnp
        import numpy as np
        D_MODEL = 256
        N_HEADS = 16
        D_HEAD = D_MODEL // N_HEADS
        D_Q = D_MODEL // 3
        D_KV = D_MODEL // 2
        D_QK_N = D_HEAD // 2
        D_QK_R = D_HEAD // 2
        EPS = 1e-05

        def _layernorm(x, g, b):
            mu = jnp.mean(x, axis=-1, keepdims=True)
            var = jnp.var(x, axis=-1, keepdims=True)
            return (x - mu) * jax.lax.rsqrt(var + EPS) * g + b

        def _rotary(x):
            d = x.shape[-1]
            inv_freq = (1.0 / 10000.0) ** (jnp.arange(0, d, 2, dtype=jnp.float32) / d)
            t = jnp.arange(x.shape[1], dtype=jnp.float32)
            freqs = t[:, None] * inv_freq[None, :]
            cos = jnp.cos(freqs)[None, :, None, :]
            sin = jnp.sin(freqs)[None, :, None, :]
            x1, x2 = jnp.split(x, 2, axis=3)
            return jnp.concatenate([x1 * cos + x2 * sin, -x1 * sin + x2 * cos], axis=3)
        key = jax.random.key(seed)
        ks = jax.random.split(key, 16)
        s = 0.02
        inp = {'x': jax.random.normal(ks[0], (2, 256, D_MODEL), dtype=jnp.float32), 'W_d_q': jax.random.normal(ks[1], (D_Q, D_MODEL), dtype=jnp.float32) * s, 'b_d_q': jnp.zeros((D_Q,), jnp.float32), 'q_norm_g': jnp.ones((D_Q,), jnp.float32), 'q_norm_b': jnp.zeros((D_Q,), jnp.float32), 'W_u_q': jax.random.normal(ks[2], (D_MODEL, D_Q), dtype=jnp.float32) * s, 'b_u_q': jnp.zeros((D_MODEL,), jnp.float32), 'W_d_kv': jax.random.normal(ks[3], (D_KV + D_QK_R, D_MODEL), dtype=jnp.float32) * s, 'b_d_kv': jnp.zeros((D_KV + D_QK_R,), jnp.float32), 'kv_norm_g': jnp.ones((D_KV,), jnp.float32), 'kv_norm_b': jnp.zeros((D_KV,), jnp.float32), 'W_u_kv': jax.random.normal(ks[4], (D_MODEL + N_HEADS * D_QK_N, D_KV), dtype=jnp.float32) * s, 'b_u_kv': jnp.zeros((D_MODEL + N_HEADS * D_QK_N,), jnp.float32), 'W_o': jax.random.normal(ks[5], (D_MODEL, D_MODEL), dtype=jnp.float32) * s, 'b_o': jnp.zeros((D_MODEL,), jnp.float32)}
        return inp
    _L1_attn_in = _L1_attn_setup()

    def _L1_ffn_setup():
        import jax, jax.numpy as jnp
        import numpy as np
        BLOCK_SIZE = 32
        HIDDEN_SIZE = 256
        MLP_DIM = 2048
        NVFP4_LUT = jnp.array([0.0, 0.5, 1.0, 1.5, 2.0, 3.0, 4.0, 6.0, 0.0, -0.5, -1.0, -1.5, -2.0, -3.0, -4.0, -6.0], dtype=jnp.float32)

        def dequant_nvfp4(W_packed, scales, block=BLOCK_SIZE):
            N = W_packed.shape[0]
            low = W_packed & 15
            high = W_packed >> 4 & 15
            idx = jnp.stack([low, high], axis=-1).reshape(N, -1)
            vals = NVFP4_LUT[idx]
            K = vals.shape[1]
            vals = vals.reshape(N, K // block, block) * scales[:, :, None]
            return vals.reshape(N, K)
        key = jax.random.key(seed)
        ks = jax.random.split(key, 7)
        x = jax.random.normal(ks[0], (4, 32, HIDDEN_SIZE), dtype=jnp.float32)
        gate_W_packed = jax.random.randint(ks[1], (MLP_DIM, HIDDEN_SIZE // 2), 0, 32, dtype=jnp.int32)
        gate_scales = jax.random.uniform(ks[2], (MLP_DIM, HIDDEN_SIZE // BLOCK_SIZE), dtype=jnp.float32) * 0.1 + 0.001
        up_W_packed = jax.random.randint(ks[3], (MLP_DIM, HIDDEN_SIZE // 2), 0, 32, dtype=jnp.int32)
        up_scales = jax.random.uniform(ks[4], (MLP_DIM, HIDDEN_SIZE // BLOCK_SIZE), dtype=jnp.float32) * 0.1 + 0.001
        down_W_packed = jax.random.randint(ks[5], (HIDDEN_SIZE, MLP_DIM // 2), 0, 32, dtype=jnp.int32)
        down_scales = jax.random.uniform(ks[6], (HIDDEN_SIZE, MLP_DIM // BLOCK_SIZE), dtype=jnp.float32) * 0.1 + 0.001
        return {'x': x, 'gate_W_packed': gate_W_packed, 'gate_scales': gate_scales, 'up_W_packed': up_W_packed, 'up_scales': up_scales, 'down_W_packed': down_W_packed, 'down_scales': down_scales}
    _L1_ffn_in = _L1_ffn_setup()
    _d = {'L0_attn_x': _L0_attn_in['x'], 'L0_attn_Wq': _L0_attn_in['Wq'], 'L0_attn_Wk': _L0_attn_in['Wk'], 'L0_attn_Wv': _L0_attn_in['Wv'], 'L0_attn_Wo': _L0_attn_in['Wo'], 'L0_ffn_gate_w': _L0_ffn_in['gate_w'], 'L0_ffn_shared_wg': _L0_ffn_in['shared_wg'], 'L0_ffn_shared_wu': _L0_ffn_in['shared_wu'], 'L0_ffn_shared_wd': _L0_ffn_in['shared_wd'], 'L0_ffn_exp_wg': _L0_ffn_in['exp_wg'], 'L0_ffn_exp_wu': _L0_ffn_in['exp_wu'], 'L0_ffn_exp_wd': _L0_ffn_in['exp_wd'], 'L1_attn_W_d_q': _L1_attn_in['W_d_q'], 'L1_attn_b_d_q': _L1_attn_in['b_d_q'], 'L1_attn_q_norm_g': _L1_attn_in['q_norm_g'], 'L1_attn_q_norm_b': _L1_attn_in['q_norm_b'], 'L1_attn_W_u_q': _L1_attn_in['W_u_q'], 'L1_attn_b_u_q': _L1_attn_in['b_u_q'], 'L1_attn_W_d_kv': _L1_attn_in['W_d_kv'], 'L1_attn_b_d_kv': _L1_attn_in['b_d_kv'], 'L1_attn_kv_norm_g': _L1_attn_in['kv_norm_g'], 'L1_attn_kv_norm_b': _L1_attn_in['kv_norm_b'], 'L1_attn_W_u_kv': _L1_attn_in['W_u_kv'], 'L1_attn_b_u_kv': _L1_attn_in['b_u_kv'], 'L1_attn_W_o': _L1_attn_in['W_o'], 'L1_attn_b_o': _L1_attn_in['b_o'], 'L1_ffn_gate_W_packed': _L1_ffn_in['gate_W_packed'], 'L1_ffn_gate_scales': _L1_ffn_in['gate_scales'], 'L1_ffn_up_W_packed': _L1_ffn_in['up_W_packed'], 'L1_ffn_up_scales': _L1_ffn_in['up_scales'], 'L1_ffn_down_W_packed': _L1_ffn_in['down_W_packed'], 'L1_ffn_down_scales': _L1_ffn_in['down_scales']}
    _x0 = _d['L0_attn_x']
    _d['L0_attn_x'] = jax.random.normal(jax.random.fold_in(jax.random.key(seed), 1), (8, 256, 256), dtype=_x0.dtype)
    del _x0
    return _d

def reference(L0_attn_x, L0_attn_Wq, L0_attn_Wk, L0_attn_Wv, L0_attn_Wo, L0_ffn_gate_w, L0_ffn_shared_wg, L0_ffn_shared_wu, L0_ffn_shared_wd, L0_ffn_exp_wg, L0_ffn_exp_wu, L0_ffn_exp_wd, L1_attn_W_d_q, L1_attn_b_d_q, L1_attn_q_norm_g, L1_attn_q_norm_b, L1_attn_W_u_q, L1_attn_b_u_q, L1_attn_W_d_kv, L1_attn_b_d_kv, L1_attn_kv_norm_g, L1_attn_kv_norm_b, L1_attn_W_u_kv, L1_attn_b_u_kv, L1_attn_W_o, L1_attn_b_o, L1_ffn_gate_W_packed, L1_ffn_gate_scales, L1_ffn_up_W_packed, L1_ffn_up_scales, L1_ffn_down_W_packed, L1_ffn_down_scales):

    def _L0_attn_ref(x, Wq, Wk, Wv, Wo):
        import jax, jax.numpy as jnp
        import numpy as np
        D = 256
        q = jnp.einsum('bsd,ed->bse', x, Wq)
        k = jnp.einsum('bsd,ed->bse', x, Wk)
        v = jnp.einsum('bsd,ed->bse', x, Wv)
        seq = x.shape[-2]
        denom = jnp.sqrt(jnp.float32(x.shape[-1])) / seq
        kvt = jnp.cumsum(k * v, axis=-2) * denom
        vhat = q * kvt
        return jnp.einsum('bse,fe->bsf', vhat, Wo)

    def _L0_ffn_ref(hidden_states, gate_w, shared_wg, shared_wu, shared_wd, exp_wg, exp_wu, exp_wd):
        import jax, jax.numpy as jnp
        import numpy as np
        HIDDEN = 256
        N_EXPERTS = 8
        N_SHARED = 2
        TOP_K = 2
        MOE_FF = 176
        SHARED_FF = N_SHARED * MOE_FF
        SCALE = 2.5
        BATCH, SEQ = (2, 128)
        B, S, D = hidden_states.shape
        T = B * S
        xf = hidden_states.reshape(T, D)
        scores = jax.nn.sigmoid(xf @ gate_w.T)
        topk_w, topk_idx = jax.lax.top_k(scores, TOP_K)
        topk_w = topk_w / (topk_w.sum(axis=-1, keepdims=True) + 1e-20)
        topk_w = topk_w * SCALE
        shared_out = jax.nn.silu(xf @ shared_wg.T) * (xf @ shared_wu.T) @ shared_wd.T
        h = jax.nn.silu(jnp.einsum('td,efd->etf', xf, exp_wg)) * jnp.einsum('td,efd->etf', xf, exp_wu)
        all_out = jnp.einsum('etf,edf->etd', h, exp_wd)
        picked = all_out[topk_idx, jnp.arange(T)[:, None]]
        routed_out = (topk_w[..., None] * picked).sum(axis=1)
        return (shared_out + routed_out).reshape(B, S, D)

    def _L1_attn_ref(x, W_d_q, b_d_q, q_norm_g, q_norm_b, W_u_q, b_u_q, W_d_kv, b_d_kv, kv_norm_g, kv_norm_b, W_u_kv, b_u_kv, W_o, b_o):
        import jax, jax.numpy as jnp
        import numpy as np
        D_MODEL = 256
        N_HEADS = 16
        D_HEAD = D_MODEL // N_HEADS
        D_Q = D_MODEL // 3
        D_KV = D_MODEL // 2
        D_QK_N = D_HEAD // 2
        D_QK_R = D_HEAD // 2
        EPS = 1e-05

        def _layernorm(x, g, b):
            mu = jnp.mean(x, axis=-1, keepdims=True)
            var = jnp.var(x, axis=-1, keepdims=True)
            return (x - mu) * jax.lax.rsqrt(var + EPS) * g + b

        def _rotary(x):
            d = x.shape[-1]
            inv_freq = (1.0 / 10000.0) ** (jnp.arange(0, d, 2, dtype=jnp.float32) / d)
            t = jnp.arange(x.shape[1], dtype=jnp.float32)
            freqs = t[:, None] * inv_freq[None, :]
            cos = jnp.cos(freqs)[None, :, None, :]
            sin = jnp.sin(freqs)[None, :, None, :]
            x1, x2 = jnp.split(x, 2, axis=3)
            return jnp.concatenate([x1 * cos + x2 * sin, -x1 * sin + x2 * cos], axis=3)
        B, T, C = x.shape
        H, dh, dqn, dqr, dkv = (N_HEADS, D_HEAD, D_QK_N, D_QK_R, D_KV)
        c_q = _layernorm(x @ W_d_q.T + b_d_q, q_norm_g, q_norm_b)
        q = (c_q @ W_u_q.T + b_u_q).reshape(B, T, H, dh).transpose(0, 2, 1, 3)
        q_n, q_r = (q[..., :dqn], q[..., dqn:])
        q_r = _rotary(q_r)
        c_kv = x @ W_d_kv.T + b_d_kv
        kv_n = _layernorm(c_kv[..., :dkv], kv_norm_g, kv_norm_b)
        k_r = c_kv[..., dkv:]
        kv = (kv_n @ W_u_kv.T + b_u_kv).reshape(B, T, H, dh + dqn).transpose(0, 2, 1, 3)
        k_n, v = (kv[..., :dqn], kv[..., dqn:])
        k_r = k_r.reshape(B, T, 1, dqr).transpose(0, 2, 1, 3)
        k_r = _rotary(k_r)
        k_r = jnp.broadcast_to(k_r, (B, H, T, dqr))
        q_full = jnp.concatenate([q_n, q_r], axis=-1)
        k_full = jnp.concatenate([k_n, k_r], axis=-1)
        scale = 1.0 / np.sqrt(dh)
        scores = jnp.einsum('bhqd,bhkd->bhqk', q_full, k_full) * scale
        causal = jnp.tril(jnp.ones((T, T), dtype=bool))
        scores = jnp.where(causal[None, None], scores, -jnp.inf)
        probs = jax.nn.softmax(scores, axis=-1)
        y = jnp.einsum('bhqk,bhkd->bhqd', probs, v)
        y = y.transpose(0, 2, 1, 3).reshape(B, T, C)
        return y @ W_o.T + b_o

    def _L1_ffn_ref(x, gate_W_packed, gate_scales, up_W_packed, up_scales, down_W_packed, down_scales):
        import jax, jax.numpy as jnp
        import numpy as np
        BLOCK_SIZE = 32
        HIDDEN_SIZE = 256
        MLP_DIM = 2048
        NVFP4_LUT = jnp.array([0.0, 0.5, 1.0, 1.5, 2.0, 3.0, 4.0, 6.0, 0.0, -0.5, -1.0, -1.5, -2.0, -3.0, -4.0, -6.0], dtype=jnp.float32)

        def dequant_nvfp4(W_packed, scales, block=BLOCK_SIZE):
            N = W_packed.shape[0]
            low = W_packed & 15
            high = W_packed >> 4 & 15
            idx = jnp.stack([low, high], axis=-1).reshape(N, -1)
            vals = NVFP4_LUT[idx]
            K = vals.shape[1]
            vals = vals.reshape(N, K // block, block) * scales[:, :, None]
            return vals.reshape(N, K)
        B, S, H = x.shape
        xt = x.reshape(B * S, H)
        Wg = dequant_nvfp4(gate_W_packed, gate_scales)
        Wu = dequant_nvfp4(up_W_packed, up_scales)
        Wd = dequant_nvfp4(down_W_packed, down_scales)
        gate = jnp.einsum('th,nh->tn', xt, Wg)
        up = jnp.einsum('th,nh->tn', xt, Wu)
        gelu = jnp.tanh(0.7978845608028654 * (gate + 0.044715 * gate ** 3)) * gate * 0.5 + gate * 0.5
        inter = gelu * up
        out = jnp.einsum('tn,hn->th', inter, Wd)
        return out.reshape(B, S, H)
    x = L0_attn_x
    xn = _layernorm(x, axis=-1)
    x = x + _L0_attn_ref(xn, L0_attn_Wq, L0_attn_Wk, L0_attn_Wv, L0_attn_Wo) + _L0_ffn_ref(xn, L0_ffn_gate_w, L0_ffn_shared_wg, L0_ffn_shared_wu, L0_ffn_shared_wd, L0_ffn_exp_wg, L0_ffn_exp_wu, L0_ffn_exp_wd)
    xn = _layernorm(x, axis=-1)
    x = x + _L1_attn_ref(xn, L1_attn_W_d_q, L1_attn_b_d_q, L1_attn_q_norm_g, L1_attn_q_norm_b, L1_attn_W_u_q, L1_attn_b_u_q, L1_attn_W_d_kv, L1_attn_b_d_kv, L1_attn_kv_norm_g, L1_attn_kv_norm_b, L1_attn_W_u_kv, L1_attn_b_u_kv, L1_attn_W_o, L1_attn_b_o) + _L1_ffn_ref(xn, L1_ffn_gate_W_packed, L1_ffn_gate_scales, L1_ffn_up_W_packed, L1_ffn_up_scales, L1_ffn_down_W_packed, L1_ffn_down_scales)
    return x

_drawn_inputs = setup_inputs


def setup_inputs(seed=0):
    import zlib

    import numpy as np

    out = dict(_drawn_inputs(seed))
    spreads = {'L1_attn_b_d_q': (0.0, 0.8),
     'L1_attn_q_norm_g': (1.0, 0.6),
     'L1_attn_q_norm_b': (0.0, 0.8),
     'L1_attn_b_u_q': (0.0, 0.8),
     'L1_attn_b_d_kv': (0.0, 0.8),
     'L1_attn_kv_norm_g': (1.0, 0.6),
     'L1_attn_kv_norm_b': (0.0, 0.8),
     'L1_attn_b_u_kv': (0.0, 0.8),
     'L1_attn_b_o': (0.0, 0.8)}
    factors = {'L1_attn_W_d_q': 8.0,
     'L1_attn_W_u_q': 8.0,
     'L1_attn_W_d_kv': 8.0,
     'L1_attn_W_u_kv': 8.0,
     'L1_attn_W_o': 8.0}
    for name, (base, spread) in spreads.items():
        noise = np.random.default_rng([zlib.crc32(name.encode()), seed]).standard_normal(out[name].shape)
        drawn = base * np.exp(spread * noise) if base else spread * noise
        out[name] = jnp.asarray(drawn.astype(out[name].dtype))
    for name, factor in factors.items():
        out[name] = (out[name] * factor).astype(out[name].dtype)
    return out
```

```python
from contextlib import ExitStack

import concourse.bass as bass
from concourse import mybir

F32 = mybir.dt.float32
F32R = mybir.dt.float32r
BF16 = mybir.dt.bfloat16
F16 = mybir.dt.float16
I32 = mybir.dt.int32
U16 = mybir.dt.uint16
ALU = mybir.AluOpType
ACT = mybir.ActivationFunctionType
AX = mybir.AxisListType

P = 128
D = 256
KD = D // P
BATCHES, SEQ = 8, 256
TOKENS = BATCHES * SEQ
NT = 512
G = TOKENS // NT
EPS = 1e-5

E_FF, N_EXP, SH_FF = 176, 8, 352
XT = N_EXP * E_FF // P
ST = 3
ST_M = [128, 128, SH_FF - 256]
T0 = ST + XT
ROUTE_SCALE = 2.5
DENOM = float(D) ** 0.5 / SEQ

MLP = 2048
T1 = MLP // P
H, DH, DN, DR = 16, 16, 8, 8
D_Q, D_KV = D // 3, D // 2
C_W = D_Q + D_KV + DR
SCALE = float(DH) ** -0.5
SLOT = 6 * DH
MASKED = -1e30

O_QKVO = 0
O_SG = 4 * KD * D
O_SU = O_SG + KD * SH_FF
O_SD = O_SU + KD * SH_FF
O_EG = O_SD + ST * D
O_EU = O_EG + KD * XT * P
O_ED = O_EU + KD * XT * P
W0_COLS = O_ED + XT * D
CHUNKS0 = [(0, O_SG), (O_SG, O_EG), (O_EG, O_EU), (O_EU, O_ED), (O_ED, W0_COLS)]
O_G4 = 0
O_U4 = KD * MLP
O_D4 = 2 * KD * MLP
A_DN = 0
A_UQ = A_DN + KD * 256
A_UKV = A_UQ + D
A_O = A_UKV + D + H * DN
WA_COLS = A_O + KD * D
STAGE = max(b - a for a, b in CHUNKS0)
QW = 512
NQ = 3 * MLP // QW


def transformer_blocks(nc, xT, w0, gateT, wa, biasc, biasq, biaskv, lng, bo, ones_c, sel_c, selm_c, ident_c, identb_c,
                       mask_c, rot_c, tie_c, q4, s4, out):
    ctx = ExitStack()
    with ctx:
        def sb(name, shape, dt, where=ctx):
            return where.enter_context(nc.sbuf_tensor(name, shape, dt))

        def sem(name):
            return ctx.enter_context(nc.semaphore(name))

        wh = sb("wh", [P, W0_COLS], F32R)
        wl = sb("wl", [P, W0_COLS], F32R)
        ah = sb("ah", [P, WA_COLS], F32R)
        al = sb("al", [P, WA_COLS], F32R)
        x = sb("x", [P, KD, TOKENS], F32)
        ones = sb("ones", [P, P], F32)
        epsb = sb("epsb", [P, 1], F32)
        identf = sb("identf", [P, P], F32)
        xc = sb("xc", [P, KD, NT], F32)
        sq = sb("sq", [P, KD, NT], F32)
        std = sb("std", [P, NT], F32)
        rstd = std
        xh = sb("xh", [P, KD, NT], F32R)
        xl = sb("xl", [P, KD, NT], F32R)
        act = sb("act", [P, 2, NT], F32)
        hf = sb("hf", [P, 2, NT], F32)
        hh = sb("hh", [P, 2, NT], F32R)
        hl = sb("hl", [P, 2, NT], F32R)

        c0 = ExitStack()
        stage = sb("stage", [P, STAGE], F32, c0)
        sel = sb("sel", [P, XT * P], F32R, c0)
        gw = sb("gw", [P, 2, KD, N_EXP], F32R, c0)
        gwf = sb("gwf", [P, KD, N_EXP], F32, c0)
        vs = sb("vs", [P, 2, NT], F32, c0)
        kv0 = sb("kv0", [P, 2, NT], F32, c0)
        vhh = sb("vhh", [P, KD, NT], F32R, c0)
        vhl = sb("vhl", [P, KD, NT], F32R, c0)
        sig = sb("sig", [N_EXP, NT], F32, c0)
        sc = sb("sc", [P, 4, N_EXP], F32, c0)
        gt = sb("gt", [P, 4, N_EXP, N_EXP], F32, c0)
        ge = sb("ge", [P, 4, N_EXP, N_EXP], F32, c0)
        unit = sb("unit", [P, SEQ], F32, c0)
        tie = sb("tie", [P, N_EXP, N_EXP], F32, c0)
        rank = sb("rank", [P, 4, N_EXP], F32, c0)
        rw = sb("rw", [P, 4, N_EXP], F32, c0)
        rsum = sb("rsum", [P, 4], F32, c0)
        rrec = sb("rrec", [P, 4], F32, c0)
        rwn = sb("rwn", [P, 4, N_EXP], F32, c0)
        wT = sb("wT", [P, NT], F32R, c0)
        kvt = vs
        vfl = hf
        c0.close()

        c1 = ctx
        bc = sb("bc", [P, C_W], F32, c1)
        bq = sb("bq", [P, D], F32, c1)
        bkv = sb("bkv", [P, D + H * DN], F32, c1)
        gb = sb("gb", [P, 4], F32, c1)
        bout = sb("bout", [P, KD], F32, c1)
        rot = sb("rot", [P, 2, H, 4], F32, c1)
        ident = sb("ident", [P, P], BF16, c1)
        maskq = sb("maskq", [P, P], BF16, c1)
        maskk = sb("maskk", [P, P], BF16, c1)
        selm = sb("selm", [P, H, P], BF16, c1)
        bst = sb("bst", [P, 4, 6], F32, c1)
        mv = sb("mv", [P, 4, 2], F32, c1)
        cstd = sb("cstd", [P, 4], F32, c1)
        crs = sb("crs", [P, 4], F32, c1)
        rt = sb("rt", [P, 4, 2, H, 4], F32, c1)
        v3 = sb("v3", [P, 2, H, 3, DH + 1], BF16, c1)
        qT = sb("qT", [P, H, SEQ], BF16, c1)
        kT = sb("kT", [P, H, SEQ], BF16, c1)
        mx = sb("mx", [P, 2, H], F32, c1)
        nm = sb("nm", [P, 2, 2, H], BF16, c1)
        mT = sb("mT", [P, SEQ], BF16, c1)
        c2 = ExitStack()
        words = sb("words", [P, QW], I32, c2)
        fbits = sb("fbits", [P, QW], I32, c2)
        gval = sb("gval", [P, QW], F32, c2)
        sbits = sb("sbits", [P, QW], I32, c2)
        scl = sb("scl", [P, QW], F32, c2)
        wf = sb("wf", [P, QW], F32, c2)
        c2.close()
        c2 = ExitStack()
        qs = sb("qs", [P, 2, H, SLOT], BF16, c2)
        ks = sb("ks", [P, 2, H, SLOT], BF16, c2)
        c2.close()
        ph = sb("ph", [P, 6, NT], F16)
        pl = sb("pl", [P, 6, NT], F16)
        flat = lambda t: t[:, :, :].rearrange("p a b -> p (a b)")
        kf = xc[:, 0, :].rearrange("p (t h d) -> p t h d", t=2, h=H)
        vf = xc[:, 1, :].rearrange("p (t h d) -> p t h d", t=2, h=H)
        qf = flat(sq)[:, 0:2 * H * DH].rearrange("p (t h d) -> p t h d", t=2, h=H)
        c = flat(sq)[:, KD * NT - 2 * C_W:].rearrange("p (t n) -> p t n", t=2)
        cn = c
        ctf = std[:, :].rearrange("p (w t) -> p w t", w=2)
        cth, ctl = hh[:, :, SEQ:], hl[:, :, SEQ:]
        yh, yl = hh[:, :, 0:SEQ], hl[:, :, 0:SEQ]
        ex = hf
        y = act[:, 0, :].rearrange("p (i h d) -> p i h d", i=2, h=H)
        ys = act[:, 1, 0:8 * (DH + 1)].rearrange("p (x d) -> p x d", x=8)
        yr = act[:, 1, NT - 8:]
        qbuf = [[qs, qf, qT], [ks, kf, kT]]

        acc = ctx.enter_context(nc.psum_tensor("acc", [P, KD, NT], F32))
        ring = [ctx.enter_context(nc.psum_tensor(f"ring{i}", [P, NT], F32)) for i in range(4)]
        pm = ctx.enter_context(nc.psum_tensor("pm", [P, NT], F32))
        pv = ctx.enter_context(nc.psum_tensor("pv", [P, NT], F32))

        s_x = [sem(f"x_in{g}") for g in range(G)]
        s_const = sem("constants_in")
        s_stage = sem("weights_in")
        s_whi = sem("weights_hi")
        s_wlo = sem("weights_split")
        s_prep = sem("small_set_up")
        s_mean, s_xc, s_sq, s_var, s_std = map(sem, ("mean", "centred", "squares", "variance", "deviation"))
        s_rstd, s_xn, s_xh, s_xl = map(sem, ("inverse_deviation", "normed", "normed_hi", "normed_split"))
        s_xdone = sem("normed_used")
        s_v, s_k, s_q = map(sem, ("v_product", "k_product", "q_product"))
        s_vs, s_kv, s_scan, s_vh, s_vhh, s_vhl = map(
            sem, ("v_scaled", "kv", "kv_summed", "vhat", "vhat_hi", "vhat_split"))
        s_oproj = sem("vhat_used")
        s_lg, s_sig, s_st, s_rk, s_wt, s_wth, s_wtl = map(
            sem, ("logits", "scores", "scores_turned", "route_steps", "weights_turned", "weights_hi_in",
                  "weights_lo_in"))
        s_gu, s_act, s_wbc, s_h, s_hw, s_hh, s_hl, s_dn = map(
            sem, ("gate_up", "activated", "route_spread", "gated", "routed", "h_hi", "h_split", "h_used"))
        s_res = sem("residual")
        s_out = sem("stored")
        s_words, s_scl, s_bits, s_sgn, s_w, s_w4h, s_w4l = map(
            sem, ("words_in", "scales_in", "bit_steps", "signs", "w4", "w4_hi", "w4_split"))
        s_cps, s_c, s_bn, s_cstd, s_crs, s_cn, s_ctr, s_ct, s_cth, s_ctl = map(
            sem, ("latents", "latents_biased", "latent_stats", "latent_deviation", "latent_inverse",
                  "latents_normed", "latents_turned", "latents_affine", "latents_hi", "latents_split"))
        s_qkv, s_qkvb, s_rope, s_split, s_copy = map(
            sem, ("qkv", "qkv_biased", "rotary_steps", "split_steps", "slots_copied"))
        s_tr, s_evA, s_evD = map(sem, ("slots_turned", "turned_by_act", "turned_by_dve"))
        s_s, s_mx, s_nm, s_mtr, s_mT = map(sem, ("score_bank", "score_max", "max_split", "max_turned", "max_in"))
        s_sT, s_e, s_ph, s_pl, s_y, s_yst, s_yn = map(
            sem, ("score_bank_turned", "exponentials", "probs_hi", "probs_split", "y_bank", "y_steps", "y_normed"))
        s_ytr, s_yh, s_yl, s_ao = map(sem, ("y_turned", "y_hi", "y_split", "y_used"))

        SETUP0, SETUP1 = 4, 3
        LN_OF = lambda n: n % G

        def xg(g):
            return x[:, :, g * NT:(g + 1) * NT]

        def w0k(off, width, k, a, b):
            return slice(off + k * width + a, off + k * width + b)

        consts = [(ones, ones_c), (identf, ident_c)]
        def w4_at(dst, n, j):
            if n < 8:
                off = (O_G4, O_U4)[n // 4] + j * MLP + (n % 4) * QW
                return dst[:, off:off + QW]
            v = dst[:, O_D4:O_D4 + T1 * D].rearrange("p (c j d) -> p c j d", c=T1 // 2, j=2)
            return v[:, 2 * (n - 8):2 * (n - 8) + 2, j, :]

        block = ctx.enter_context(nc.Block())

        @block.sync
        def _(sp):
            sp.dma_start(xg(0), xT[:, :, 0:NT]).then_inc(s_x[0], 16)
            for t, src in consts:
                sp.dma_start(t[:, :], src).then_inc(s_const, 16)
            sp.dma_start(gwf[:, :, :], gateT).then_inc(s_const, 16)
            sp.dma_start(tie[:, :, :], tie_c).then_inc(s_const, 16)
            for n, (a, b) in enumerate(CHUNKS0):
                if n >= 1:
                    sp.wait_ge(s_wlo, n)
                sp.dma_start(stage[:, 0:b - a], w0[:, a:b]).then_inc(s_stage, 16)
                if n == 0:
                    for g in range(1, G):
                        sp.dma_start(xg(g), xT[:, :, g * NT:(g + 1) * NT]).then_inc(s_x[g], 16)
            sp.wait_ge(s_wlo, 5)
            sp.dma_start(stage[:, 0:XT * P], sel_c).then_inc(s_stage, 16)
            sp.wait_ge(s_whi, 7)
            sp.dma_start(stage[:, 0:WA_COLS], wa).then_inc(s_stage, 16)
            sp.wait_ge(s_res, G)
            for t, src in ((bc[:, :], biasc.partition_broadcast(P)), (bq[:, :], biasq.partition_broadcast(P)),
                           (bkv[:, :], biaskv.partition_broadcast(P)), (gb[:, :], lng), (bout[:, :], bo),
                           (rot[:, :, :, :], rot_c), (ident[:, :], identb_c.bitcast(BF16)),
                           (maskq[:, :], mask_c[0].bitcast(BF16)), (maskk[:, :], mask_c[1].bitcast(BF16)),
                           (selm[:, :, :], selm_c.bitcast(BF16))):
                sp.dma_start(t, src).then_inc(s_const, 16)
            for n in range(NQ):
                if n >= 1:
                    sp.wait_ge(s_w4l, 2 * n)
                sp.dma_start(words[:, :], q4[:, n, :]).then_inc(s_words, 16)
                sp.dma_start(scl[:, :], s4[:, n, :]).then_inc(s_scl, 16)
            for g in range(G):
                sp.wait_ge(s_res, G + g + 1)
                sp.dma_start(out[:, :, g * NT:(g + 1) * NT], xg(g)).then_inc(s_out, 16)
            sp.wait_ge(s_out, 16 * G)

        @block.tensor
        def _(pe):
            def prod(o, lo_hi_w, x_hi, x_lo, first, last):
                w_hi, w_lo = lo_hi_w
                pe.matmul(o, w_hi, x_hi, start=first, stop=False, skip_group_check=True)
                pe.matmul(o, w_lo, x_hi, start=False, stop=False, skip_group_check=True)
                return pe.matmul(o, w_hi, x_lo, start=False, stop=last, skip_group_check=True)

            def layernorm(n):
                g = LN_OF(n)
                if n < G:
                    pe.wait_ge(s_x[g], 16)
                else:
                    pe.wait_ge(s_res, G)
                if 1 <= n <= G:
                    pe.wait_ge(s_hw, XT * n)
                for k in range(KD):
                    mm = pe.matmul(pm[:, :], ones[:, :], xg(g)[:, k, :], start=k == 0, stop=k == KD - 1)
                mm.then_inc(s_mean, 1)
                pe.wait_ge(s_sq, n + 1)
                for k in range(KD):
                    mm = pe.matmul(pv[:, :], ones[:, :], sq[:, k, :], start=k == 0, stop=k == KD - 1)
                mm.then_inc(s_var, 1)
                pe.wait_ge(s_xl, n + 1)
                pe.wait_ge(s_xh, n + 1)

            def w(off, width, k, a, b):
                s = w0k(off, width, k, a, b)
                return wh[:, s], wl[:, s]

            def down(tile_no, off, kt, rows, last):
                pe.wait_ge(s_hl, tile_no + 1)
                b = tile_no % 2
                for m in range(KD):
                    s = w0k(off, D, kt, m * P, (m + 1) * P)
                    mm = prod(acc[:, m, :], (wh[0:rows, s], wl[0:rows, s]), hh[0:rows, b, :], hl[0:rows, b, :],
                              False, last)
                mm.then_inc(s_dn, 1)

            pe.wait_ge(s_const, 64)
            for g in range(G):
                layernorm(g)
                if g == 0:
                    pe.wait_ge(s_wlo, 1)
                    pe.wait_ge(s_prep, SETUP0)
                else:
                    pe.wait_ge(s_h, T0 * g)
                for m in range(KD):
                    for j, (which, bank, s) in enumerate(((2, (0, 3), s_v), (1, (1, 0), s_k), (0, (2, 1), s_q))):
                        if m == 1 and j == 1:
                            pe.wait_ge(s_vs, 2 * g + 1)
                        if m == 1 and j == 2:
                            pe.wait_ge(s_kv, 2 * g + 1)
                        for k in range(KD):
                            mm = prod(ring[bank[m]][:, :], w(O_QKVO + which * KD * D, D, k, m * P, (m + 1) * P),
                                      xh[:, k, :], xl[:, k, :], k == 0, k == KD - 1)
                        mm.then_inc(s, 1)
                for k in range(KD):
                    mm = prod(pm[0:N_EXP, :], (gw[:, 0, k, :], gw[:, 1, k, :]), xh[:, k, :], xl[:, k, :],
                              k == 0, k == KD - 1)
                mm.then_inc(s_lg, 1)
                pe.wait_ge(s_sig, g + 1)
                for t in range(4):
                    mm = pe.transpose(pv[:, t * N_EXP:(t + 1) * N_EXP], sig[:, t * P:(t + 1) * P],
                                      identf[0:N_EXP, 0:N_EXP])
                mm.then_inc(s_st, 1)
                pe.wait_ge(s_vhl, 2 * g + 2)
                if g >= 1:
                    pe.wait_ge(s_res, g)
                for m in range(KD):
                    for k in range(KD):
                        mm = prod(acc[:, m, :], w(O_QKVO + 3 * KD * D, D, k, m * P, (m + 1) * P),
                                  vhh[:, k, :], vhl[:, k, :], k == 0, False)
                mm.then_inc(s_oproj, 1)
                pe.wait_ge(s_rk, 11 * (g + 1))
                for t in range(4):
                    mm = pe.transpose(pm[0:N_EXP, t * P:(t + 1) * P], rwn[:, t, :], identf[:, :])
                mm.then_inc(s_wt, 1)

                def gate_up(t):
                    n = g * T0 + t
                    if t >= 2:
                        pe.wait_ge(s_h, n - 1)
                    else:
                        pe.wait_ge(s_vh, 2 * g + 2)
                    rows = ST_M[t] if t < ST else P
                    for o, off, eoff in ((2 * (t % 2), O_SG, O_EG), (2 * (t % 2) + 1, O_SU, O_EU)):
                        for k in range(KD):
                            if t < ST:
                                ww = w(off, SH_FF, k, t * P, t * P + rows)
                            else:
                                ww = w(eoff, XT * P, k, (t - ST) * P, (t - ST + 1) * P)
                            mm = prod(ring[o][0:rows, :], ww, xh[:, k, :], xl[:, k, :], k == 0, k == KD - 1)
                    mm.then_inc(s_gu, 1)
                    if t >= ST:
                        e = g * XT + t - ST
                        if t == ST:
                            pe.wait_ge(s_wtl, g + 1)
                            pe.wait_ge(s_rk, 11 * g + 1)
                        if e >= 2:
                            pe.wait_ge(s_hw, e - 1)
                        bank = (pm, pv)[e % 2]
                        pe.matmul(bank[:, :], sel[:, (t - ST) * P:(t - ST + 1) * P], wT[:, :], start=True,
                                  stop=True).then_inc(s_wbc, 1)

                for t in range(T0):
                    if g == 0 and t == 0:
                        pe.wait_ge(s_wlo, 2)
                    if g == 0 and t == ST:
                        pe.wait_ge(s_wlo, 5)
                        pe.wait_ge(s_whi, 7)
                    gate_up(t)
                    if t >= 1:
                        u = t - 1
                        down(g * T0 + u, O_SD if u < ST else O_ED, u if u < ST else u - ST,
                             ST_M[u] if u < ST else P, False)
                down(g * T0 + T0 - 1, O_ED, XT - 1, P, True)

            pe.wait_ge(s_const, 16 * 14)
            pe.wait_ge(s_prep, SETUP0 + SETUP1)
            for g in range(G):
                layernorm(G + g)
                for hb in range(2):
                    nb = 2 * g + hb
                    tok = lambda t: slice(hb * SEQ + t * P, hb * SEQ + (t + 1) * P)
                    if nb == 0:
                        pe.wait_ge(s_h, T0 * G)
                        pe.wait_ge(s_wlo, 6)
                    elif hb == 0:
                        pe.wait_ge(s_h, T0 * G + T1 * g)
                    else:
                        pe.wait_ge(s_e, 12 * nb)
                    for t in range(2):
                        for k in range(KD):
                            s = w0k(A_DN, 256, k, 0, 256)
                            xx = (xh[:, k, tok(t)], xl[:, k, tok(t)])
                            pe.matmul(ring[t][:, 0:256], xx[0], ah[:, s], start=k == 0, stop=False)
                            pe.matmul(ring[t][:, 0:256], xx[1], ah[:, s], start=False, stop=False)
                            mm = pe.matmul(ring[t][:, 0:256], xx[0], al[:, s], start=False, stop=k == KD - 1)
                        mm.then_inc(s_cps, 1)
                    pe.wait_ge(s_cn, 4 * (nb + 1))
                    for t in range(2):
                        pe.transpose(pm[0:D_Q, t * P:(t + 1) * P], cn[:, t, 0:D_Q], identf[:, :])
                        mm = pe.transpose(pm[:, SEQ + t * P:SEQ + (t + 1) * P], cn[:, t, D_Q:D_Q + D_KV], identf[:, :])
                    mm.then_inc(s_ctr, 1)
                    pe.wait_ge(s_ctl, 2 * nb + 2)
                    for t in range(2):
                        for which, off, width, bank in ((0, A_UQ, D, t), (1, A_UKV, D + H * DN, 2 + t)):
                            rows = (D_Q, P)[which]
                            ch, cl = cth[0:rows, which, t * P:(t + 1) * P], ctl[0:rows, which, t * P:(t + 1) * P]
                            o = ring[bank][:, 0:width]
                            pe.matmul(o, ch, ah[0:rows, off:off + width], start=True, stop=False)
                            pe.matmul(o, cl, ah[0:rows, off:off + width], start=False, stop=False)
                            mm = pe.matmul(o, ch, al[0:rows, off:off + width], start=False, stop=True)
                        mm.then_inc(s_qkv, 1)
                    pe.wait_ge(s_split, 12 * (nb + 1))
                    pe.wait_ge(s_copy, 6 * (nb + 1))
                    for f in range(8):
                        if f >= 4:
                            (pe.wait_ge(s_evA, 4 * nb + (f - 4) // 2 + 1) if f % 2 == 0
                             else pe.wait_ge(s_evD, 4 * nb + (f - 4) // 2 + 1))
                        src = qbuf[f // 4][0]
                        bank = ring[f % 4][:, :].bitcast(BF16)
                        for h in range(4):
                            for t in range(2):
                                mm = pe.transpose(bank[0:SLOT, h * SEQ + t * P:h * SEQ + (t + 1) * P],
                                                  src[:, t, 4 * (f % 4) + h, :], ident[:, :])
                        mm.then_inc(s_tr, 1)
                    for f in range(12):
                        if f < 4:
                            (pe.wait_ge(s_evA, 4 * nb + 4) if f == 0 else None)
                            (pe.wait_ge(s_evD, 4 * nb + 4) if f == 0 else None)
                        else:
                            pe.wait_ge(s_mx, 12 * nb + f - 3)
                        i = 0 if f < 4 else 1
                        width = (i + 1) * P
                        heads = range(4 * f, 4 * f + 4) if i == 0 else range(2 * (f - 4), 2 * (f - 4) + 2)
                        for n, h in enumerate(heads):
                            o = ring[f % 4][:, n * width:(n + 1) * width]
                            pe.matmul(o, qT[0:SLOT, h, i * P:(i + 1) * P], kT[0:SLOT, h, 0:width], start=True, stop=False,
                                      skip_group_check=True)
                            mm = pe.matmul(o[:, i * P:(i + 1) * P], ident[:, :], maskq[:, :], start=False, stop=True,
                                           skip_group_check=True)
                        mm.then_inc(s_s, 1)
                    pe.wait_ge(s_nm, 2 * nb + 2)
                    mbank = pm[:, :].bitcast(BF16)
                    for i in range(2):
                        mm = pe.transpose(mbank[0:2 * H, i * P:(i + 1) * P],
                                          nm[:, i, :, :].rearrange("p a h -> p (a h)"), ident[:, :])
                    mm.then_inc(s_mtr, 1)
                    pe.wait_ge(s_mT, nb + 1)

                    def probs(hg, nb=nb):
                        for part in range(3):
                            f = 3 * hg + part
                            if f >= 4:
                                pe.wait_ge(s_e, 12 * nb + f - 3)
                            elif f == 0:
                                pe.wait_ge(s_mx, 12 * nb + 12)
                            kt = 0 if part < 2 else 1
                            heads = range(4 * hg + 2 * part, 4 * hg + 2 * part + 2) if kt == 0 else \
                                range(4 * hg, 4 * hg + 4)
                            width = SEQ - kt * P
                            for n, h in enumerate(heads):
                                o = ring[f % 4][:, n * width:(n + 1) * width]
                                pe.matmul(o, kT[0:SLOT, h, kt * P:(kt + 1) * P], qT[0:SLOT, h, kt * P:SEQ], start=True,
                                          stop=False, skip_group_check=True)
                                pe.matmul(o, selm[:, h, :], mT[:, kt * P:SEQ], start=False, stop=False,
                                          skip_group_check=True)
                                mm = pe.matmul(o[:, 0:P], ident[:, :], maskk[:, :], start=False, stop=True,
                                               skip_group_check=True)
                            mm.then_inc(s_sT, 1)

                    def values(hg, nb=nb):
                        pe.wait_ge(s_ph, 12 * nb + 3 * hg + 3)
                        pe.wait_ge(s_pl, 12 * nb + 3 * hg + 3)
                        bank = (pm, pv)[hg % 2]
                        if hg >= 2:
                            pe.wait_ge(s_yn, 4 * nb + hg - 1)
                        half = 3 * (hg % 2)
                        for i in range(2):
                            for hn in range(4):
                                o = bank[:, (4 * i + hn) * 51:(4 * i + hn + 1) * 51]
                                for kt in range(i + 1):
                                    if kt == 0:
                                        slot, col = half + hn // 2, (hn % 2) * SEQ + i * P
                                    else:
                                        slot, col = half + 2, hn * P
                                    vv = v3[:, kt, 4 * hg + hn, :, :].rearrange("p s d -> p (s d)")
                                    pe.matmul(o, ph[:, slot, col:col + P], vv, start=kt == 0, stop=False,
                                              skip_group_check=True)
                                    mm = pe.matmul(o, pl[:, slot, col:col + P], vv, start=False, stop=kt == i,
                                                   skip_group_check=True)
                        mm.then_inc(s_y, 1)

                    probs(0)
                    for hg in range(4):
                        if hg < 3:
                            probs(hg + 1)
                        values(hg)
                    pe.wait_ge(s_yn, 4 * nb + 4)
                    for m in range(KD):
                        for i in range(2):
                            mm = pe.transpose(pm[:, m * SEQ + i * P:m * SEQ + (i + 1) * P],
                                              y[:, i, 8 * m:8 * m + 8, :].rearrange("p h d -> p (h d)"), identf[:, :])
                    mm.then_inc(s_ytr, 1)
                    pe.wait_ge(s_yl, nb + 1)
                    if hb == 0:
                        pe.wait_ge(s_res, G + g)
                    for m in range(KD):
                        for k in range(KD):
                            s = w0k(A_O, D, k, m * P, (m + 1) * P)
                            mm = prod(acc[:, m, hb * SEQ:(hb + 1) * SEQ], (ah[:, s], al[:, s]), yh[:, k, :],
                                      yl[:, k, :], hb == 0 and k == 0, False)
                    mm.then_inc(s_ao, 1)

                def gate_up1(t):
                    n = T0 * G + g * T1 + t
                    if t >= 2:
                        pe.wait_ge(s_h, n - 1)
                    else:
                        pe.wait_ge(s_e, 24 * (g + 1))
                    for o, off in ((2 * (t % 2), O_G4), (2 * (t % 2) + 1, O_U4)):
                        for k in range(KD):
                            mm = prod(ring[o][:, :], w(off, MLP, k, t * P, (t + 1) * P), xh[:, k, :], xl[:, k, :],
                                      k == 0, k == KD - 1)
                    mm.then_inc(s_gu, 1)

                if g == 0:
                    pe.wait_ge(s_w4l, 2 * NQ)
                for t in range(T1):
                    gate_up1(t)
                    if t >= 1:
                        down(T0 * G + g * T1 + t - 1, O_D4, t - 1, P, False)
                down(T0 * G + g * T1 + T1 - 1, O_D4, T1 - 1, P, True)

        @block.scalar
        def _(a):
            def layernorm(n):
                a.wait_ge(s_xc, n + 1)
                a.activation(sq[:, :, :], xc[:, :, :], ACT.Square).then_inc(s_sq, 1)
                a.wait_ge(s_var, n + 1)
                a.activation(std[:, :], pv[:, :], ACT.Sqrt, bias=epsb[:, :]).then_inc(s_std, 1)
                a.wait_ge(s_xn, n + 1)
                if n >= 1:
                    a.wait_ge(s_gu, T0 * n if n <= G else T0 * G + T1 * (n - G))
                a.activation(xh[:, :, :], xc[:, :, :], ACT.Copy).then_inc(s_xh, 1)

            def weights(n, a0, b0, dst):
                a.wait_ge(s_stage, 16 * (n + 1))
                a.activation(dst[:, a0:b0], stage[:, 0:b0 - a0], ACT.Copy).then_inc(s_whi, 1)

            def activate(n, g_t, rows, func):
                a.wait_ge(s_gu, n + 1)
                if n >= 2:
                    a.wait_ge(s_h, n - 1)
                a.activation(act[0:rows, n % 2, :], ring[2 * (g_t % 2)][0:rows, :], func).then_inc(s_act, 1)

            def split_h(n, rows, routed):
                if routed is None:
                    a.wait_ge(s_h, n + 1)
                else:
                    a.wait_ge(s_hw, routed + 1)
                if n >= 2:
                    a.wait_ge(s_dn, n - 1)
                a.activation(hh[0:rows, n % 2, :], hf[0:rows, n % 2, :], ACT.Copy).then_inc(s_hh, 1)

            weights(0, *CHUNKS0[0], wh)
            a.wait_ge(s_const, 64)
            a.activation(gw[:, 0, :, :], gwf[:, :, :], ACT.Copy).then_inc(s_whi, 1)
            a.wait_ge(s_prep, SETUP0)
            for g in range(G):
                layernorm(g)
                for m in range(KD):
                    a.wait_ge(s_v, 2 * g + m + 1)
                    a.activation(vs[:, m, :], ring[(0, 3)[m]][:, :], ACT.Copy, scale=DENOM).then_inc(s_vs, 1)
                if g == 0:
                    weights(1, *CHUNKS0[1], wh)
                a.wait_ge(s_lg, g + 1)
                a.activation(sig[:, :], pm[0:N_EXP, :], ACT.Sigmoid).then_inc(s_sig, 1)
                for m in range(KD):
                    a.wait_ge(s_vh, 2 * g + m + 1)
                    if g >= 1 and m == 0:
                        a.wait_ge(s_oproj, g)
                    a.activation(vhh[:, m, :], vfl[:, m, :], ACT.Copy).then_inc(s_vhh, 1)
                if g == 0:
                    for n in (2, 3, 4):
                        weights(n, *CHUNKS0[n], wh)
                    weights(5, 0, XT * P, sel)
                a.wait_ge(s_wt, g + 1)
                if g >= 1:
                    a.wait_ge(s_wbc, XT * g)
                a.activation(wT[0:N_EXP, :], pm[0:N_EXP, :], ACT.Copy).then_inc(s_wth, 1)
                for t in range(T0):
                    n = g * T0 + t
                    activate(n, t, ST_M[t] if t < ST else P, ACT.Silu)
                    if t >= 1:
                        u = t - 1
                        split_h(n - 1, ST_M[u] if u < ST else P, None if u < ST else g * XT + u - ST)
                split_h(g * T0 + T0 - 1, P, g * XT + XT - 1)
                if g == 0:
                    weights(6, 0, WA_COLS, ah)

            for g in range(G):
                layernorm(G + g)
                for hb in range(2):
                    nb = 2 * g + hb
                    a.wait_ge(s_bn, 8 * (nb + 1))
                    a.activation(cstd[:, :], mv[:, :, 1], ACT.Sqrt, bias=epsb[:, :]).then_inc(s_cstd, 1)
                    if nb == 0:
                        for n in range(NQ):
                            for j in range(2):
                                a.wait_ge(s_w, 2 * n + j + 1)
                                a.activation(w4_at(wh, n, j), wf[:, :], ACT.Copy).then_inc(s_w4h, 1)
                    for which in range(2):
                        a.wait_ge(s_ct, 2 * nb + which + 1)
                        rows = (D_Q, P)[which]
                        a.activation(cth[0:rows, which, :], ctf[0:rows, which, :], ACT.Copy).then_inc(s_cth, 1)
                    for f in range(0, 8, 2):
                        a.wait_ge(s_tr, 8 * nb + f + 1)
                        a.activation(qbuf[f // 4][2][0:SLOT, 4 * (f % 4):4 * (f % 4) + 4, :].rearrange("p h t -> p (h t)"),
                                     ring[f % 4][0:SLOT, :].bitcast(BF16), ACT.Copy).then_inc(s_evA, 1)
                    a.wait_ge(s_mtr, nb + 1)
                    a.activation(mT[0:2 * H, :], pm[:, :].bitcast(BF16)[0:2 * H, 0:SEQ], ACT.Copy).then_inc(s_mT, 1)
                    for f in range(12):
                        n = 12 * nb + f
                        a.wait_ge(s_sT, n + 1)
                        if f == 0 and hb == 0:
                            a.wait_ge(s_hl, T0 * G + T1 * g)
                        if n >= 2:
                            a.wait_ge(s_ph, n - 1)
                            a.wait_ge(s_pl, n - 1)
                        a.activation(ex[:, n % 2, :], ring[f % 4][:, :], ACT.Exp, scale=SCALE).then_inc(s_e, 1)
                    a.wait_ge(s_ytr, nb + 1)
                    if nb >= 1:
                        a.wait_ge(s_ao, nb)
                    a.activation(yh[:, :, :], pm[:, :].rearrange("p (k t) -> p k t", k=KD), ACT.Copy).then_inc(s_yh, 1)
                for t in range(T1):
                    n = T0 * G + g * T1 + t
                    activate(n, t, P, ACT.Gelu_apprx_tanh)
                    if t >= 1:
                        split_h(n - 1, P, None)
                split_h(T0 * G + g * T1 + T1 - 1, P, None)

        @block.gpsimd
        def _(pool):
            def low(dst, src, hi):
                return pool.tensor_tensor(dst, src, hi.bitcast(F32), ALU.subtract)

            def split_h(n, rows):
                pool.wait_ge(s_hh, n + 1)
                low(hl[0:rows, n % 2, :], hf[0:rows, n % 2, :], hh[0:rows, n % 2, :]).then_inc(s_hl, 1)

            for n, (a0, b0) in enumerate(CHUNKS0):
                pool.wait_ge(s_whi, n + 1 + (n >= 1))
                low(wl[:, a0:b0], stage[:, 0:b0 - a0], wh[:, a0:b0]).then_inc(s_wlo, 1)
            for g in range(G):
                for t in range(T0):
                    split_h(g * T0 + t, ST_M[t] if t < ST else P)
                if g == 0:
                    pool.wait_ge(s_whi, 8)
                    low(al[:, :], stage[:, 0:WA_COLS], ah[:, :]).then_inc(s_wlo, 1)
            pool.wait_ge(s_prep, SETUP0 + SETUP1)
            for g in range(G):
                for hb in range(2):
                    nb = 2 * g + hb
                    if nb == 0:
                        for n in range(NQ):
                            for j in range(2):
                                pool.wait_ge(s_w4h, 2 * n + j + 1)
                                low(w4_at(wl, n, j), wf[:, :], w4_at(wh, n, j)).then_inc(s_w4l, 1)
                    for step, t, a0, b0 in ((1, qs, 0, 1), (2, ks, 0, 2), (1, qs, 0, 4), (2, ks, 0, 5), (7, qs, 2, 3),
                                            (8, ks, 1, 3)):
                        pool.wait_ge(s_split, 12 * nb + step)
                        pool.tensor_copy(t[:, :, :, b0 * DH:(b0 + 1) * DH],
                                         t[:, :, :, a0 * DH:(a0 + 1) * DH]).then_inc(s_copy, 1)
                    for f in range(12):
                        n = 12 * nb + f
                        slot = 3 * (f // 3 % 2) + f % 3
                        pool.wait_ge(s_ph, n + 1)
                        pool.tensor_tensor(pl[:, slot, :], ex[:, n % 2, :], ph[:, slot, :],
                                           ALU.subtract).then_inc(s_pl, 1)
                for t in range(T1):
                    split_h(T0 * G + g * T1 + t, P)

        @block.vector
        def _(v):
            def sub(dst, src, hi):
                return v.tensor_tensor(dst, src, hi.bitcast(F32), ALU.subtract)

            def layernorm(n):
                g = LN_OF(n)
                if n < G:
                    v.wait_ge(s_x[g], 16)
                v.wait_ge(s_mean, n + 1)
                mean = pm[:, :].unsqueeze(1).to_broadcast([P, KD, NT])
                v.tensor_tensor(xc[:, :, :], xg(g), mean, ALU.subtract).then_inc(s_xc, 1)
                v.wait_ge(s_std, n + 1)
                v.reciprocal(rstd[:, :], std[:, :]).then_inc(s_rstd, 1)
                v.wait_ge(s_rstd, n + 1)
                v.tensor_tensor(xc[:, :, :], xc[:, :, :], rstd[:, :].unsqueeze(1).to_broadcast([P, KD, NT]),
                                ALU.mult).then_inc(s_xn, 1)
                v.wait_ge(s_xh, n + 1)
                sub(xl[:, :, :], xc[:, :, :], xh[:, :, :]).then_inc(s_xl, 1)

            def gated(n, t, rows):
                v.wait_ge(s_act, n + 1)
                if n >= 2:
                    v.wait_ge(s_hl, n - 1)
                v.tensor_tensor(hf[0:rows, n % 2, :], act[0:rows, n % 2, :], ring[2 * (t % 2) + 1][0:rows, :],
                                ALU.mult).then_inc(s_h, 1)

            v.memset(epsb[:, :], EPS).then_inc(s_prep, 1)
            v.memset(unit[:, :], 1.0).then_inc(s_prep, 1)
            v.memset(wT[:, :].bitcast(F32), 0.0).then_inc(s_prep, 1)
            v.wait_ge(s_whi, 2)
            sub(gw[:, 1, :, :], gwf[:, :, :], gw[:, 0, :, :]).then_inc(s_prep, 1)
            v.wait_ge(s_prep, SETUP0)
            v.wait_ge(s_const, 64)
            for g in range(G):
                layernorm(g)
                for m in range(KD):
                    n = 2 * g + m
                    v.wait_ge(s_k, n + 1)
                    v.wait_ge(s_vs, n + 1)
                    v.tensor_tensor(kv0[:, m, :], ring[(1, 0)[m]][:, :], vs[:, m, :], ALU.mult).then_inc(s_kv, 1)
                    v.wait_ge(s_kv, n + 1)
                    for b in range(NT // SEQ):
                        cols = slice(b * SEQ, (b + 1) * SEQ)
                        v.tensor_tensor_scan(kvt[:, m, cols], unit[:, :], kv0[:, m, cols], 0.0, ALU.mult,
                                             ALU.add).then_inc(s_scan, 1)
                    v.wait_ge(s_scan, 2 * n + 2)
                    v.wait_ge(s_q, n + 1)
                    if m == 0 and g >= 1:
                        v.wait_ge(s_hl, T0 * g)
                    v.tensor_tensor(vfl[:, m, :], ring[(2, 1)[m]][:, :], kvt[:, m, :], ALU.mult).then_inc(s_vh, 1)
                for m in range(KD):
                    v.wait_ge(s_vh, 2 * g + m + 1)
                    v.wait_ge(s_vhh, 2 * g + m + 1)
                    sub(vhl[:, m, :], vfl[:, m, :], vhh[:, m, :]).then_inc(s_vhl, 1)
                r = 11 * g
                v.wait_ge(s_st, g + 1)
                v.tensor_copy(sc[:, :, :].rearrange("p t e -> p (t e)"), pv[:, 0:4 * N_EXP]).then_inc(s_rk, 1)
                v.wait_ge(s_rk, r + 1)
                other = sc[:, :, :].unsqueeze(2).to_broadcast([P, 4, N_EXP, N_EXP])
                own = sc[:, :, :].unsqueeze(3).to_broadcast([P, 4, N_EXP, N_EXP])
                v.tensor_tensor(gt[:, :, :, :], other, own, ALU.is_gt).then_inc(s_rk, 1)
                v.tensor_tensor(ge[:, :, :, :], other, own, ALU.is_ge).then_inc(s_rk, 1)
                v.wait_ge(s_rk, r + 3)
                v.tensor_tensor(ge[:, :, :, :], ge[:, :, :, :],
                                tie[:, :, :].unsqueeze(1).to_broadcast([P, 4, N_EXP, N_EXP]),
                                ALU.mult).then_inc(s_rk, 1)
                v.wait_ge(s_rk, r + 4)
                v.tensor_tensor(gt[:, :, :, :], gt[:, :, :, :], ge[:, :, :, :], ALU.max).then_inc(s_rk, 1)
                v.wait_ge(s_rk, r + 5)
                v.tensor_reduce(rank[:, :, :], gt[:, :, :, :], AX.X, ALU.add).then_inc(s_rk, 1)
                v.wait_ge(s_rk, r + 6)
                v.scalar_tensor_tensor(out=rw[:, :, :], in0=rank[:, :, :], scalar=1.5, in1=sc[:, :, :],
                                       op0=ALU.is_lt, op1=ALU.mult).then_inc(s_rk, 1)
                v.wait_ge(s_rk, r + 7)
                v.tensor_reduce(rsum[:, :], rw[:, :, :], AX.X, ALU.add).then_inc(s_rk, 1)
                v.wait_ge(s_rk, r + 8)
                v.tensor_scalar(rsum[:, :], rsum[:, :], 1e-20, None, ALU.add).then_inc(s_rk, 1)
                v.wait_ge(s_rk, r + 9)
                v.reciprocal(rrec[:, :], rsum[:, :]).then_inc(s_rk, 1)
                v.wait_ge(s_rk, r + 10)
                v.scalar_tensor_tensor(out=rwn[:, :, :], in0=rw[:, :, :], scalar=ROUTE_SCALE,
                                       in1=rrec[:, :].unsqueeze(2).to_broadcast([P, 4, N_EXP]),
                                       op0=ALU.mult, op1=ALU.mult).then_inc(s_rk, 1)
                v.wait_ge(s_wth, g + 1)
                sub(wT[32:32 + N_EXP, :], pm[0:N_EXP, :], wT[0:N_EXP, :]).then_inc(s_wtl, 1)
                for t in range(T0):
                    n = g * T0 + t
                    gated(n, t, ST_M[t] if t < ST else P)
                    if t >= ST:
                        e = g * XT + t - ST
                        v.wait_ge(s_h, n + 1)
                        v.wait_ge(s_wbc, e + 1)
                        v.tensor_tensor(hf[:, n % 2, :], hf[:, n % 2, :], (pm, pv)[e % 2][:, :],
                                        ALU.mult).then_inc(s_hw, 1)
                v.wait_ge(s_dn, T0 * (g + 1))
                v.tensor_tensor(xg(g), xg(g), acc[:, :, :], ALU.add).then_inc(s_res, 1)

            v.wait_ge(s_res, G)
            v.memset(v3[:, :, :, :, DH:], 0.0).then_inc(s_prep, 1)
            v.wait_ge(s_prep, SETUP0 + 1)
            v.memset(v3[:, :, :, 0, DH:], 1.0).then_inc(s_prep, 1)
            v.memset(mT[:, :], 0.0).then_inc(s_prep, 1)
            v.wait_ge(s_prep, SETUP0 + SETUP1)
            v.wait_ge(s_const, 16 * 14)

            def dequantize():
                u32 = mybir.dt.uint32
                for n in range(NQ):
                    v.wait_ge(s_words, 16 * (n + 1))
                    v.wait_ge(s_scl, 16 * (n + 1))
                    for j in range(2):
                        i = 5 * (2 * n + j)
                        w32, f32v = words[:, :].bitcast(u32), fbits[:, :].bitcast(F32)
                        v.tensor_scalar(fbits[:, :].bitcast(u32), w32, 22 - 4 * j, 7 << 22, ALU.logical_shift_left,
                                        ALU.bitwise_and).then_inc(s_bits, 1)
                        v.tensor_scalar(sbits[:, :].bitcast(u32), w32, 28 - 4 * j, 1 << 31, ALU.logical_shift_left,
                                        ALU.bitwise_and).then_inc(s_bits, 1)
                        v.wait_ge(s_bits, i + 2)
                        v.tensor_scalar(fbits[:, :].bitcast(u32), fbits[:, :].bitcast(u32), 124 << 23, None,
                                        ALU.bitwise_or).then_inc(s_bits, 1)
                        v.wait_ge(s_bits, i + 3)
                        v.tensor_scalar(gval[:, :], f32v, 8.0, -1.0, ALU.mult, ALU.add).then_inc(s_bits, 1)
                        v.wait_ge(s_bits, i + 4)
                        v.scalar_tensor_tensor(out=gval[:, :], in0=f32v, scalar=4.0, in1=gval[:, :], op0=ALU.mult,
                                               op1=ALU.min).then_inc(s_bits, 1)
                        v.wait_ge(s_bits, i + 5)
                        v.tensor_tensor(gval[:, :].bitcast(u32), gval[:, :].bitcast(u32), sbits[:, :].bitcast(u32),
                                        ALU.bitwise_or).then_inc(s_sgn, 1)
                        v.wait_ge(s_sgn, 2 * n + j + 1)
                        if n or j:
                            v.wait_ge(s_w4l, 2 * n + j)
                        v.tensor_tensor(wf[:, :], gval[:, :], scl[:, :], ALU.mult).then_inc(s_w, 1)

            for g in range(G):
                layernorm(G + g)
                for hb in range(2):
                    nb = 2 * g + hb
                    for t in range(2):
                        v.wait_ge(s_cps, 2 * nb + t + 1)
                        v.tensor_tensor(c[:, t, :], ring[t][:, 0:C_W], bc[:, :], ALU.add).then_inc(s_c, 1)
                    v.wait_ge(s_c, 2 * nb + 2)
                    seg = (slice(0, D_Q), slice(D_Q, D_Q + D_KV))
                    for t in range(2):
                        for w in range(2):
                            v.bn_stats(bst[:, 2 * t + w, :], c[:, t, seg[w]]).then_inc(s_bn, 1)
                    v.wait_ge(s_bn, 8 * nb + 4)
                    for i in range(4):
                        v.bn_aggr(mv[:, i, :], bst[:, i, :]).then_inc(s_bn, 1)
                    v.wait_ge(s_cstd, nb + 1)
                    v.wait_ge(s_bn, 8 * nb + 8)
                    v.reciprocal(crs[:, :], cstd[:, :]).then_inc(s_crs, 1)
                    v.wait_ge(s_crs, nb + 1)
                    for t in range(2):
                        for w in range(2):
                            i = 2 * t + w
                            v.tensor_scalar(cn[:, t, seg[w]], c[:, t, seg[w]], mv[:, i, 0:1], crs[:, i:i + 1],
                                            ALU.subtract, ALU.mult).then_inc(s_cn, 1)
                    if nb == 0:
                        dequantize()
                    v.wait_ge(s_ctr, nb + 1)
                    for w, rows in ((0, D_Q), (1, P)):
                        v.tensor_scalar(ctf[0:rows, w, :], pm[0:rows, w * SEQ:(w + 1) * SEQ], gb[0:rows, 2 * w:2 * w + 1],
                                        gb[0:rows, 2 * w + 1:2 * w + 2], ALU.mult, ALU.add).then_inc(s_ct, 1)
                    for w, rows in ((0, D_Q), (1, P)):
                        v.wait_ge(s_cth, 2 * nb + w + 1)
                        sub(ctl[0:rows, w, :], ctf[0:rows, w, :], cth[0:rows, w, :]).then_inc(s_ctl, 1)
                    for t in range(2):
                        v.wait_ge(s_qkv, 2 * nb + t + 1)
                        heads = lambda ap: ap.rearrange("p (h d) -> p h d", h=H)
                        kvp, kvb = heads(ring[2 + t][:, 0:D + H * DN]), heads(bkv[:, :])
                        v.tensor_tensor(qf[:, t, :, :], heads(ring[t][:, 0:D]), heads(bq[:, :]),
                                        ALU.add).then_inc(s_qkvb, 1)
                        v.tensor_tensor(kf[:, t, :, 0:DN], kvp[:, :, 0:DN], kvb[:, :, 0:DN], ALU.add).then_inc(s_qkvb, 1)
                        v.tensor_tensor(vf[:, t, :, :], kvp[:, :, DN:], kvb[:, :, DN:], ALU.add).then_inc(s_qkvb, 1)
                    v.wait_ge(s_qkvb, 6 * (nb + 1))
                    x1, x2 = qf[:, :, :, DN:DN + 4], qf[:, :, :, DN + 4:]
                    cos, sin = (rot[:, i, :, :].unsqueeze(1).to_broadcast([P, 2, H, 4]) for i in range(2))
                    for i, (xx, tt) in enumerate(((x1, cos), (x2, sin), (x1, sin), (x2, cos))):
                        v.tensor_tensor(rt[:, i, :, :, :], xx, tt, ALU.mult).then_inc(s_rope, 1)
                    v.wait_ge(s_rope, 7 * nb + 4)
                    v.tensor_tensor(x1, rt[:, 0, :, :, :], rt[:, 1, :, :, :], ALU.add).then_inc(s_rope, 1)
                    v.tensor_tensor(x2, rt[:, 3, :, :, :], rt[:, 2, :, :, :], ALU.subtract).then_inc(s_rope, 1)
                    for t in range(2):
                        kr = v.tensor_copy(kf[:, t, :, DN:],
                                           c[:, t, D_Q + D_KV:].unsqueeze(1).to_broadcast([P, H, DR]))
                    kr.then_inc(s_rope, 1)
                    v.wait_ge(s_rope, 7 * nb + 7)
                    slot = lambda t, i: t[:, :, :, i * DH:(i + 1) * DH]
                    q_f = qf
                    parts = ((q_f, slot(qs, 0), slot(qs, 2), slot(qs, 5)), (kf[:, :, :, :], slot(ks, 0), slot(ks, 1), slot(ks, 4)),
                             (vf[:, :, :, :], v3[:, :, :, 0, 0:DH], v3[:, :, :, 1, 0:DH], v3[:, :, :, 2, 0:DH]))
                    s = 12 * nb
                    if nb == 0:
                        v.wait_ge(s_w4l, 2 * NQ)
                    for full, p0, p1, p2 in parts:
                        v.tensor_copy(p0, full).then_inc(s_split, 1)
                    v.wait_ge(s_split, s + 3)
                    for full, p0, p1, p2 in parts:
                        v.tensor_tensor(full, full, p0, ALU.subtract).then_inc(s_split, 1)
                    v.wait_ge(s_split, s + 6)
                    for full, p0, p1, p2 in parts:
                        v.tensor_copy(p1, full).then_inc(s_split, 1)
                    v.wait_ge(s_split, s + 9)
                    for full, p0, p1, p2 in parts:
                        v.tensor_tensor(p2, full, p1, ALU.subtract).then_inc(s_split, 1)
                    for f in range(1, 8, 2):
                        v.wait_ge(s_tr, 8 * nb + f + 1)
                        v.tensor_copy(qbuf[f // 4][2][0:SLOT, 4 * (f % 4):4 * (f % 4) + 4, :].rearrange("p h t -> p (h t)"),
                                      ring[f % 4][0:SLOT, :].bitcast(BF16)).then_inc(s_evD, 1)
                    for f in range(12):
                        v.wait_ge(s_s, 12 * nb + f + 1)
                        i = 0 if f < 4 else 1
                        nh = 4 if i == 0 else 2
                        h0 = 4 * f if i == 0 else 2 * (f - 4)
                        v.tensor_reduce(mx[:, i, h0:h0 + nh], ring[f % 4][:, :].rearrange("p (n k) -> p n k", n=nh),
                                        AX.X, ALU.max).then_inc(s_mx, 1)
                    v.wait_ge(s_mx, 12 * (nb + 1))
                    v.tensor_scalar(nm[:, :, 0, :], mx[:, :, :], -1.0, None, ALU.mult).then_inc(s_nm, 1)
                    v.wait_ge(s_nm, 2 * nb + 1)
                    v.scalar_tensor_tensor(out=nm[:, :, 1, :], in0=mx[:, :, :], scalar=-1.0, in1=nm[:, :, 0, :],
                                           op0=ALU.mult, op1=ALU.subtract).then_inc(s_nm, 1)

                    def probs(hg, nb=nb):
                        for part in range(3):
                            n = 12 * nb + 3 * hg + part
                            v.wait_ge(s_e, n + 1)
                            if hg >= 2:
                                v.wait_ge(s_y, 4 * nb + hg - 1)
                            v.tensor_copy(ph[:, 3 * (hg % 2) + part, :], ex[:, n % 2, :]).then_inc(s_ph, 1)

                    def normalize(hg, nb=nb):
                        n = 4 * nb + hg
                        v.wait_ge(s_y, n + 1)
                        if n >= 1:
                            v.wait_ge(s_yn, n)
                        bank = (pm, pv)[hg % 2][:, 0:8 * 51].rearrange("p (x s d) -> p x d s", x=8, s=3)
                        v.tensor_reduce(ys[:, :, :], bank, AX.X, ALU.add).then_inc(s_yst, 1)
                        v.wait_ge(s_yst, 2 * n + 1)
                        v.reciprocal(yr[:, :], ys[:, :, DH]).then_inc(s_yst, 1)
                        v.wait_ge(s_yst, 2 * n + 2)
                        for i in range(2):
                            last = v.tensor_tensor(y[:, i, 4 * hg:4 * hg + 4, :], ys[:, 4 * i:4 * i + 4, 0:DH],
                                                   yr[:, 4 * i:4 * i + 4].unsqueeze(2).to_broadcast([P, 4, DH]),
                                                   ALU.mult)
                        last.then_inc(s_yn, 1)

                    probs(0)
                    for hg in range(4):
                        if hg < 3:
                            probs(hg + 1)
                        normalize(hg)
                    v.wait_ge(s_yh, nb + 1)
                    if nb >= 1:
                        v.wait_ge(s_ao, nb)
                    sub(yl[:, :, :], pm[:, :].rearrange("p (k t) -> p k t", k=KD), yh[:, :, :]).then_inc(s_yl, 1)
                v.wait_ge(s_pl, 24 * (g + 1))
                for t in range(T1):
                    gated(T0 * G + g * T1 + t, t, P)
                v.wait_ge(s_dn, T0 * G + T1 * (g + 1))
                for j in range(KD):
                    last = v.scalar_tensor_tensor(out=xg(g)[:, j, :], in0=acc[:, j, :], scalar=bout[:, j:j + 1],
                                                  in1=xg(g)[:, j, :], op0=ALU.add, op1=ALU.add)
                last.then_inc(s_res, 1)


def _layouts(i):
    import numpy as np

    a = {k: np.asarray(v) for k, v in i.items()}
    f = np.float32
    perm = np.concatenate([np.arange(0, D, 2), np.arange(1, D, 2)])

    def rows2(w):
        return w.reshape(P, KD, -1)

    def tiles(w, n):
        full = np.zeros((n * P, w.shape[1]), f)
        full[:w.shape[0]] = w
        return full.reshape(n, P, -1).transpose(1, 0, 2)

    flat = lambda parts: np.ascontiguousarray(np.concatenate([p.reshape(P, -1) for p in parts], 1))
    ew = lambda w: w.reshape(N_EXP * E_FF, D).T
    w0 = flat([rows2(a["L0_attn_Wq"].T), rows2(a["L0_attn_Wk"].T), rows2(a["L0_attn_Wv"].T),
               tiles(a["L0_attn_Wo"].T[:, perm], KD),
               rows2(a["L0_ffn_shared_wg"].T), rows2(a["L0_ffn_shared_wu"].T),
               tiles(a["L0_ffn_shared_wd"].T[:, perm], ST),
               rows2(ew(a["L0_ffn_exp_wg"])), rows2(ew(a["L0_ffn_exp_wu"])),
               tiles(a["L0_ffn_exp_wd"].transpose(0, 2, 1).reshape(N_EXP * E_FF, D)[:, perm], XT)])
    dn = np.zeros((D, 256), f)
    dn[:, :D_Q] = a["L1_attn_W_d_q"].T
    dn[:, D_Q:C_W] = a["L1_attn_W_d_kv"].T
    wa = flat([rows2(dn), tiles(a["L1_attn_W_u_q"].T, 1), tiles(a["L1_attn_W_u_kv"].T, 1),
               tiles(a["L1_attn_W_o"].T[:, perm], KD)])
    lng = np.zeros((P, 4), f)
    lng[:D_Q, 0], lng[:D_Q, 1] = a["L1_attn_q_norm_g"], a["L1_attn_q_norm_b"]
    lng[:, 2], lng[:, 3] = a["L1_attn_kv_norm_g"], a["L1_attn_kv_norm_b"]
    order = np.array([2 * ((t // 2) * P + p) + t % 2 for t in range(T1) for p in range(P)])
    up = lambda w: w[order].T.reshape(P, 4, QW)
    down = a["L1_ffn_down_W_packed"].T[:, perm].reshape(8, P, D).transpose(1, 0, 2).reshape(P, 4, QW)
    q4 = np.concatenate([up(a["L1_ffn_gate_W_packed"]), up(a["L1_ffn_up_W_packed"]), down], 1)
    ups = lambda w: np.repeat(w[order].T, 16, 0).reshape(P, 4, QW)
    downs = np.repeat(a["L1_ffn_down_scales"].T[:, perm], 16, 0).reshape(8, P, D).transpose(1, 0, 2).reshape(P, 4, QW)
    s4 = np.concatenate([ups(a["L1_ffn_gate_scales"]), ups(a["L1_ffn_up_scales"]), downs], 1)

    bf16 = lambda c: (c.view(np.uint32) >> 16).astype(np.uint16)
    sel = np.zeros((P, N_EXP * E_FF), f)
    for e in range(N_EXP):
        sel[[e, 32 + e], e * E_FF:(e + 1) * E_FF] = 1
    selm = np.zeros((P, H, P), f)
    for h in range(H):
        selm[[h, H + h], h, :] = 1
    masks = np.zeros((2, P, P), f)
    masks[0][np.triu_indices(P, 1)] = MASKED
    masks[1][np.tril_indices(P, -1)] = MASKED
    inv = ((1.0 / 10000.0) ** (np.arange(0, DR, 2, dtype=f) / DR)).astype(f)
    angle = np.arange(H, dtype=f)[:, None] * inv[None, :]
    rot = np.broadcast_to(np.stack([np.cos(angle), np.sin(angle)]).astype(f), (P, 2, H, 4))
    tie = np.broadcast_to((np.arange(N_EXP)[None, :] < np.arange(N_EXP)[:, None]).astype(f), (P, N_EXP, N_EXP))
    return {
        "xT": a["L0_attn_x"].reshape(TOKENS, P, KD).transpose(1, 2, 0), "w0": w0, "gateT": rows2(a["L0_ffn_gate_w"].T),
        "wa": wa, "biasc": np.concatenate([a["L1_attn_b_d_q"], a["L1_attn_b_d_kv"]]), "biasq": a["L1_attn_b_u_q"],
        "biaskv": a["L1_attn_b_u_kv"], "lng": lng, "bo": a["L1_attn_b_o"].reshape(P, KD),
        "ones_c": np.full((P, P), 1.0 / D, f), "sel_c": sel, "selm_c": bf16(selm), "ident_c": np.eye(P, dtype=f),
        "identb_c": bf16(np.eye(P, dtype=f)), "mask_c": bf16(masks), "rot_c": rot, "tie_c": tie, "q4": q4, "s4": s4,
    }


def kernel(**inputs):
    import numpy as np
    import concourse.bacc as bacc
    from concourse.bass_utils import run_bass_kernel_spmd

    nc = bacc.Bacc("TRN2", target_bir_lowering=False, num_devices=1)
    arrays, args = {}, {}
    for name, a in _layouts(inputs).items():
        a = np.ascontiguousarray(a)
        arrays[name] = a
        args[name] = nc.dram_tensor(name, a.shape, mybir.dt.from_np(a.dtype), kind="ExternalInput").ap()
    args["out"] = nc.dram_tensor("out", (P, KD, TOKENS), F32, kind="ExternalOutput").ap()
    transformer_blocks(nc, **args)
    r = run_bass_kernel_spmd(nc, [arrays], core_ids=[0])
    o = r.results[0]["out"]
    return np.ascontiguousarray(o.transpose(2, 0, 1)).reshape(BATCHES, SEQ, D)
```

```python
from contextlib import ExitStack

import concourse.bass as bass
from concourse import mybir

F32 = mybir.dt.float32
F32R = mybir.dt.float32r
BF16 = mybir.dt.bfloat16
F16 = mybir.dt.float16
I32 = mybir.dt.int32
U16 = mybir.dt.uint16
ALU = mybir.AluOpType
ACT = mybir.ActivationFunctionType
AX = mybir.AxisListType

P = 128
D = 256
KD = D // P
BATCHES, SEQ = 8, 256
TOKENS = BATCHES * SEQ
NT = 512
G = TOKENS // NT
EPS = 1e-5

E_FF, N_EXP, SH_FF = 176, 8, 352
XT = N_EXP * E_FF // P
ST = 3
ST_M = [128, 128, SH_FF - 256]
T0 = ST + XT
LN_AT = 5
ROUTE_SCALE = 2.5
DENOM = float(D) ** 0.5 / SEQ

MLP = 2048
T1 = MLP // P
H, DH, DN, DR = 16, 16, 8, 8
D_Q, D_KV = D // 3, D // 2
C_W = D_Q + D_KV + DR
SCALE = float(DH) ** -0.5
SLOT = 6 * DH
MASKED = -1e30

O_QKVO = 0
O_SG = 4 * KD * D
O_SU = O_SG + KD * SH_FF
O_SD = O_SU + KD * SH_FF
O_EG = O_SD + ST * D
O_EU = O_EG + KD * XT * P
O_ED = O_EU + KD * XT * P
W0_COLS = O_ED + XT * D
PIECES0 = [(o + i * w // 2, o + (i + 1) * w // 2) for o, w in (
    (0, O_SG), (O_SG, O_EG - O_SG), (O_EG, O_EU - O_EG), (O_EU, O_ED - O_EU), (O_ED, W0_COLS - O_ED)) for i in range(2)]
O_G4 = 0
O_U4 = KD * MLP
O_D4 = 2 * KD * MLP
A_DN = 0
A_UQ = A_DN + KD * 256
A_UKV = A_UQ + D
A_O = A_UKV + D + H * DN
WA_COLS = A_O + KD * D
STAGE = max(b - a for a, b in PIECES0)
SEL_PIECE = len(PIECES0)
QW = 512
NQ = 3 * MLP // QW
Q0 = T0
HB = 3


def transformer_blocks(nc, xT, w0, gateT, wa, biasc, biasq, biaskv, lng, bo, ones_c, sel_c, selm_c, ident_c, identb_c,
                       mask_c, rot_c, tie_c, q4, s4, x1s, w4s, out):
    ctx = ExitStack()
    with ctx:
        def sb(name, shape, dt, where=ctx):
            return where.enter_context(nc.sbuf_tensor(name, shape, dt))

        def sem(name):
            return ctx.enter_context(nc.semaphore(name))

        wh = sb("wh", [P, W0_COLS], F32R)
        wl = sb("wl", [P, W0_COLS], F32R)
        ah = sb("ah", [P, WA_COLS], F32R)
        al = sb("al", [P, WA_COLS], F32R)
        x = sb("x", [P, 2, KD, NT], F32)
        ones = sb("ones", [P, P], F32)
        epsb = sb("epsb", [P, 1], F32)
        identf = sb("identf", [P, P], F32)
        xc = sb("xc", [P, KD, NT], F32)
        sq = sb("sq", [P, KD, NT], F32)
        std = sb("std", [P, NT], F32)
        rstd = std
        xh = sb("xh", [P, KD, NT], F32R)
        xl = sb("xl", [P, KD, NT], F32R)
        act = sb("act", [P, 2, NT], F32)
        hf = sb("hf", [P, 2, NT], F32)
        hh = sb("hh", [P, HB, NT], F32R)
        hl = sb("hl", [P, HB, NT], F32R)

        c0 = ExitStack()
        cs = ExitStack()
        stage = sb("stage", [P, 2, STAGE], F32, cs)
        cs.close()
        words = sb("words", [P, 2, QW], I32, c0)
        fbits = sb("fbits", [P, QW], I32, c0)
        sbits = sb("sbits", [P, QW], I32, c0)
        gval = sb("gval", [P, 2, QW], F32, c0)
        scl = sb("scl", [P, QW], F32, c0)
        wf = sb("wf", [P, QW], F32, c0)
        w4h = sb("w4h", [P, 2, QW], F32R, c0)
        w4l = sb("w4l", [P, 2, QW], F32R, c0)
        sel = sb("sel", [P, XT * P], F32R, c0)
        gw = sb("gw", [P, 2, KD, N_EXP], F32R, c0)
        gwf = sb("gwf", [P, KD, N_EXP], F32, c0)
        vs = sb("vs", [P, 2, NT], F32, c0)
        vhh = sb("vhh", [P, KD, NT], F32R, c0)
        vhl = sb("vhl", [P, KD, NT], F32R, c0)
        sig = sb("sig", [N_EXP, NT], F32, c0)
        sc = sb("sc", [P, 4, N_EXP], F32, c0)
        gt = sb("gt", [P, 4, N_EXP, N_EXP], F32, c0)
        ge = sb("ge", [P, 4, N_EXP, N_EXP], F32, c0)
        unit = sb("unit", [P, 1], F32, c0)
        tie = sb("tie", [P, N_EXP, N_EXP], F32, c0)
        rank = sb("rank", [P, 4, N_EXP], F32, c0)
        rw = sb("rw", [P, 4, N_EXP], F32, c0)
        rsum = sb("rsum", [P, 4], F32, c0)
        rrec = sb("rrec", [P, 4], F32, c0)
        rwn = sb("rwn", [P, 4, N_EXP], F32, c0)
        wT = sb("wT", [P, NT], F32R, c0)
        kv0 = sq
        kvt = vs
        vfl = hf
        c0.close()

        c1 = ctx
        bc = sb("bc", [P, C_W], F32, c1)
        bq = sb("bq", [P, D], F32, c1)
        bkv = sb("bkv", [P, D + H * DN], F32, c1)
        gb = sb("gb", [P, 4], F32, c1)
        bout = sb("bout", [P, KD], F32, c1)
        rot = sb("rot", [P, 2, H, 4], F32, c1)
        ident = sb("ident", [P, P], BF16, c1)
        maskq = sb("maskq", [P, P], BF16, c1)
        maskk = sb("maskk", [P, P], BF16, c1)
        selm = sb("selm", [P, H, P], BF16, c1)
        bst = sb("bst", [P, 4, 6], F32, c1)
        mv = sb("mv", [P, 4, 2], F32, c1)
        cstd = sb("cstd", [P, 4], F32, c1)
        crs = sb("crs", [P, 4], F32, c1)
        rt = sb("rt", [P, 4, 2, H, 4], F32, c1)
        v3 = sb("v3", [P, 2, H, 3, DH + 1], BF16, c1)
        qT = sb("qT", [P, H, SEQ], BF16, c1)
        kT = sb("kT", [P, H, SEQ], BF16, c1)
        mx = sb("mx", [P, 2, H], F32, c1)
        nm = sb("nm", [P, 2, 2, H], BF16, c1)
        mT = sb("mT", [P, SEQ], BF16, c1)
        c2 = ExitStack()
        qs = sb("qs", [P, 2, H, SLOT], BF16, c2)
        ks = sb("ks", [P, 2, H, SLOT], BF16, c2)
        c2.close()
        ph = sb("ph", [P, 6, NT], F16)
        pl = sb("pl", [P, 6, NT], F16)
        flat = lambda t: t[:, :, :].rearrange("p a b -> p (a b)")
        kf = xc[:, 0, :].rearrange("p (t h d) -> p t h d", t=2, h=H)
        vf = xc[:, 1, :].rearrange("p (t h d) -> p t h d", t=2, h=H)
        qf = flat(sq)[:, 0:2 * H * DH].rearrange("p (t h d) -> p t h d", t=2, h=H)
        c = flat(sq)[:, KD * NT - 2 * C_W:].rearrange("p (t n) -> p t n", t=2)
        cn = c
        ctf = std[:, :].rearrange("p (w t) -> p w t", w=2)
        cth, ctl = hh[:, 0:2, SEQ:], hl[:, 0:2, SEQ:]
        yh, yl = hh[:, 0:2, 0:SEQ], hl[:, 0:2, 0:SEQ]
        ex = hf
        y = act[:, 0, :].rearrange("p (i h d) -> p i h d", i=2, h=H)
        ys = act[:, 1, 0:8 * (DH + 1)].rearrange("p (x d) -> p x d", x=8)
        yr = act[:, 1, NT - 8:]
        qbuf = [[qs, qf, qT], [ks, kf, kT]]

        acc = ctx.enter_context(nc.psum_tensor("acc", [P, KD, NT], F32))
        ring = [ctx.enter_context(nc.psum_tensor(f"ring{i}", [P, NT], F32)) for i in range(4)]
        pm = ctx.enter_context(nc.psum_tensor("pm", [P, NT], F32))
        pv = ctx.enter_context(nc.psum_tensor("pv", [P, NT], F32))

        s_x = sem("x_in")
        s_const = sem("constants_in")
        s_stage = [sem(f"weights_in{i}") for i in range(2)]
        s_whi = sem("weights_hi")
        s_wlo = [sem(f"weights_split{i}") for i in range(2)]
        s_gwh = sem("gate_hi")
        s_prep = sem("small_set_up")
        s_mean, s_xc, s_sq, s_var, s_std = map(sem, ("mean", "centred", "squares", "variance", "deviation"))
        s_rstd, s_xn, s_xh, s_xl = map(sem, ("inverse_deviation", "normed", "normed_hi", "normed_split"))
        s_xdone = sem("normed_used")
        s_v, s_k, s_q = map(sem, ("v_product", "k_product", "q_product"))
        s_vs, s_kv, s_scan, s_vh, s_vhh, s_vhl = map(
            sem, ("v_scaled", "kv", "kv_summed", "vhat", "vhat_hi", "vhat_split"))
        s_oproj = sem("vhat_used")
        s_lg, s_sig, s_st, s_rk, s_wt, s_wth, s_wtl = map(
            sem, ("logits", "scores", "scores_turned", "route_steps", "weights_turned", "weights_hi_in",
                  "weights_lo_in"))
        s_gu, s_act, s_wbc, s_h, s_hw, s_hh, s_hl, s_dn = map(
            sem, ("gate_up", "activated", "route_spread", "gated", "routed", "h_hi", "h_split", "h_used"))
        s_res = sem("residual")
        s_out = sem("stored")
        s_words = [sem(f'words_in{i}') for i in range(2)]
        s_scl, s_bits, s_val, s_sgn, s_w, s_w4h, s_w4l = map(
            sem, ("scales_in", "bit_steps", "values", "signs", "w4", "w4_hi", "w4_split"))
        s_w4out, s_w4in = [sem(f"w4_stored{i}") for i in range(2)], sem("w4_in")
        s_cps, s_c, s_bn, s_cstd, s_crs, s_cn, s_ctr, s_ct, s_cth, s_ctl = map(
            sem, ("latents", "latents_biased", "latent_stats", "latent_deviation", "latent_inverse",
                  "latents_normed", "latents_turned", "latents_affine", "latents_hi", "latents_split"))
        s_qkv, s_qkvb, s_rope, s_split, s_copy = map(
            sem, ("qkv", "qkv_biased", "rotary_steps", "split_steps", "slots_copied"))
        s_tr, s_evA, s_evD = map(sem, ("slots_turned", "turned_by_act", "turned_by_dve"))
        s_s, s_mx, s_nm, s_mtr, s_mT = map(sem, ("score_bank", "score_max", "max_split", "max_turned", "max_in"))
        s_sT, s_e, s_ph, s_pl, s_y, s_yst, s_yn = map(
            sem, ("score_bank_turned", "exponentials", "probs_hi", "probs_split", "y_bank", "y_steps", "y_normed"))
        s_ytr, s_yh, s_yl, s_ao = map(sem, ("y_turned", "y_hi", "y_split", "y_used"))

        SETUP0, SETUP1 = 4, 3

        def xg(n):
            return x[:, n % 2, :, :]

        def x1_at(g):
            return x1s[:, :, g * NT:(g + 1) * NT]

        pieces = [(w0[:, a:b], wh[:, a:b], wl[:, a:b]) for a, b in PIECES0]
        pieces.append((sel_c, sel[:, :], None))
        pieces += [(wa[:, a:b], ah[:, a:b], al[:, a:b]) for a, b in ((0, WA_COLS // 2), (WA_COLS // 2, WA_COLS))]
        step_at = lambda tile: 2 * ((tile - Q0) // 3) + (tile - Q0) % 3 if (tile - Q0) % 3 < 2 else -1
        step_at = lambda tile: 2 * ((tile - Q0) // 3) + (tile - Q0) % 3 if (tile - Q0) % 3 < 2 else -1
        staged = lambda n: stage[:, n % 2, 0:pieces[n][0].shape[1]]
        lo_of = {0: [n for n in range(0, len(pieces), 2) if n != SEL_PIECE], 1: list(range(1, len(pieces), 2))}

        def w0k(off, width, k, a, b):
            return slice(off + k * width + a, off + k * width + b)

        consts = [(ones, ones_c), (identf, ident_c)]
        def w4_at(dst, n, j):
            if n < 8:
                off = (O_G4, O_U4)[n // 4] + j * MLP + (n % 4) * QW
                return dst[:, off:off + QW]
            v = dst[:, O_D4:O_D4 + T1 * D].rearrange("p (c j d) -> p c j d", c=T1 // 2, j=2)
            return v[:, 2 * (n - 8):2 * (n - 8) + 2, j, :]

        block = ctx.enter_context(nc.Block())

        @block.sync
        def _(sp):
            sp.dma_start(xg(0), xT[:, :, 0:NT]).then_inc(s_x, 16)
            for t, src in consts:
                sp.dma_start(t[:, :], src).then_inc(s_const, 16)
            sp.dma_start(gwf[:, :, :], gateT).then_inc(s_const, 16)
            sp.dma_start(tie[:, :, :], tie_c).then_inc(s_const, 16)
            for n, (src, _, _) in enumerate(pieces):
                if n - 2 == SEL_PIECE:
                    sp.wait_ge(s_whi, SEL_PIECE + 1)
                elif n >= 2:
                    sp.wait_ge(s_wlo[n % 2], lo_of[n % 2].index(n - 2) + 1)
                sp.dma_start(staged(n), src).then_inc(s_stage[n % 2], 16)
                if n == 1:
                    sp.wait_ge(s_x, 16)
                    sp.dma_start(xg(1), xT[:, :, NT:2 * NT]).then_inc(s_x, 16)
            for i in range(2):
                sp.wait_ge(s_wlo[i], len(lo_of[i]))
            for k in range(2 * NQ + 2):
                if k % 2 == 0:
                    for n in (0, 1) if k == 0 else (k // 2 + 1,) if k // 2 + 1 < NQ else ():
                        if n >= 2:
                            sp.wait_ge(s_bits, 6 * (n - 1))
                        sp.dma_start(words[:, n % 2, :], q4[:, n, :]).then_inc(s_words[n % 2], 16)
                if k >= 2:
                    sp.wait_ge(s_w4l, k - 1)
                    for i, part in enumerate((w4h, w4l)):
                        sp.dma_start(w4_at(w4s[i], (k - 2) // 2, k % 2), part[:, k % 2, :].bitcast(F32)).then_inc(
                            s_w4out[k % 2], 16)
                if k % 2 == 0 and k < 2 * NQ:
                    if k:
                        sp.wait_ge(s_w, k)
                    sp.dma_start(scl[:, :], s4[:, k // 2, :]).then_inc(s_scl, 16)
            for i in range(2):
                sp.wait_ge(s_w4out[i], 32 * NQ)

            def w4_load(a, b):
                for i, dst in enumerate((wh, wl)):
                    sp.dma_start(dst[:, a:b].bitcast(F32), w4s[i][:, a:b]).then_inc(s_w4in, 16)

            sp.wait_ge(s_oproj, G)
            w4_load(0, O_SG)
            sp.wait_ge(s_res, G)
            for t, src in ((bc[:, :], biasc.partition_broadcast(P)), (bq[:, :], biasq.partition_broadcast(P)),
                           (bkv[:, :], biaskv.partition_broadcast(P)), (gb[:, :], lng), (bout[:, :], bo),
                           (rot[:, :, :, :], rot_c), (ident[:, :], identb_c.bitcast(BF16)),
                           (maskq[:, :], mask_c[0].bitcast(BF16)), (maskk[:, :], mask_c[1].bitcast(BF16)),
                           (selm[:, :, :], selm_c.bitcast(BF16))):
                sp.dma_start(t, src).then_inc(s_const, 16)
            sp.dma_start(x1_at(G - 1), xg(G - 1)).then_inc(s_out, 16)
            sp.wait_ge(s_dn, T0 * G)
            w4_load(O_SG, 3 * KD * MLP)
            for n in range(G, 2 * G + 1):
                if n > G:
                    sp.wait_ge(s_res, n)
                    sp.dma_start(out[:, :, (n - 1 - G) * NT:(n - G) * NT], xg(n - 1)).then_inc(s_out, 16)
                sp.wait_ge(s_out, 16 * n)
                if n + 1 < 2 * G:
                    sp.dma_start(xg(n + 1), x1_at(n + 1 - G)).then_inc(s_x, 16)

        @block.tensor
        def _(pe):
            def prod(o, lo_hi_w, x_hi, x_lo, first, last):
                w_hi, w_lo = lo_hi_w
                pe.matmul(o, w_hi, x_hi, start=first, stop=False, skip_group_check=True)
                pe.matmul(o, w_lo, x_hi, start=False, stop=False, skip_group_check=True)
                return pe.matmul(o, w_hi, x_lo, start=False, stop=last, skip_group_check=True)

            def ln_mean(n):
                pe.wait_ge(s_x, 16 * (n + 1))
                for k in range(KD):
                    mm = pe.matmul(pm[:, :], ones[:, :], xg(n)[:, k, :], start=k == 0, stop=k == KD - 1)
                mm.then_inc(s_mean, 1)

            def ln_var(n):
                pe.wait_ge(s_sq, n + 1)
                for k in range(KD):
                    mm = pe.matmul(pm[:, :], ones[:, :], sq[:, k, :], start=k == 0, stop=k == KD - 1)
                mm.then_inc(s_var, 1)

            def normed(n):
                pe.wait_ge(s_xl, n + 1)
                pe.wait_ge(s_xh, n + 1)

            def w(off, width, k, a, b):
                s = w0k(off, width, k, a, b)
                return wh[:, s], wl[:, s]

            def down(tile_no, off, kt, rows, last):
                pe.wait_ge(s_hl, tile_no + 1)
                b = tile_no % HB
                for m in range(KD):
                    s = w0k(off, D, kt, m * P, (m + 1) * P)
                    mm = prod(acc[:, m, :], (wh[0:rows, s], wl[0:rows, s]), hh[0:rows, b, :], hl[0:rows, b, :],
                              False, last)
                mm.then_inc(s_dn, 1)

            pe.wait_ge(s_const, 64)
            for g in range(G):
                if g == 0:
                    ln_mean(0)
                    ln_var(0)
                normed(g)
                if g == 0:
                    pe.wait_ge(s_wlo[0], 1)
                    pe.wait_ge(s_wlo[1], 1)
                    pe.wait_ge(s_prep, SETUP0)
                else:
                    pe.wait_ge(s_h, T0 * g)
                for m in range(KD):
                    for j, (which, bank, s) in enumerate(((2, (0, 3), s_v), (1, (1, 0), s_k), (0, (2, 1), s_q))):
                        if m == 1 and j == 1:
                            pe.wait_ge(s_vs, 2 * g + 1)
                        if m == 1 and j == 2:
                            pe.wait_ge(s_kv, 2 * g + 1)
                        for k in range(KD):
                            mm = prod(ring[bank[m]][:, :], w(O_QKVO + which * KD * D, D, k, m * P, (m + 1) * P),
                                      xh[:, k, :], xl[:, k, :], k == 0, k == KD - 1)
                        mm.then_inc(s, 1)
                for k in range(KD):
                    mm = prod(pm[0:N_EXP, :], (gw[:, 0, k, :], gw[:, 1, k, :]), xh[:, k, :], xl[:, k, :],
                              k == 0, k == KD - 1)
                mm.then_inc(s_lg, 1)
                pe.wait_ge(s_sig, g + 1)
                for t in range(4):
                    mm = pe.transpose(pv[:, t * N_EXP:(t + 1) * N_EXP], sig[:, t * P:(t + 1) * P],
                                      identf[0:N_EXP, 0:N_EXP])
                mm.then_inc(s_st, 1)
                pe.wait_ge(s_vhl, 2 * g + 2)
                if g >= 1:
                    pe.wait_ge(s_res, g)
                for m in range(KD):
                    for k in range(KD):
                        mm = prod(acc[:, m, :], w(O_QKVO + 3 * KD * D, D, k, m * P, (m + 1) * P),
                                  vhh[:, k, :], vhl[:, k, :], k == 0, False)
                mm.then_inc(s_oproj, 1)
                pe.wait_ge(s_rk, 11 * (g + 1))
                for t in range(4):
                    mm = pe.transpose(pm[0:N_EXP, t * P:(t + 1) * P], rwn[:, t, :], identf[:, :])
                mm.then_inc(s_wt, 1)

                def gate_up(t):
                    n = g * T0 + t
                    if t >= 2:
                        pe.wait_ge(s_h, n - 1)
                    else:
                        pe.wait_ge(s_vh, 2 * g + 2)
                    rows = ST_M[t] if t < ST else P
                    for o, off, eoff in ((2 * (t % 2), O_SG, O_EG), (2 * (t % 2) + 1, O_SU, O_EU)):
                        for k in range(KD):
                            if t < ST:
                                ww = w(off, SH_FF, k, t * P, t * P + rows)
                            else:
                                ww = w(eoff, XT * P, k, (t - ST) * P, (t - ST + 1) * P)
                            mm = prod(ring[o][0:rows, :], ww, xh[:, k, :], xl[:, k, :], k == 0, k == KD - 1)
                    mm.then_inc(s_gu, 1)
                    if t >= ST:
                        e = g * XT + t - ST
                        if t == ST:
                            pe.wait_ge(s_wtl, g + 1)
                            pe.wait_ge(s_rk, 11 * g + 1)
                        if e >= 1:
                            pe.wait_ge(s_hw, e)
                        pe.matmul(pv[:, :], sel[:, (t - ST) * P:(t - ST + 1) * P], wT[:, :], start=True,
                                  stop=True).then_inc(s_wbc, 1)

                def down0(u):
                    down(g * T0 + u, O_SD if u < ST else O_ED, u if u < ST else u - ST, ST_M[u] if u < ST else P,
                         u == T0 - 1)

                for t in range(T0):
                    if g == 0 and t == 0:
                        pe.wait_ge(s_wlo[0], 2)
                        pe.wait_ge(s_wlo[1], 2)
                    if g == 0 and t == ST:
                        pe.wait_ge(s_wlo[0], 5)
                        pe.wait_ge(s_wlo[1], 5)
                        pe.wait_ge(s_whi, SEL_PIECE + 1)
                    gate_up(t)
                    if t >= 2:
                        down0(t - 2)
                    if t == LN_AT:
                        ln_mean(g + 1)
                    if t == LN_AT + 3:
                        ln_var(g + 1)
                down0(T0 - 2)
                down0(T0 - 1)

            pe.wait_ge(s_const, 16 * 14)
            pe.wait_ge(s_prep, SETUP0 + SETUP1)
            for g in range(G):
                normed(G + g)
                for hb in range(2):
                    nb = 2 * g + hb
                    tok = lambda t: slice(hb * SEQ + t * P, hb * SEQ + (t + 1) * P)
                    if nb == 0:
                        pe.wait_ge(s_h, T0 * G)
                        pe.wait_ge(s_res, G)
                        pe.wait_ge(s_wlo[0], len(lo_of[0]))
                        pe.wait_ge(s_wlo[1], len(lo_of[1]))
                    elif hb == 0:
                        pe.wait_ge(s_h, T0 * G + T1 * g)
                    else:
                        pe.wait_ge(s_e, 12 * nb)
                    for t in range(2):
                        for k in range(KD):
                            s = w0k(A_DN, 256, k, 0, 256)
                            xx = (xh[:, k, tok(t)], xl[:, k, tok(t)])
                            pe.matmul(ring[t][:, 0:256], xx[0], ah[:, s], start=k == 0, stop=False)
                            pe.matmul(ring[t][:, 0:256], xx[1], ah[:, s], start=False, stop=False)
                            mm = pe.matmul(ring[t][:, 0:256], xx[0], al[:, s], start=False, stop=k == KD - 1)
                        mm.then_inc(s_cps, 1)
                    pe.wait_ge(s_cn, 4 * (nb + 1))
                    for t in range(2):
                        pe.transpose(pm[0:D_Q, t * P:(t + 1) * P], cn[:, t, 0:D_Q], identf[:, :])
                        mm = pe.transpose(pm[:, SEQ + t * P:SEQ + (t + 1) * P], cn[:, t, D_Q:D_Q + D_KV], identf[:, :])
                    mm.then_inc(s_ctr, 1)
                    pe.wait_ge(s_ctl, 2 * nb + 2)
                    for t in range(2):
                        for which, off, width, bank in ((0, A_UQ, D, t), (1, A_UKV, D + H * DN, 2 + t)):
                            rows = (D_Q, P)[which]
                            ch, cl = cth[0:rows, which, t * P:(t + 1) * P], ctl[0:rows, which, t * P:(t + 1) * P]
                            o = ring[bank][:, 0:width]
                            pe.matmul(o, ch, ah[0:rows, off:off + width], start=True, stop=False)
                            pe.matmul(o, cl, ah[0:rows, off:off + width], start=False, stop=False)
                            mm = pe.matmul(o, ch, al[0:rows, off:off + width], start=False, stop=True)
                        mm.then_inc(s_qkv, 1)
                    pe.wait_ge(s_split, 12 * (nb + 1))
                    pe.wait_ge(s_copy, 6 * (nb + 1))
                    for f in range(8):
                        if f >= 4:
                            (pe.wait_ge(s_evA, 4 * nb + (f - 4) // 2 + 1) if f % 2 == 0
                             else pe.wait_ge(s_evD, 4 * nb + (f - 4) // 2 + 1))
                        src = qbuf[f // 4][0]
                        bank = ring[f % 4][:, :].bitcast(BF16)
                        for h in range(4):
                            for t in range(2):
                                mm = pe.transpose(bank[0:SLOT, h * SEQ + t * P:h * SEQ + (t + 1) * P],
                                                  src[:, t, 4 * (f % 4) + h, :], ident[:, :])
                        mm.then_inc(s_tr, 1)
                    for f in range(12):
                        if f < 4:
                            (pe.wait_ge(s_evA, 4 * nb + 4) if f == 0 else None)
                            (pe.wait_ge(s_evD, 4 * nb + 4) if f == 0 else None)
                        else:
                            pe.wait_ge(s_mx, 12 * nb + f - 3)
                        i = 0 if f < 4 else 1
                        width = (i + 1) * P
                        heads = range(4 * f, 4 * f + 4) if i == 0 else range(2 * (f - 4), 2 * (f - 4) + 2)
                        for n, h in enumerate(heads):
                            o = ring[f % 4][:, n * width:(n + 1) * width]
                            pe.matmul(o, qT[0:SLOT, h, i * P:(i + 1) * P], kT[0:SLOT, h, 0:width], start=True, stop=False,
                                      skip_group_check=True)
                            mm = pe.matmul(o[:, i * P:(i + 1) * P], ident[:, :], maskq[:, :], start=False, stop=True,
                                           skip_group_check=True)
                        mm.then_inc(s_s, 1)
                    pe.wait_ge(s_nm, 2 * nb + 2)
                    mbank = pm[:, :].bitcast(BF16)
                    for i in range(2):
                        mm = pe.transpose(mbank[0:2 * H, i * P:(i + 1) * P],
                                          nm[:, i, :, :].rearrange("p a h -> p (a h)"), ident[:, :])
                    mm.then_inc(s_mtr, 1)
                    pe.wait_ge(s_mT, nb + 1)

                    def probs(hg, nb=nb):
                        for part in range(3):
                            f = 3 * hg + part
                            if f >= 4:
                                pe.wait_ge(s_e, 12 * nb + f - 3)
                            elif f == 0:
                                pe.wait_ge(s_mx, 12 * nb + 12)
                            kt = 0 if part < 2 else 1
                            heads = range(4 * hg + 2 * part, 4 * hg + 2 * part + 2) if kt == 0 else \
                                range(4 * hg, 4 * hg + 4)
                            width = SEQ - kt * P
                            for n, h in enumerate(heads):
                                o = ring[f % 4][:, n * width:(n + 1) * width]
                                pe.matmul(o, kT[0:SLOT, h, kt * P:(kt + 1) * P], qT[0:SLOT, h, kt * P:SEQ], start=True,
                                          stop=False, skip_group_check=True)
                                pe.matmul(o, selm[:, h, :], mT[:, kt * P:SEQ], start=False, stop=False,
                                          skip_group_check=True)
                                mm = pe.matmul(o[:, 0:P], ident[:, :], maskk[:, :], start=False, stop=True,
                                               skip_group_check=True)
                            mm.then_inc(s_sT, 1)

                    def values(hg, nb=nb):
                        pe.wait_ge(s_ph, 12 * nb + 3 * hg + 3)
                        pe.wait_ge(s_pl, 12 * nb + 3 * hg + 3)
                        bank = (pm, pv)[hg % 2]
                        if hg >= 2:
                            pe.wait_ge(s_yn, 4 * nb + hg - 1)
                        half = 3 * (hg % 2)
                        for i in range(2):
                            for hn in range(4):
                                o = bank[:, (4 * i + hn) * 51:(4 * i + hn + 1) * 51]
                                for kt in range(i + 1):
                                    if kt == 0:
                                        slot, col = half + hn // 2, (hn % 2) * SEQ + i * P
                                    else:
                                        slot, col = half + 2, hn * P
                                    vv = v3[:, kt, 4 * hg + hn, :, :].rearrange("p s d -> p (s d)")
                                    pe.matmul(o, ph[:, slot, col:col + P], vv, start=kt == 0, stop=False,
                                              skip_group_check=True)
                                    mm = pe.matmul(o, pl[:, slot, col:col + P], vv, start=False, stop=kt == i,
                                                   skip_group_check=True)
                        mm.then_inc(s_y, 1)

                    probs(0)
                    for hg in range(4):
                        if hg < 3:
                            probs(hg + 1)
                        values(hg)
                    pe.wait_ge(s_yn, 4 * nb + 4)
                    for m in range(KD):
                        for i in range(2):
                            mm = pe.transpose(pm[:, m * SEQ + i * P:m * SEQ + (i + 1) * P],
                                              y[:, i, 8 * m:8 * m + 8, :].rearrange("p h d -> p (h d)"), identf[:, :])
                    mm.then_inc(s_ytr, 1)
                    pe.wait_ge(s_yl, nb + 1)
                    if hb == 0:
                        pe.wait_ge(s_res, G + g)
                    for m in range(KD):
                        for k in range(KD):
                            s = w0k(A_O, D, k, m * P, (m + 1) * P)
                            mm = prod(acc[:, m, hb * SEQ:(hb + 1) * SEQ], (ah[:, s], al[:, s]), yh[:, k, :],
                                      yl[:, k, :], hb == 0 and k == 0, False)
                    mm.then_inc(s_ao, 1)

                def gate_up1(t):
                    n = T0 * G + g * T1 + t
                    if t >= 2:
                        pe.wait_ge(s_h, n - 1)
                    else:
                        pe.wait_ge(s_e, 24 * (g + 1))
                    for o, off in ((2 * (t % 2), O_G4), (2 * (t % 2) + 1, O_U4)):
                        for k in range(KD):
                            mm = prod(ring[o][:, :], w(off, MLP, k, t * P, (t + 1) * P), xh[:, k, :], xl[:, k, :],
                                      k == 0, k == KD - 1)
                    mm.then_inc(s_gu, 1)

                if g == 0:
                    pe.wait_ge(s_w4in, 64)
                for t in range(T1):
                    gate_up1(t)
                    if t >= 2:
                        down(T0 * G + g * T1 + t - 2, O_D4, t - 2, P, False)
                    if g < G - 1 and t == LN_AT:
                        ln_mean(G + g + 1)
                    if g < G - 1 and t == LN_AT + 3:
                        ln_var(G + g + 1)
                for t in (T1 - 2, T1 - 1):
                    down(T0 * G + g * T1 + t, O_D4, t, P, t == T1 - 1)

        @block.scalar
        def _(a):
            def ln_square(n):
                a.wait_ge(s_xc, n + 1)
                a.activation(sq[:, :, :], xc[:, :, :], ACT.Square).then_inc(s_sq, 1)

            def ln_std(n):
                a.wait_ge(s_var, n + 1)
                a.activation(std[:, :], pm[:, :], ACT.Sqrt, bias=epsb[:, :]).then_inc(s_std, 1)

            def ln_hi(n):
                a.wait_ge(s_xn, n + 1)
                if n >= 1:
                    a.wait_ge(s_gu, T0 * n if n <= G else T0 * G + T1 * (n - G))
                a.activation(xh[:, :, :], xc[:, :, :], ACT.Copy).then_inc(s_xh, 1)

            def weights(*which):
                for n in which:
                    a.wait_ge(s_stage[n % 2], 16 * (n // 2 + 1))
                    a.activation(pieces[n][1], staged(n), ACT.Copy).then_inc(s_whi, 1)

            def dequant(k):
                if 2 <= k < 2 * NQ + 2:
                    a.wait_ge(s_w, k - 1)
                    if k >= 4:
                        a.wait_ge(s_w4out[k % 2], 32 * (k // 2 - 1))
                    a.activation(w4h[:, k % 2, :], wf[:, :], ACT.Copy).then_inc(s_w4h, 1)
                if 0 <= k < 2 * NQ:
                    a.wait_ge(s_bits, 3 * (k + 1))
                    a.activation(gval[:, k % 2, :], fbits[:, :].bitcast(F32), ACT.Copy, bias=-1.0,
                                 scale=8.0).then_inc(s_val, 1)

            def activate(n, g_t, rows, func):
                a.wait_ge(s_gu, n + 1)
                if n >= 2:
                    a.wait_ge(s_h, n - 1)
                a.activation(act[0:rows, n % 2, :], ring[2 * (g_t % 2)][0:rows, :], func).then_inc(s_act, 1)

            def split_h(n, rows, routed):
                if routed is None:
                    a.wait_ge(s_h, n + 1)
                else:
                    a.wait_ge(s_hw, routed + 1)
                if n >= HB:
                    a.wait_ge(s_dn, n - HB + 1)
                a.activation(hh[0:rows, n % HB, :], hf[0:rows, n % 2, :], ACT.Copy).then_inc(s_hh, 1)

            weights(0)
            ln_square(0)
            weights(1)
            a.wait_ge(s_const, 64)
            a.activation(gw[:, 0, :, :], gwf[:, :, :], ACT.Copy).then_inc(s_gwh, 1)
            a.wait_ge(s_prep, SETUP0)
            ln_std(0)
            ln_hi(0)
            for g in range(G):
                if g == 0:
                    weights(2)
                for m in range(KD):
                    a.wait_ge(s_v, 2 * g + m + 1)
                    a.activation(vs[:, m, :], ring[(0, 3)[m]][:, :], ACT.Copy, scale=DENOM).then_inc(s_vs, 1)
                    if g == 0 and m == 0:
                        weights(3)
                if g >= 1:
                    a.wait_ge(s_res, g)
                    a.dma_start(x1_at(g - 1), xg(g - 1)).then_inc(s_out, 16)
                if g == 0:
                    weights(4)
                a.wait_ge(s_lg, g + 1)
                a.activation(sig[:, :], pm[0:N_EXP, :], ACT.Sigmoid).then_inc(s_sig, 1)
                for m in range(KD):
                    a.wait_ge(s_vh, 2 * g + m + 1)
                    if g >= 1 and m == 0:
                        a.wait_ge(s_oproj, g)
                    a.activation(vhh[:, m, :], vfl[:, m, :], ACT.Copy).then_inc(s_vhh, 1)
                if g == 0:
                    weights(5, 6)
                a.wait_ge(s_wt, g + 1)
                if g >= 1:
                    a.wait_ge(s_wbc, XT * g)
                a.activation(wT[0:N_EXP, :], pm[0:N_EXP, :], ACT.Copy).then_inc(s_wth, 1)
                if g >= 1:
                    a.wait_ge(s_out, 16 * g)
                    a.dma_start(xg(g + 1), xT[:, :, (g + 1) * NT:(g + 2) * NT] if g + 1 < G else x1_at(0)).then_inc(s_x, 16)
                for t in range(T0):
                    n = g * T0 + t
                    activate(n, t, ST_M[t] if t < ST else P, ACT.Silu)
                    if g == 0 and t < ST:
                        weights(*((7, 8), (9,), (SEL_PIECE, SEL_PIECE + 1, SEL_PIECE + 2))[t])
                    if t >= 1:
                        u = t - 1
                        split_h(n - 1, ST_M[u] if u < ST else P, None if u < ST else g * XT + u - ST)
                    dequant(step_at(n))
                    if t == LN_AT + 2:
                        ln_square(g + 1)
                    if t == LN_AT + 4:
                        ln_std(g + 1)
                split_h(g * T0 + T0 - 1, P, g * XT + XT - 1)
                ln_hi(g + 1)

            for g in range(G):
                for hb in range(2):
                    nb = 2 * g + hb
                    a.wait_ge(s_bn, 8 * (nb + 1))
                    a.activation(cstd[:, :], mv[:, :, 1], ACT.Sqrt, bias=epsb[:, :]).then_inc(s_cstd, 1)
                    for which in range(2):
                        a.wait_ge(s_ct, 2 * nb + which + 1)
                        rows = (D_Q, P)[which]
                        a.activation(cth[0:rows, which, :], ctf[0:rows, which, :], ACT.Copy).then_inc(s_cth, 1)
                    for f in range(0, 8, 2):
                        a.wait_ge(s_tr, 8 * nb + f + 1)
                        a.activation(qbuf[f // 4][2][0:SLOT, 4 * (f % 4):4 * (f % 4) + 4, :].rearrange("p h t -> p (h t)"),
                                     ring[f % 4][0:SLOT, :].bitcast(BF16), ACT.Copy).then_inc(s_evA, 1)
                    a.wait_ge(s_mtr, nb + 1)
                    a.activation(mT[0:2 * H, :], pm[:, :].bitcast(BF16)[0:2 * H, 0:SEQ], ACT.Copy).then_inc(s_mT, 1)
                    for f in range(12):
                        n = 12 * nb + f
                        a.wait_ge(s_sT, n + 1)
                        if f == 0 and hb == 0:
                            a.wait_ge(s_hl, T0 * G + T1 * g)
                        if n >= 2:
                            a.wait_ge(s_ph, n - 1)
                            a.wait_ge(s_pl, n - 1)
                        a.activation(ex[:, n % 2, :], ring[f % 4][:, :], ACT.Exp, scale=SCALE).then_inc(s_e, 1)
                    a.wait_ge(s_ytr, nb + 1)
                    if nb >= 1:
                        a.wait_ge(s_ao, nb)
                    a.activation(yh[:, :, :], pm[:, :].rearrange("p (k t) -> p k t", k=KD), ACT.Copy).then_inc(s_yh, 1)
                for t in range(T1):
                    n = T0 * G + g * T1 + t
                    activate(n, t, P, ACT.Gelu_apprx_tanh)
                    if t >= 1:
                        split_h(n - 1, P, None)
                    if g < G - 1 and t == LN_AT + 2:
                        ln_square(G + g + 1)
                    if g < G - 1 and t == LN_AT + 4:
                        ln_std(G + g + 1)
                split_h(T0 * G + g * T1 + T1 - 1, P, None)
                if g < G - 1:
                    ln_hi(G + g + 1)

        @block.gpsimd
        def _(pool):
            def low(dst, src, hi):
                return pool.tensor_tensor(dst, src, hi.bitcast(F32), ALU.subtract)

            def split_h(n, rows):
                pool.wait_ge(s_hh, n + 1)
                low(hl[0:rows, n % HB, :], hf[0:rows, n % 2, :], hh[0:rows, n % HB, :]).then_inc(s_hl, 1)

            def weights(*which):
                for n in which:
                    pool.wait_ge(s_whi, n + 1)
                    low(pieces[n][2], staged(n), pieces[n][1]).then_inc(s_wlo[1], 1)

            def dequant(k):
                if 2 <= k < 2 * NQ + 2:
                    pool.wait_ge(s_w4h, k - 1)
                    low(w4l[:, k % 2, :], wf[:, :], w4h[:, k % 2, :]).then_inc(s_w4l, 1)
                if 1 <= k < 2 * NQ + 1:
                    pool.wait_ge(s_sgn, 2 * k)
                    pool.wait_ge(s_scl, 16 * ((k - 1) // 2 + 1))
                    if k >= 2:
                        pool.wait_ge(s_w4l, k - 1)
                    pool.tensor_tensor(wf[:, :], gval[:, (k - 1) % 2, :], scl[:, :], ALU.mult).then_inc(s_w, 1)

            weights(1, 3, 5, 7)
            for g in range(G):
                for t in range(T0):
                    split_h(g * T0 + t, ST_M[t] if t < ST else P)
                    if g == 0 and t < 2:
                        weights((9, SEL_PIECE + 1)[t])
                    dequant(step_at(g * T0 + t))
            pool.wait_ge(s_prep, SETUP0 + SETUP1)
            for g in range(G):
                for hb in range(2):
                    nb = 2 * g + hb
                    for step, t, a0, b0 in ((1, qs, 0, 1), (2, ks, 0, 2), (1, qs, 0, 4), (2, ks, 0, 5), (7, qs, 2, 3),
                                            (8, ks, 1, 3)):
                        pool.wait_ge(s_split, 12 * nb + step)
                        pool.tensor_copy(t[:, :, :, b0 * DH:(b0 + 1) * DH],
                                         t[:, :, :, a0 * DH:(a0 + 1) * DH]).then_inc(s_copy, 1)
                    for f in range(12):
                        n = 12 * nb + f
                        slot = 3 * (f // 3 % 2) + f % 3
                        pool.wait_ge(s_ph, n + 1)
                        pool.tensor_tensor(pl[:, slot, :], ex[:, n % 2, :], ph[:, slot, :],
                                           ALU.subtract).then_inc(s_pl, 1)
                for t in range(T1):
                    split_h(T0 * G + g * T1 + t, P)

        @block.vector
        def _(v):
            def sub(dst, src, hi):
                return v.tensor_tensor(dst, src, hi.bitcast(F32), ALU.subtract)

            def ln_centre(n):
                v.wait_ge(s_x, 16 * (n + 1))
                v.wait_ge(s_mean, n + 1)
                mean = pm[:, :].unsqueeze(1).to_broadcast([P, KD, NT])
                v.tensor_tensor(xc[:, :, :], xg(n), mean, ALU.subtract).then_inc(s_xc, 1)

            def ln_scale(n):
                v.wait_ge(s_std, n + 1)
                v.reciprocal(rstd[:, :], std[:, :]).then_inc(s_rstd, 1)
                v.wait_ge(s_rstd, n + 1)
                v.tensor_tensor(xc[:, :, :], xc[:, :, :], rstd[:, :].unsqueeze(1).to_broadcast([P, KD, NT]),
                                ALU.mult).then_inc(s_xn, 1)

            def ln_lo(n):
                v.wait_ge(s_xh, n + 1)
                sub(xl[:, :, :], xc[:, :, :], xh[:, :, :]).then_inc(s_xl, 1)

            def weights(*which):
                for n in which:
                    v.wait_ge(s_whi, n + 1)
                    sub(pieces[n][2], staged(n), pieces[n][1]).then_inc(s_wlo[0], 1)

            u32 = mybir.dt.uint32

            def dequant(k):
                if 1 <= k < 2 * NQ + 1:
                    v.wait_ge(s_val, k)
                    val = gval[:, (k - 1) % 2, :]
                    v.scalar_tensor_tensor(out=val, in0=fbits[:, :].bitcast(F32), scalar=4.0, in1=val, op0=ALU.mult,
                                           op1=ALU.min).then_inc(s_sgn, 1)
                    v.wait_ge(s_sgn, 2 * k - 1)
                    v.tensor_tensor(val.bitcast(u32), val.bitcast(u32), sbits[:, :].bitcast(u32),
                                    ALU.bitwise_or).then_inc(s_sgn, 1)
                if 0 <= k < 2 * NQ:
                    j = k % 2
                    v.wait_ge(s_words[k // 2 % 2], 16 * (k // 4 + 1))
                    if k:
                        v.wait_ge(s_sgn, 2 * k)
                    w32, f32 = words[:, k // 2 % 2, :].bitcast(u32), fbits[:, :].bitcast(u32)
                    v.tensor_scalar(f32, w32, 22 - 4 * j, 7 << 22, ALU.logical_shift_left,
                                    ALU.bitwise_and).then_inc(s_bits, 1)
                    v.tensor_scalar(sbits[:, :].bitcast(u32), w32, 28 - 4 * j, 1 << 31, ALU.logical_shift_left,
                                    ALU.bitwise_and).then_inc(s_bits, 1)
                    v.wait_ge(s_bits, 3 * k + 2)
                    v.tensor_scalar(f32, f32, 124 << 23, None, ALU.bitwise_or).then_inc(s_bits, 1)

            def gated(n, t, rows):
                v.wait_ge(s_act, n + 1)
                if n >= 2:
                    v.wait_ge(s_hl, n - 1)
                v.tensor_tensor(hf[0:rows, n % 2, :], act[0:rows, n % 2, :], ring[2 * (t % 2) + 1][0:rows, :],
                                ALU.mult).then_inc(s_h, 1)

            v.wait_ge(s_const, 64)
            ln_centre(0)
            weights(0)
            v.memset(epsb[:, :], EPS).then_inc(s_prep, 1)
            v.memset(unit[:, :], 1.0).then_inc(s_prep, 1)
            v.memset(wT[:, :].bitcast(F32), 0.0).then_inc(s_prep, 1)
            v.wait_ge(s_gwh, 1)
            sub(gw[:, 1, :, :], gwf[:, :, :], gw[:, 0, :, :]).then_inc(s_prep, 1)
            v.wait_ge(s_prep, SETUP0)
            ln_scale(0)
            ln_lo(0)
            for g in range(G):
                if g == 0:
                    weights(2)
                for m in range(KD):
                    n = 2 * g + m
                    v.wait_ge(s_k, n + 1)
                    v.wait_ge(s_vs, n + 1)
                    v.tensor_tensor(kv0[:, m, :], ring[(1, 0)[m]][:, :], vs[:, m, :], ALU.mult).then_inc(s_kv, 1)
                    v.wait_ge(s_kv, n + 1)
                    for b in range(NT // SEQ):
                        cols = slice(b * SEQ, (b + 1) * SEQ)
                        v.tensor_tensor_scan(kvt[:, m, cols], unit[:, :].to_broadcast([P, SEQ]), kv0[:, m, cols], 0.0, ALU.mult,
                                             ALU.add).then_inc(s_scan, 1)
                    v.wait_ge(s_scan, 2 * n + 2)
                    v.wait_ge(s_q, n + 1)
                    if m == 0 and g >= 1:
                        v.wait_ge(s_hl, T0 * g)
                    v.tensor_tensor(vfl[:, m, :], ring[(2, 1)[m]][:, :], kvt[:, m, :], ALU.mult).then_inc(s_vh, 1)
                for m in range(KD):
                    v.wait_ge(s_vh, 2 * g + m + 1)
                    v.wait_ge(s_vhh, 2 * g + m + 1)
                    sub(vhl[:, m, :], vfl[:, m, :], vhh[:, m, :]).then_inc(s_vhl, 1)
                if g == 0:
                    weights(4)
                r = 11 * g
                v.wait_ge(s_st, g + 1)
                v.tensor_copy(sc[:, :, :].rearrange("p t e -> p (t e)"), pv[:, 0:4 * N_EXP]).then_inc(s_rk, 1)
                v.wait_ge(s_rk, r + 1)
                other = sc[:, :, :].unsqueeze(2).to_broadcast([P, 4, N_EXP, N_EXP])
                own = sc[:, :, :].unsqueeze(3).to_broadcast([P, 4, N_EXP, N_EXP])
                v.tensor_tensor(gt[:, :, :, :], other, own, ALU.is_gt).then_inc(s_rk, 1)
                v.tensor_tensor(ge[:, :, :, :], other, own, ALU.is_ge).then_inc(s_rk, 1)
                v.wait_ge(s_rk, r + 3)
                v.tensor_tensor(ge[:, :, :, :], ge[:, :, :, :],
                                tie[:, :, :].unsqueeze(1).to_broadcast([P, 4, N_EXP, N_EXP]),
                                ALU.mult).then_inc(s_rk, 1)
                v.wait_ge(s_rk, r + 4)
                v.tensor_tensor(gt[:, :, :, :], gt[:, :, :, :], ge[:, :, :, :], ALU.max).then_inc(s_rk, 1)
                v.wait_ge(s_rk, r + 5)
                v.tensor_reduce(rank[:, :, :], gt[:, :, :, :], AX.X, ALU.add).then_inc(s_rk, 1)
                v.wait_ge(s_rk, r + 6)
                v.scalar_tensor_tensor(out=rw[:, :, :], in0=rank[:, :, :], scalar=1.5, in1=sc[:, :, :],
                                       op0=ALU.is_lt, op1=ALU.mult).then_inc(s_rk, 1)
                v.wait_ge(s_rk, r + 7)
                v.tensor_reduce(rsum[:, :], rw[:, :, :], AX.X, ALU.add).then_inc(s_rk, 1)
                v.wait_ge(s_rk, r + 8)
                v.tensor_scalar(rsum[:, :], rsum[:, :], 1e-20, None, ALU.add).then_inc(s_rk, 1)
                v.wait_ge(s_rk, r + 9)
                v.reciprocal(rrec[:, :], rsum[:, :]).then_inc(s_rk, 1)
                v.wait_ge(s_rk, r + 10)
                v.scalar_tensor_tensor(out=rwn[:, :, :], in0=rw[:, :, :], scalar=ROUTE_SCALE,
                                       in1=rrec[:, :].unsqueeze(2).to_broadcast([P, 4, N_EXP]),
                                       op0=ALU.mult, op1=ALU.mult).then_inc(s_rk, 1)
                if g == 0:
                    weights(6)
                v.wait_ge(s_wth, g + 1)
                sub(wT[32:32 + N_EXP, :], pm[0:N_EXP, :], wT[0:N_EXP, :]).then_inc(s_wtl, 1)
                for t in range(T0):
                    n = g * T0 + t
                    gated(n, t, ST_M[t] if t < ST else P)
                    if g == 0 and t in (0, 2):
                        weights(8 if t == 0 else SEL_PIECE + 2)
                    if t >= ST:
                        e = g * XT + t - ST
                        v.wait_ge(s_h, n + 1)
                        v.wait_ge(s_wbc, e + 1)
                        v.tensor_tensor(hf[:, n % 2, :], hf[:, n % 2, :], pv[:, :], ALU.mult).then_inc(s_hw, 1)
                    dequant(step_at(n))
                    if t == LN_AT + 1:
                        ln_centre(g + 1)
                    if t == LN_AT + 5:
                        ln_scale(g + 1)
                ln_lo(g + 1)
                v.wait_ge(s_dn, T0 * (g + 1))
                v.tensor_tensor(xg(g), xg(g), acc[:, :, :], ALU.add).then_inc(s_res, 1)

            v.wait_ge(s_res, G)
            for i in range(2):
                v.wait_ge(s_w4out[i], 32 * NQ)
            v.memset(v3[:, :, :, :, DH:], 0.0).then_inc(s_prep, 1)
            v.wait_ge(s_prep, SETUP0 + 1)
            v.memset(v3[:, :, :, 0, DH:], 1.0).then_inc(s_prep, 1)
            v.memset(mT[:, :], 0.0).then_inc(s_prep, 1)
            v.wait_ge(s_prep, SETUP0 + SETUP1)
            v.wait_ge(s_const, 16 * 14)

            for g in range(G):
                for hb in range(2):
                    nb = 2 * g + hb
                    for t in range(2):
                        v.wait_ge(s_cps, 2 * nb + t + 1)
                        v.tensor_tensor(c[:, t, :], ring[t][:, 0:C_W], bc[:, :], ALU.add).then_inc(s_c, 1)
                    v.wait_ge(s_c, 2 * nb + 2)
                    seg = (slice(0, D_Q), slice(D_Q, D_Q + D_KV))
                    for t in range(2):
                        for w in range(2):
                            v.bn_stats(bst[:, 2 * t + w, :], c[:, t, seg[w]]).then_inc(s_bn, 1)
                    v.wait_ge(s_bn, 8 * nb + 4)
                    for i in range(4):
                        v.bn_aggr(mv[:, i, :], bst[:, i, :]).then_inc(s_bn, 1)
                    v.wait_ge(s_cstd, nb + 1)
                    v.wait_ge(s_bn, 8 * nb + 8)
                    v.reciprocal(crs[:, :], cstd[:, :]).then_inc(s_crs, 1)
                    v.wait_ge(s_crs, nb + 1)
                    for t in range(2):
                        for w in range(2):
                            i = 2 * t + w
                            v.tensor_scalar(cn[:, t, seg[w]], c[:, t, seg[w]], mv[:, i, 0:1], crs[:, i:i + 1],
                                            ALU.subtract, ALU.mult).then_inc(s_cn, 1)
                    v.wait_ge(s_ctr, nb + 1)
                    for w, rows in ((0, D_Q), (1, P)):
                        v.tensor_scalar(ctf[0:rows, w, :], pm[0:rows, w * SEQ:(w + 1) * SEQ], gb[0:rows, 2 * w:2 * w + 1],
                                        gb[0:rows, 2 * w + 1:2 * w + 2], ALU.mult, ALU.add).then_inc(s_ct, 1)
                    for w, rows in ((0, D_Q), (1, P)):
                        v.wait_ge(s_cth, 2 * nb + w + 1)
                        sub(ctl[0:rows, w, :], ctf[0:rows, w, :], cth[0:rows, w, :]).then_inc(s_ctl, 1)
                    for t in range(2):
                        v.wait_ge(s_qkv, 2 * nb + t + 1)
                        heads = lambda ap: ap.rearrange("p (h d) -> p h d", h=H)
                        kvp, kvb = heads(ring[2 + t][:, 0:D + H * DN]), heads(bkv[:, :])
                        v.tensor_tensor(qf[:, t, :, :], heads(ring[t][:, 0:D]), heads(bq[:, :]),
                                        ALU.add).then_inc(s_qkvb, 1)
                        v.tensor_tensor(kf[:, t, :, 0:DN], kvp[:, :, 0:DN], kvb[:, :, 0:DN], ALU.add).then_inc(s_qkvb, 1)
                        v.tensor_tensor(vf[:, t, :, :], kvp[:, :, DN:], kvb[:, :, DN:], ALU.add).then_inc(s_qkvb, 1)
                    v.wait_ge(s_qkvb, 6 * (nb + 1))
                    x1, x2 = qf[:, :, :, DN:DN + 4], qf[:, :, :, DN + 4:]
                    cos, sin = (rot[:, i, :, :].unsqueeze(1).to_broadcast([P, 2, H, 4]) for i in range(2))
                    for i, (xx, tt) in enumerate(((x1, cos), (x2, sin), (x1, sin), (x2, cos))):
                        v.tensor_tensor(rt[:, i, :, :, :], xx, tt, ALU.mult).then_inc(s_rope, 1)
                    v.wait_ge(s_rope, 7 * nb + 4)
                    v.tensor_tensor(x1, rt[:, 0, :, :, :], rt[:, 1, :, :, :], ALU.add).then_inc(s_rope, 1)
                    v.tensor_tensor(x2, rt[:, 3, :, :, :], rt[:, 2, :, :, :], ALU.subtract).then_inc(s_rope, 1)
                    for t in range(2):
                        kr = v.tensor_copy(kf[:, t, :, DN:],
                                           c[:, t, D_Q + D_KV:].unsqueeze(1).to_broadcast([P, H, DR]))
                    kr.then_inc(s_rope, 1)
                    v.wait_ge(s_rope, 7 * nb + 7)
                    slot = lambda t, i: t[:, :, :, i * DH:(i + 1) * DH]
                    q_f = qf
                    parts = ((q_f, slot(qs, 0), slot(qs, 2), slot(qs, 5)), (kf[:, :, :, :], slot(ks, 0), slot(ks, 1), slot(ks, 4)),
                             (vf[:, :, :, :], v3[:, :, :, 0, 0:DH], v3[:, :, :, 1, 0:DH], v3[:, :, :, 2, 0:DH]))
                    s = 12 * nb
                    for full, p0, p1, p2 in parts:
                        v.tensor_copy(p0, full).then_inc(s_split, 1)
                    v.wait_ge(s_split, s + 3)
                    for full, p0, p1, p2 in parts:
                        v.tensor_tensor(full, full, p0, ALU.subtract).then_inc(s_split, 1)
                    v.wait_ge(s_split, s + 6)
                    for full, p0, p1, p2 in parts:
                        v.tensor_copy(p1, full).then_inc(s_split, 1)
                    v.wait_ge(s_split, s + 9)
                    for full, p0, p1, p2 in parts:
                        v.tensor_tensor(p2, full, p1, ALU.subtract).then_inc(s_split, 1)
                    for f in range(1, 8, 2):
                        v.wait_ge(s_tr, 8 * nb + f + 1)
                        v.tensor_copy(qbuf[f // 4][2][0:SLOT, 4 * (f % 4):4 * (f % 4) + 4, :].rearrange("p h t -> p (h t)"),
                                      ring[f % 4][0:SLOT, :].bitcast(BF16)).then_inc(s_evD, 1)
                    for f in range(12):
                        v.wait_ge(s_s, 12 * nb + f + 1)
                        i = 0 if f < 4 else 1
                        nh = 4 if i == 0 else 2
                        h0 = 4 * f if i == 0 else 2 * (f - 4)
                        v.tensor_reduce(mx[:, i, h0:h0 + nh], ring[f % 4][:, :].rearrange("p (n k) -> p n k", n=nh),
                                        AX.X, ALU.max).then_inc(s_mx, 1)
                    v.wait_ge(s_mx, 12 * (nb + 1))
                    v.tensor_scalar(nm[:, :, 0, :], mx[:, :, :], -1.0, None, ALU.mult).then_inc(s_nm, 1)
                    v.wait_ge(s_nm, 2 * nb + 1)
                    v.scalar_tensor_tensor(out=nm[:, :, 1, :], in0=mx[:, :, :], scalar=-1.0, in1=nm[:, :, 0, :],
                                           op0=ALU.mult, op1=ALU.subtract).then_inc(s_nm, 1)

                    def probs(hg, nb=nb):
                        for part in range(3):
                            n = 12 * nb + 3 * hg + part
                            v.wait_ge(s_e, n + 1)
                            if hg >= 2:
                                v.wait_ge(s_y, 4 * nb + hg - 1)
                            v.tensor_copy(ph[:, 3 * (hg % 2) + part, :], ex[:, n % 2, :]).then_inc(s_ph, 1)

                    def normalize(hg, nb=nb):
                        n = 4 * nb + hg
                        v.wait_ge(s_y, n + 1)
                        if n >= 1:
                            v.wait_ge(s_yn, n)
                        bank = (pm, pv)[hg % 2][:, 0:8 * 51].rearrange("p (x s d) -> p x d s", x=8, s=3)
                        v.tensor_reduce(ys[:, :, :], bank, AX.X, ALU.add).then_inc(s_yst, 1)
                        v.wait_ge(s_yst, 2 * n + 1)
                        v.reciprocal(yr[:, :], ys[:, :, DH]).then_inc(s_yst, 1)
                        v.wait_ge(s_yst, 2 * n + 2)
                        for i in range(2):
                            last = v.tensor_tensor(y[:, i, 4 * hg:4 * hg + 4, :], ys[:, 4 * i:4 * i + 4, 0:DH],
                                                   yr[:, 4 * i:4 * i + 4].unsqueeze(2).to_broadcast([P, 4, DH]),
                                                   ALU.mult)
                        last.then_inc(s_yn, 1)

                    probs(0)
                    for hg in range(4):
                        if hg < 3:
                            probs(hg + 1)
                        normalize(hg)
                    v.wait_ge(s_yh, nb + 1)
                    if nb >= 1:
                        v.wait_ge(s_ao, nb)
                    sub(yl[:, :, :], pm[:, :].rearrange("p (k t) -> p k t", k=KD), yh[:, :, :]).then_inc(s_yl, 1)
                v.wait_ge(s_pl, 24 * (g + 1))
                for t in range(T1):
                    gated(T0 * G + g * T1 + t, t, P)
                    if g < G - 1 and t == LN_AT + 1:
                        ln_centre(G + g + 1)
                    if g < G - 1 and t == LN_AT + 5:
                        ln_scale(G + g + 1)
                if g < G - 1:
                    ln_lo(G + g + 1)
                v.wait_ge(s_dn, T0 * G + T1 * (g + 1))
                for j in range(KD):
                    last = v.scalar_tensor_tensor(out=xg(g)[:, j, :], in0=acc[:, j, :], scalar=bout[:, j:j + 1],
                                                  in1=xg(g)[:, j, :], op0=ALU.add, op1=ALU.add)
                last.then_inc(s_res, 1)


def _layouts(i):
    import numpy as np

    a = {k: np.asarray(v) for k, v in i.items()}
    f = np.float32
    perm = np.concatenate([np.arange(0, D, 2), np.arange(1, D, 2)])

    def rows2(w):
        return w.reshape(P, KD, -1)

    def tiles(w, n):
        full = np.zeros((n * P, w.shape[1]), f)
        full[:w.shape[0]] = w
        return full.reshape(n, P, -1).transpose(1, 0, 2)

    flat = lambda parts: np.ascontiguousarray(np.concatenate([p.reshape(P, -1) for p in parts], 1))
    ew = lambda w: w.reshape(N_EXP * E_FF, D).T
    w0 = flat([rows2(a["L0_attn_Wq"].T), rows2(a["L0_attn_Wk"].T), rows2(a["L0_attn_Wv"].T),
               tiles(a["L0_attn_Wo"].T[:, perm], KD),
               rows2(a["L0_ffn_shared_wg"].T), rows2(a["L0_ffn_shared_wu"].T),
               tiles(a["L0_ffn_shared_wd"].T[:, perm], ST),
               rows2(ew(a["L0_ffn_exp_wg"])), rows2(ew(a["L0_ffn_exp_wu"])),
               tiles(a["L0_ffn_exp_wd"].transpose(0, 2, 1).reshape(N_EXP * E_FF, D)[:, perm], XT)])
    dn = np.zeros((D, 256), f)
    dn[:, :D_Q] = a["L1_attn_W_d_q"].T
    dn[:, D_Q:C_W] = a["L1_attn_W_d_kv"].T
    wa = flat([rows2(dn), tiles(a["L1_attn_W_u_q"].T, 1), tiles(a["L1_attn_W_u_kv"].T, 1),
               tiles(a["L1_attn_W_o"].T[:, perm], KD)])
    lng = np.zeros((P, 4), f)
    lng[:D_Q, 0], lng[:D_Q, 1] = a["L1_attn_q_norm_g"], a["L1_attn_q_norm_b"]
    lng[:, 2], lng[:, 3] = a["L1_attn_kv_norm_g"], a["L1_attn_kv_norm_b"]
    order = np.array([2 * ((t // 2) * P + p) + t % 2 for t in range(T1) for p in range(P)])
    up = lambda w: w[order].T.reshape(P, 4, QW)
    down = a["L1_ffn_down_W_packed"].T[:, perm].reshape(8, P, D).transpose(1, 0, 2).reshape(P, 4, QW)
    q4 = np.concatenate([up(a["L1_ffn_gate_W_packed"]), up(a["L1_ffn_up_W_packed"]), down], 1)
    ups = lambda w: np.repeat(w[order].T, 16, 0).reshape(P, 4, QW)
    downs = np.repeat(a["L1_ffn_down_scales"].T[:, perm], 16, 0).reshape(8, P, D).transpose(1, 0, 2).reshape(P, 4, QW)
    s4 = np.concatenate([ups(a["L1_ffn_gate_scales"]), ups(a["L1_ffn_up_scales"]), downs], 1)

    bf16 = lambda c: (c.view(np.uint32) >> 16).astype(np.uint16)
    sel = np.zeros((P, N_EXP * E_FF), f)
    for e in range(N_EXP):
        sel[[e, 32 + e], e * E_FF:(e + 1) * E_FF] = 1
    selm = np.zeros((P, H, P), f)
    for h in range(H):
        selm[[h, H + h], h, :] = 1
    masks = np.zeros((2, P, P), f)
    masks[0][np.triu_indices(P, 1)] = MASKED
    masks[1][np.tril_indices(P, -1)] = MASKED
    inv = ((1.0 / 10000.0) ** (np.arange(0, DR, 2, dtype=f) / DR)).astype(f)
    angle = np.arange(H, dtype=f)[:, None] * inv[None, :]
    rot = np.broadcast_to(np.stack([np.cos(angle), np.sin(angle)]).astype(f), (P, 2, H, 4))
    tie = np.broadcast_to((np.arange(N_EXP)[None, :] < np.arange(N_EXP)[:, None]).astype(f), (P, N_EXP, N_EXP))
    return {
        "xT": a["L0_attn_x"].reshape(TOKENS, P, KD).transpose(1, 2, 0), "w0": w0, "gateT": rows2(a["L0_ffn_gate_w"].T),
        "wa": wa, "biasc": np.concatenate([a["L1_attn_b_d_q"], a["L1_attn_b_d_kv"]]), "biasq": a["L1_attn_b_u_q"],
        "biaskv": a["L1_attn_b_u_kv"], "lng": lng, "bo": a["L1_attn_b_o"].reshape(P, KD),
        "ones_c": np.full((P, P), 1.0 / D, f), "sel_c": sel, "selm_c": bf16(selm), "ident_c": np.eye(P, dtype=f),
        "identb_c": bf16(np.eye(P, dtype=f)), "mask_c": bf16(masks), "rot_c": rot, "tie_c": tie, "q4": q4, "s4": s4,
    }


def kernel(**inputs):
    import numpy as np
    import concourse.bacc as bacc
    from concourse.bass_utils import run_bass_kernel_spmd

    nc = bacc.Bacc("TRN2", target_bir_lowering=False, num_devices=1)
    arrays, args = {}, {}
    for name, a in _layouts(inputs).items():
        a = np.ascontiguousarray(a)
        arrays[name] = a
        args[name] = nc.dram_tensor(name, a.shape, mybir.dt.from_np(a.dtype), kind="ExternalInput").ap()
    args["out"] = nc.dram_tensor("out", (P, KD, TOKENS), F32, kind="ExternalOutput").ap()
    args["x1s"] = nc.dram_tensor("x1s", (P, KD, TOKENS), F32, kind="Internal").ap()
    args["w4s"] = nc.dram_tensor("w4s", (2, P, 3 * KD * MLP), F32, kind="Internal").ap()
    transformer_blocks(nc, **args)
    r = run_bass_kernel_spmd(nc, [arrays], core_ids=[0])
    o = r.results[0]["out"]
    return np.ascontiguousarray(o.transpose(2, 0, 1)).reshape(BATCHES, SEQ, D)
```

```python
from contextlib import ExitStack

import concourse.bass as bass
from concourse import mybir

F32 = mybir.dt.float32
F32R = mybir.dt.float32r
BF16 = mybir.dt.bfloat16
F16 = mybir.dt.float16
I32 = mybir.dt.int32
U16 = mybir.dt.uint16
ALU = mybir.AluOpType
ACT = mybir.ActivationFunctionType
AX = mybir.AxisListType

P = 128
D = 256
KD = D // P
BATCHES, SEQ = 8, 256
TOKENS = BATCHES * SEQ
NT = 512
G = TOKENS // NT
EPS = 1e-5

E_FF, N_EXP, SH_FF = 176, 8, 352
XT = N_EXP * E_FF // P
ST = 3
ST_M = [128, 128, SH_FF - 256]
T0 = ST + XT
LN_AT = 4
ROUTE_SCALE = 2.5
DENOM = float(D) ** 0.5 / SEQ

MLP = 2048
T1 = MLP // P
H, DH, DN, DR = 16, 16, 8, 8
D_Q, D_KV = D // 3, D // 2
C_W = D_Q + D_KV + DR
SCALE = float(DH) ** -0.5
SLOT = 6 * DH
MASKED = -1e30

O_QKVO = 0
O_SG = 4 * KD * D
O_SU = O_SG + KD * SH_FF
O_SD = O_SU + KD * SH_FF
O_EG = O_SD + ST * D
O_EU = O_EG + KD * XT * P
O_ED = O_EU + KD * XT * P
W0_COLS = O_ED + XT * D
PIECES0 = [(o + i * w // 2, o + (i + 1) * w // 2) for o, w in (
    (0, O_SG), (O_SG, O_EG - O_SG), (O_EG, O_EU - O_EG), (O_EU, O_ED - O_EU), (O_ED, W0_COLS - O_ED)) for i in range(2)]
O_G4 = 0
O_U4 = KD * MLP
O_D4 = 2 * KD * MLP
A_DN = 0
A_UQ = A_DN + KD * 256
A_UKV = A_UQ + D
A_O = A_UKV + D + H * DN
WA_COLS = A_O + KD * D
NS = 4
STAGE = max(b - a for a, b in PIECES0)
SEL_PIECE = len(PIECES0)
QW = 512
NQ = 3 * MLP // QW
Q0 = T0
MID = [0, 6, 6, 6]
REST = [m + 4 for m in MID]
LN_AT1 = 11
COPY_AT = 9
NP = 5
HB = 3


def transformer_blocks(nc, xT, w0, gateT, wa, biasc, biasq, biaskv, lng, bo, ones_c, sel_c, ident_c, identb_c,
                       mask_c, rot_c, tie_c, q4, s4, x1s, w4s, out):
    ctx = ExitStack()
    with ctx:
        def sb(name, shape, dt, where=ctx):
            return where.enter_context(nc.sbuf_tensor(name, shape, dt))

        def sem(name):
            return ctx.enter_context(nc.semaphore(name))

        wh = sb("wh", [P, W0_COLS], F32R)
        wl = sb("wl", [P, W0_COLS], F32R)
        ah = sb("ah", [P, WA_COLS], F32R)
        al = sb("al", [P, WA_COLS], F32R)
        x = sb("x", [P, 2, KD, NT], F32)
        ones = sb("ones", [P, P], F32)
        epsb = sb("epsb", [P, 1], F32)
        identf = sb("identf", [P, P], F32)
        cy = ExitStack()
        yh = sb("yh", [P, KD, SEQ], F32R, cy)
        cy.close()
        xc = sb("xc", [P, KD, NT], F32)
        cy = ExitStack()
        yl = sb("yl", [P, KD, SEQ], F32R, cy)
        cy.close()
        sq = sb("sq", [P, KD, NT], F32)
        std = sb("std", [P, NT], F32)
        rstd = std
        xh = sb("xh", [P, KD, NT], F32R)
        xl = sb("xl", [P, KD, NT], F32R)
        act = sb("act", [P, 2, NT], F32)
        hf = sb("hf", [P, 2, NT], F32)
        hh = sb("hh", [P, HB, NT], F32R)
        hl = sb("hl", [P, HB, NT], F32R)

        c0 = ExitStack()
        cs = ExitStack()
        stage = sb("stage", [P, NS, STAGE], F32, cs)
        cs.close()
        words = sb("words", [P, 2, QW], I32, c0)
        fbits = sb("fbits", [P, QW], I32, c0)
        sbits = sb("sbits", [P, QW], I32, c0)
        gval = sb("gval", [P, 2, QW], F32, c0)
        scl = sb("scl", [P, QW], F32, c0)
        wf = sb("wf", [P, QW], F32, c0)
        w4h = sb("w4h", [P, 2, QW], F32R, c0)
        w4l = sb("w4l", [P, 2, QW], F32R, c0)
        sel = sb("sel", [P, XT * P], F32R, c0)
        gw = sb("gw", [P, 2, KD, N_EXP], F32R, c0)
        gwf = sb("gwf", [P, KD, N_EXP], F32, c0)
        vs = sb("vs", [P, 2, NT], F32, c0)
        vhh = sb("vhh", [P, KD, NT], F32R, c0)
        vhl = sb("vhl", [P, KD, NT], F32R, c0)
        sig = sb("sig", [N_EXP, NT], F32, c0)
        sc = sb("sc", [P, 4, N_EXP], F32, c0)
        gt = sb("gt", [P, 4, N_EXP, N_EXP], F32, c0)
        ge = sb("ge", [P, 4, N_EXP, N_EXP], F32, c0)
        unit = sb("unit", [P, 1], F32, c0)
        tie = sb("tie", [P, N_EXP, N_EXP], F32, c0)
        rank = sb("rank", [P, 4, N_EXP], F32, c0)
        rw = sb("rw", [P, 4, N_EXP], F32, c0)
        rsum = sb("rsum", [P, 4], F32, c0)
        rrec = sb("rrec", [P, 4], F32, c0)
        rwn = sb("rwn", [P, 4, N_EXP], F32, c0)
        wT = sb("wT", [P, NT], F32R, c0)
        kv0 = sq
        kvt = vs
        vfl = hf
        c0.close()

        c1 = ctx
        bc = sb("bc", [P, C_W], F32, c1)
        bq = sb("bq", [P, D], F32, c1)
        bkv = sb("bkv", [P, D + H * DN], F32, c1)
        gb = sb("gb", [P, 4], F32, c1)
        bout = sb("bout", [P, KD], F32, c1)
        rot = sb("rot", [P, 2, H, 4], F32, c1)
        ident = sb("ident", [P, P], BF16, c1)
        maskq = sb("maskq", [P, P], BF16, c1)
        maskk = sb("maskk", [P, P], BF16, c1)
        ys = sb("ys", [P, 8, DH + 1], F32, c1)
        yr = sb("yr", [P, 8], F32, c1)
        bst = sb("bst", [P, 4, 6], F32, c1)
        mv = sb("mv", [P, 4, 2], F32, c1)
        cstd = sb("cstd", [P, 4], F32, c1)
        crs = sb("crs", [P, 4], F32, c1)
        v3 = sb("v3", [P, 2, H, 3, DH + 1], BF16, c1)
        qT = sb("qT", [P, H, SEQ], BF16, c1)
        kT = sb("kT", [P, H, SEQ], BF16, c1)
        mx = sb("mx", [P, 2, H], F32, c1)
        nm = sb("nm", [P, 2, 2, H], BF16, c1)
        mT = sb("mT", [P, SEQ], BF16, c1)
        c2 = ExitStack()
        cth = sb("cth", [P, 2, SEQ], F32R, c2)
        ctl = sb("ctl", [P, 2, SEQ], F32R, c2)
        rt = sb("rt", [P, 4, 2, H, 4], F32, c2)
        c2.close()
        qs = sb("qs", [P, 2, H, SLOT], BF16, c1)
        ks = sb("ks", [P, 2, H, SLOT], BF16, c1)
        ph = sb("ph", [P, NP, NT], F16)
        pl = sb("pl", [P, NP, NT], F16)
        flat = lambda t: t[:, :, :].rearrange("p a b -> p (a b)")
        kf = xc[:, 0, :].rearrange("p (t h d) -> p t h d", t=2, h=H)
        vf = xc[:, 1, :].rearrange("p (t h d) -> p t h d", t=2, h=H)
        qf = flat(sq)[:, 0:2 * H * DH].rearrange("p (t h d) -> p t h d", t=2, h=H)
        c = flat(sq)[:, KD * NT - 2 * C_W:].rearrange("p (t n) -> p t n", t=2)
        cn = c
        ctf = std[:, :].rearrange("p (w t) -> p w t", w=2)
        y = std[:, :].rearrange("p (i h d) -> p i h d", i=2, h=H)
        qbuf = [[qs, qf, qT], [ks, kf, kT]]

        acc = ctx.enter_context(nc.psum_tensor("acc", [P, KD, NT], F32))
        ring = [ctx.enter_context(nc.psum_tensor(f"ring{i}", [P, NT], F32)) for i in range(4)]
        pm = ctx.enter_context(nc.psum_tensor("pm", [P, NT], F32))
        pv = ctx.enter_context(nc.psum_tensor("pv", [P, NT], F32))

        s_x = sem("x_in")
        s_const = sem("constants_in")
        s_bc = sem("latent_biases_in")
        s_stage = [sem(f"weights_in{i}") for i in range(NS)]
        s_whi = sem("weights_hi")
        s_wlo = [sem(f"weights_split{i}") for i in range(2)]
        s_gwh = sem("gate_hi")
        s_prep = sem("small_set_up")
        s_mean, s_xc, s_sq, s_var, s_std = map(sem, ("mean", "centred", "squares", "variance", "deviation"))
        s_rstd, s_xn, s_xh, s_xl = map(sem, ("inverse_deviation", "normed", "normed_hi", "normed_split"))
        s_xdone = sem("normed_used")
        s_v, s_k, s_q = map(sem, ("v_product", "k_product", "q_product"))
        s_vs, s_kv, s_scan, s_vh, s_vhh, s_vhl = map(
            sem, ("v_scaled", "kv", "kv_summed", "vhat", "vhat_hi", "vhat_split"))
        s_oproj = sem("vhat_used")
        s_lg, s_sig, s_st, s_rk, s_wt, s_wth, s_wtl = map(
            sem, ("logits", "scores", "scores_turned", "route_steps", "weights_turned", "weights_hi_in",
                  "weights_lo_in"))
        s_gu, s_act, s_wbc, s_h, s_hw, s_hh, s_hl, s_dn = map(
            sem, ("gate_up", "activated", "route_spread", "gated", "routed", "h_hi", "h_split", "h_used"))
        s_res = sem("residual")
        s_out = sem("stored")
        s_words = [sem(f'words_in{i}') for i in range(2)]
        s_scl, s_bits, s_val, s_sgn, s_w, s_w4h, s_w4l = map(
            sem, ("scales_in", "bit_steps", "values", "signs", "w4", "w4_hi", "w4_split"))
        s_w4out, s_w4in = [sem(f"w4_stored{i}") for i in range(2)], sem("w4_in")
        s_cps, s_c, s_bn, s_cstd, s_crs, s_cn, s_ctr, s_ct, s_cth, s_ctl = map(
            sem, ("latents", "latents_biased", "latent_stats", "latent_deviation", "latent_inverse",
                  "latents_normed", "latents_turned", "latents_affine", "latents_hi", "latents_split"))
        s_qkv, s_qkvb, s_rope, s_split, s_copy = map(
            sem, ("qkv", "qkv_biased", "rotary_steps", "split_steps", "slots_copied"))
        s_tr, s_evA, s_evD = map(sem, ("slots_turned", "turned_by_act", "turned_by_dve"))
        s_s, s_mx, s_nm, s_mtr, s_mT = map(sem, ("score_bank", "score_max", "max_split", "max_turned", "max_in"))
        s_phs = [sem(f"probs_hi{i}") for i in range(2)]
        s_pls = [sem(f"probs_split{i}") for i in range(2)]
        s_md, s_vsp = sem("max_placed"), sem("values_split")
        s_sT, s_e, s_y, s_yst, s_yn = map(
            sem, ("score_bank_turned", "exponentials", "y_bank", "y_steps", "y_normed"))
        s_ytr, s_yh, s_yl, s_ao = map(sem, ("y_turned", "y_hi", "y_split", "y_used"))

        SETUP0, SETUP1 = 4, 3

        def xg(n):
            return x[:, n % 2, :, :]

        def exps(n):
            return x[:, (n // 24 + 1) % 2, n % 2, :]

        def bank_of(g, t, up):
            if MID[g] <= t < REST[g]:
                return (pm, pv)[up]
            return ring[2 * (t % 2) + up]

        def x1_at(g):
            return x1s[:, :, g * NT:(g + 1) * NT]

        pieces = [(w0[:, a:b], wh[:, a:b], wl[:, a:b]) for a, b in PIECES0]
        pieces.append((sel_c, sel[:, :], None))
        pieces += [(wa[:, a:b], ah[:, a:b], al[:, a:b]) for a, b in ((0, WA_COLS // 2), (WA_COLS // 2, WA_COLS))]
        step_at = lambda tile: 2 * ((tile - Q0) // 3) + (tile - Q0) % 3 if (tile - Q0) % 3 < 2 else -1
        step_at = lambda tile: 2 * ((tile - Q0) // 3) + (tile - Q0) % 3 if (tile - Q0) % 3 < 2 else -1
        staged = lambda n: stage[:, n % NS, 0:pieces[n][0].shape[1]]
        lo_of = {0: [n for n in range(0, len(pieces), 2) if n != SEL_PIECE], 1: list(range(1, len(pieces), 2))}

        def w0k(off, width, k, a, b):
            return slice(off + k * width + a, off + k * width + b)

        consts = [(ones, ones_c), (identf, ident_c)]
        def w4_at(dst, n, j):
            if n < 8:
                off = (O_G4, O_U4)[n // 4] + j * MLP + (n % 4) * QW
                return dst[:, off:off + QW]
            v = dst[:, O_D4:O_D4 + T1 * D].rearrange("p (c j d) -> p c j d", c=T1 // 2, j=2)
            return v[:, 2 * (n - 8):2 * (n - 8) + 2, j, :]

        block = ctx.enter_context(nc.Block())

        @block.sync
        def _(sp):
            sp.dma_start(xg(0), xT[:, :, 0:NT]).then_inc(s_x, 16)
            for t, src in consts:
                sp.dma_start(t[:, :], src).then_inc(s_const, 16)
            for n, (src, _, _) in enumerate(pieces):
                if n >= NS:
                    sp.wait_ge(s_wlo[n % 2], lo_of[n % 2].index(n - NS) + 1)
                sp.dma_start(staged(n), src).then_inc(s_stage[n % NS], 16)
                if n == 1:
                    sp.wait_ge(s_x, 16)
                    sp.dma_start(xg(1), xT[:, :, NT:2 * NT]).then_inc(s_x, 16)
            for i in range(2):
                sp.wait_ge(s_wlo[i], len(lo_of[i]))
            for k in range(2 * NQ + 2):
                if k % 2 == 0:
                    for n in (0, 1) if k == 0 else (k // 2 + 1,) if k // 2 + 1 < NQ else ():
                        if n >= 2:
                            sp.wait_ge(s_bits, 6 * (n - 1))
                        sp.dma_start(words[:, n % 2, :], q4[:, n, :]).then_inc(s_words[n % 2], 16)
                if k >= 2:
                    sp.wait_ge(s_w4l, k - 1)
                    for i, part in enumerate((w4h, w4l)):
                        sp.dma_start(w4_at(w4s[i], (k - 2) // 2, k % 2), part[:, k % 2, :].bitcast(F32)).then_inc(
                            s_w4out[k % 2], 16)
                if k % 2 == 0 and k < 2 * NQ:
                    if k:
                        sp.wait_ge(s_w, k)
                    sp.dma_start(scl[:, :], s4[:, k // 2, :]).then_inc(s_scl, 16)
            for i in range(2):
                sp.wait_ge(s_w4out[i], 32 * NQ)

            def w4_load(a, b):
                for i, dst in enumerate((wh, wl)):
                    sp.dma_start(dst[:, a:b].bitcast(F32), w4s[i][:, a:b]).then_inc(s_w4in, 16)

            sp.wait_ge(s_oproj, G)
            w4_load(0, O_SG)
            sp.wait_ge(s_res, G)
            sp.dma_start(bc[:, :], biasc.partition_broadcast(P)).then_inc(s_bc, 16)
            for t, src in ((bq[:, :], biasq.partition_broadcast(P)),
                           (bkv[:, :], biaskv.partition_broadcast(P)), (gb[:, :], lng), (bout[:, :], bo),
                           (rot[:, :, :, :], rot_c), (ident[:, :], identb_c.bitcast(BF16)),
                           (maskq[:, :], mask_c[0].bitcast(BF16)), (maskk[:, :], mask_c[1].bitcast(BF16))):
                sp.dma_start(t, src).then_inc(s_const, 16)
            sp.dma_start(x1_at(G - 1), xg(G - 1)).then_inc(s_out, 16)
            sp.wait_ge(s_dn, T0 * G)
            w4_load(O_SG, 3 * KD * MLP)
            for n in range(G, 2 * G + 1):
                if n > G:
                    sp.wait_ge(s_res, n)
                    sp.dma_start(out[:, :, (n - 1 - G) * NT:(n - G) * NT], xg(n - 1)).then_inc(s_out, 16)
                sp.wait_ge(s_out, 16 * n)
                if n + 1 < 2 * G:
                    for i in range(2):
                        sp.wait_ge(s_pls[i], 12 * (n - G + 1))
                    sp.dma_start(xg(n + 1), x1_at(n + 1 - G)).then_inc(s_x, 16)

        @block.tensor
        def _(pe):
            def prod(o, lo_hi_w, x_hi, x_lo, first, last):
                w_hi, w_lo = lo_hi_w
                pe.matmul(o, w_hi, x_hi, start=first, stop=False, skip_group_check=True)
                pe.matmul(o, w_lo, x_hi, start=False, stop=False, skip_group_check=True)
                return pe.matmul(o, w_hi, x_lo, start=False, stop=last, skip_group_check=True)

            def ln_mean(n):
                pe.wait_ge(s_x, 16 * (n + 1))
                for k in range(KD):
                    mm = pe.matmul(pm[:, :], ones[:, :], xg(n)[:, k, :], start=k == 0, stop=k == KD - 1)
                mm.then_inc(s_mean, 1)

            def ln_var(n):
                pe.wait_ge(s_sq, n + 1)
                for k in range(KD):
                    mm = pe.matmul(pm[:, :], ones[:, :], sq[:, k, :], start=k == 0, stop=k == KD - 1)
                mm.then_inc(s_var, 1)

            def normed(n):
                pe.wait_ge(s_xl, n + 1)
                pe.wait_ge(s_xh, n + 1)

            def w(off, width, k, a, b):
                s = w0k(off, width, k, a, b)
                return wh[:, s], wl[:, s]

            def down(tile_no, off, kt, rows, last, first=False):
                pe.wait_ge(s_hl, tile_no + 1)
                b = tile_no % HB
                for m in range(KD):
                    s = w0k(off, D, kt, m * P, (m + 1) * P)
                    mm = prod(acc[:, m, :], (wh[0:rows, s], wl[0:rows, s]), hh[0:rows, b, :], hl[0:rows, b, :],
                              first, last)
                mm.then_inc(s_dn, 1)

            def down0(g, u):
                down(g * T0 + u, O_SD if u < ST else O_ED, u if u < ST else u - ST, ST_M[u] if u < ST else P,
                     u == T0 - 1)

            pe.wait_ge(s_const, 64)
            for g in range(G):
                if g == 0:
                    ln_mean(0)
                    ln_var(0)
                normed(g)
                if g == 0:
                    pe.wait_ge(s_wlo[0], 1)
                    pe.wait_ge(s_wlo[1], 1)
                    pe.wait_ge(s_prep, SETUP0)
                else:
                    pe.wait_ge(s_h, T0 * g)
                for m in range(KD):
                    for j, (which, bank, s) in enumerate(((2, (0, 3), s_v), (1, (1, 0), s_k), (0, (2, 1), s_q))):
                        if m == 1 and j == 1:
                            pe.wait_ge(s_vs, 2 * g + 1)
                        if m == 1 and j == 2:
                            pe.wait_ge(s_kv, 2 * g + 1)
                        if g and m == 0 and j == 1:
                            down0(g - 1, T0 - 1)
                        for k in range(KD):
                            mm = prod(ring[bank[m]][:, :], w(O_QKVO + which * KD * D, D, k, m * P, (m + 1) * P),
                                      xh[:, k, :], xl[:, k, :], k == 0, k == KD - 1)
                        mm.then_inc(s, 1)
                for k in range(KD):
                    mm = prod(pm[0:N_EXP, :], (gw[:, 0, k, :], gw[:, 1, k, :]), xh[:, k, :], xl[:, k, :],
                              k == 0, k == KD - 1)
                mm.then_inc(s_lg, 1)
                def gate_up(t):
                    n = g * T0 + t
                    if t >= 2:
                        pe.wait_ge(s_h, n - 1)
                    else:
                        pe.wait_ge(s_vh, 2 * g + 2)
                    rows = ST_M[t] if t < ST else P
                    for o, off, eoff in ((2 * (t % 2), O_SG, O_EG), (2 * (t % 2) + 1, O_SU, O_EU)):
                        for k in range(KD):
                            if t < ST:
                                ww = w(off, SH_FF, k, t * P, t * P + rows)
                            else:
                                ww = w(eoff, XT * P, k, (t - ST) * P, (t - ST + 1) * P)
                            mm = prod(ring[o][0:rows, :], ww, xh[:, k, :], xl[:, k, :], k == 0, k == KD - 1)
                    mm.then_inc(s_gu, 1)
                    if t >= ST:
                        e = g * XT + t - ST
                        if t == ST:
                            pe.wait_ge(s_wtl, g + 1)
                            pe.wait_ge(s_rk, 11 * g + 1)
                        if e >= 1:
                            pe.wait_ge(s_hw, e)
                        pe.matmul(pv[:, :], sel[:, (t - ST) * P:(t - ST + 1) * P], wT[:, :], start=True,
                                  stop=True).then_inc(s_wbc, 1)

                if g == 0:
                    pe.wait_ge(s_wlo[0], 2)
                    pe.wait_ge(s_wlo[1], 2)
                gate_up(0)
                pe.wait_ge(s_sig, g + 1)
                for t in range(4):
                    mm = pe.transpose(pv[:, t * N_EXP:(t + 1) * N_EXP], sig[:, t * P:(t + 1) * P],
                                      identf[0:N_EXP, 0:N_EXP])
                mm.then_inc(s_st, 1)
                pe.wait_ge(s_vhl, 2 * g + 2)
                if g >= 1:
                    pe.wait_ge(s_res, g)
                for m in range(KD):
                    for k in range(KD):
                        mm = prod(acc[:, m, :], w(O_QKVO + 3 * KD * D, D, k, m * P, (m + 1) * P),
                                  vhh[:, k, :], vhl[:, k, :], k == 0, False)
                mm.then_inc(s_oproj, 1)
                pe.wait_ge(s_rk, 11 * (g + 1))
                for t in range(4):
                    mm = pe.transpose(pm[0:N_EXP, t * P:(t + 1) * P], rwn[:, t, :], identf[:, :])
                mm.then_inc(s_wt, 1)

                for t in range(1, T0):
                    if g == 0 and t == ST:
                        pe.wait_ge(s_wlo[0], 5)
                        pe.wait_ge(s_wlo[1], 5)
                        pe.wait_ge(s_whi, SEL_PIECE + 1)
                    gate_up(t)
                    if t >= 2:
                        down0(g, t - 2)
                    if t == LN_AT:
                        ln_mean(g + 1)
                    if t == LN_AT + 3:
                        ln_var(g + 1)
                down0(g, T0 - 2)
            down0(G - 1, T0 - 1)

            pe.wait_ge(s_res, G)
            pe.wait_ge(s_h, T0 * G)
            for i in range(2):
                pe.wait_ge(s_wlo[i], len(lo_of[i]))

            def latents(nb):
                g, hb = nb // 2, nb % 2
                for t in range(2):
                    tok = slice(hb * SEQ + t * P, hb * SEQ + (t + 1) * P)
                    o = pm[:, t * 256:(t + 1) * 256]
                    for k in range(KD):
                        s = w0k(A_DN, 256, k, 0, 256)
                        xx = (xh[:, k, tok], xl[:, k, tok])
                        pe.matmul(o, xx[0], ah[:, s], start=k == 0, stop=False, skip_group_check=True)
                        pe.matmul(o, xx[1], ah[:, s], start=False, stop=False, skip_group_check=True)
                        mm = pe.matmul(o, xx[0], al[:, s], start=False, stop=k == KD - 1, skip_group_check=True)
                mm.then_inc(s_cps, 1)

            def turn_latents(nb):
                pe.wait_ge(s_cn, 4 * (nb + 1))
                if nb:
                    pe.wait_ge(s_qkvb, 3 * nb)
                for t in range(2):
                    pe.transpose(pv[0:D_Q, t * P:(t + 1) * P], cn[:, t, 0:D_Q], identf[:, :])
                    mm = pe.transpose(pv[:, SEQ + t * P:SEQ + (t + 1) * P], cn[:, t, D_Q:D_Q + D_KV], identf[:, :])
                mm.then_inc(s_ctr, 1)

            def up(nb, which):
                rows, off, seg, bank = ((D_Q, A_UQ, 0, pm), (P, A_UKV, 1, pv), (P, A_UKV + P, 1, pm))[which]
                for t in range(2):
                    ch, cl = cth[0:rows, seg, t * P:(t + 1) * P], ctl[0:rows, seg, t * P:(t + 1) * P]
                    o = bank[:, t * 256:(t + 1) * 256]
                    pe.matmul(o, ch, ah[0:rows, off:off + 256], start=True, stop=False, skip_group_check=True)
                    pe.matmul(o, cl, ah[0:rows, off:off + 256], start=False, stop=False, skip_group_check=True)
                    mm = pe.matmul(o, ch, al[0:rows, off:off + 256], start=False, stop=True, skip_group_check=True)
                mm.then_inc(s_qkv, 1)

            def up_qk(nb):
                pe.wait_ge(s_ctl, 2 * nb + 2)
                up(nb, 0)
                up(nb, 1)

            def up_v(nb):
                pe.wait_ge(s_qkvb, 3 * nb + 1)
                up(nb, 2)

            def turn_slots(nb):
                pe.wait_ge(s_split, 8 * (nb + 1))
                pe.wait_ge(s_copy, 6 * (nb + 1))
                if nb == 0:
                    pe.wait_ge(s_const, 16 * 12)
                    pe.wait_ge(s_prep, SETUP0 + SETUP1)
                if nb:
                    pe.wait_ge(s_e, 12 * nb)
                for f in range(8):
                    if f >= 3:
                        u = f - 3
                        (pe.wait_ge(s_evA, 4 * nb + u // 2 + 1) if u % 2 == 0
                         else pe.wait_ge(s_evD, 4 * nb + u // 2 + 1))
                    src = qbuf[f // 4][0]
                    bank = ring[f % 3][:, :].bitcast(BF16)
                    for h in range(4):
                        for t in range(2):
                            mm = pe.transpose(bank[0:SLOT, h * SEQ + t * P:h * SEQ + (t + 1) * P],
                                              src[:, t, 4 * (f % 4) + h, :], ident[:, :])
                    mm.then_inc(s_tr, 1)

            def scores(nb):
                pe.wait_ge(s_evA, 4 * nb + 4)
                pe.wait_ge(s_evD, 4 * nb + 4)
                for f in range(12):
                    if f >= 3:
                        pe.wait_ge(s_mx, 12 * nb + f - 2)
                    i = 0 if f < 4 else 1
                    width = (i + 1) * P
                    heads = range(4 * f, 4 * f + 4) if i == 0 else range(2 * (f - 4), 2 * (f - 4) + 2)
                    for n, h in enumerate(heads):
                        o = ring[f % 3][:, n * width:(n + 1) * width]
                        pe.matmul(o, qT[0:SLOT, h, i * P:(i + 1) * P], kT[0:SLOT, h, 0:width], start=True, stop=False,
                                  skip_group_check=True)
                        mm = pe.matmul(o[:, i * P:(i + 1) * P], ident[:, :], maskq[:, :], start=False, stop=True,
                                       skip_group_check=True)
                    mm.then_inc(s_s, 1)

            def turn_max(nb):
                pe.wait_ge(s_nm, 2 * nb + 2)
                mbank = ring[3][:, :].bitcast(BF16)
                for i in range(2):
                    mm = pe.transpose(mbank[0:2 * H, i * P:(i + 1) * P],
                                      nm[:, i, :, :].rearrange("p a h -> p (a h)"), ident[:, :])
                mm.then_inc(s_mtr, 1)

            def probs(nb, hg):
                if hg == 0:
                    pe.wait_ge(s_md, 32 * (nb + 1))
                    pe.wait_ge(s_mx, 12 * nb + 12)
                for part in range(3):
                    f = 3 * hg + part
                    if f >= 3:
                        pe.wait_ge(s_e, 12 * nb + f - 2)
                    kt = 0 if part < 2 else 1
                    heads = range(4 * hg + 2 * part, 4 * hg + 2 * part + 2) if kt == 0 else \
                        range(4 * hg, 4 * hg + 4)
                    width = SEQ - kt * P
                    for n, h in enumerate(heads):
                        o = ring[f % 3][:, n * width:(n + 1) * width]
                        pe.matmul(o, kT[0:SLOT + 2, h, kt * P:(kt + 1) * P], qT[0:SLOT + 2, h, kt * P:SEQ], start=True,
                                  stop=False, skip_group_check=True)
                        mm = pe.matmul(o[:, 0:P], ident[:, :], maskk[:, :], start=False, stop=True,
                                       skip_group_check=True)
                    mm.then_inc(s_sT, 1)

            def values(nb, hg):
                n = 4 * nb + hg
                for done in (s_phs, s_pls):
                    pe.wait_ge(done[0], (3 * n + 4) // 2)
                    pe.wait_ge(done[1], (3 * n + 3) // 2)
                if hg == 0:
                    pe.wait_ge(s_mT, nb + 1)
                    pe.wait_ge(s_vsp, 4 * (nb + 1))
                else:
                    pe.wait_ge(s_yst, 2 * n - 1)
                bank = ring[3]
                for i in range(2):
                    for hn in range(4):
                        o = bank[:, (4 * i + hn) * 51:(4 * i + hn + 1) * 51]
                        for kt in range(i + 1):
                            if kt == 0:
                                slot, col = (3 * n + hn // 2) % NP, (hn % 2) * SEQ + i * P
                            else:
                                slot, col = (3 * n + 2) % NP, hn * P
                            vv = v3[:, kt, 4 * hg + hn, :, :].rearrange("p s d -> p (s d)")
                            pe.matmul(o, ph[:, slot, col:col + P], vv, start=kt == 0, stop=False,
                                      skip_group_check=True)
                            mm = pe.matmul(o, pl[:, slot, col:col + P], vv, start=False, stop=kt == i,
                                           skip_group_check=True)
                mm.then_inc(s_y, 1)

            def turn_y(nb):
                pe.wait_ge(s_yn, 4 * nb + 4)
                for m in range(KD):
                    for i in range(2):
                        mm = pe.transpose(ring[3][:, m * SEQ + i * P:m * SEQ + (i + 1) * P],
                                          y[:, i, 8 * m:8 * m + 8, :].rearrange("p h d -> p (h d)"), identf[:, :])
                mm.then_inc(s_ytr, 1)

            def project(nb):
                g, hb = nb // 2, nb % 2
                pe.wait_ge(s_yl, nb + 1)
                for m in range(KD):
                    for k in range(KD):
                        s = w0k(A_O, D, k, m * P, (m + 1) * P)
                        mm = prod(acc[:, m, hb * SEQ:(hb + 1) * SEQ], (ah[:, s], al[:, s]), yh[:, k, :],
                                  yl[:, k, :], g == 0 and hb == 0 and k == 0, False)
                mm.then_inc(s_ao, 1)

            for g in range(G):
                fill = MID[g]

                def gate_up1(t):
                    n = T0 * G + g * T1 + t
                    if t == MID[g]:
                        pe.wait_ge(s_qkvb, 6 * (g + 1))
                    elif MID[g] < t < REST[g]:
                        pe.wait_ge(s_h, n)
                    elif t >= 2:
                        pe.wait_ge(s_h, n - 1)
                    if t == REST[g]:
                        pe.wait_ge(s_e, 24 * (g + 1))
                    for up, off in enumerate((O_G4, O_U4)):
                        for k in range(KD):
                            mm = prod(bank_of(g, t, up)[:, :], w(off, MLP, k, t * P, (t + 1) * P), xh[:, k, :],
                                      xl[:, k, :], k == 0, k == KD - 1)
                    mm.then_inc(s_gu, 1)

                def down1(t):
                    if fill and t == 0:
                        pe.wait_ge(s_res, G + g)
                    down(T0 * G + g * T1 + t, O_D4, t, P, t == T1 - 1, g > 0 and t == 0)

                b0, b1 = 2 * g, 2 * g + 1
                tile = lambda t: gate_up1(t) if t < fill else None
                drop = lambda t: down1(t) if 0 <= t < fill else None
                if g == 0:
                    normed(G)
                    latents(0)
                tile(0)
                turn_latents(b0)
                tile(1)
                up_qk(b0)
                tile(2)
                drop(0)
                up_v(b0)
                for t in range(3, fill):
                    tile(t)
                    drop(t - 2)
                drop(fill - 2)
                drop(fill - 1)
                turn_slots(b0)
                latents(b1)
                scores(b0)
                turn_max(b0)
                turn_latents(b1)
                probs(b0, 0)
                up_qk(b1)
                probs(b0, 1)
                values(b0, 0)
                up_v(b1)
                probs(b0, 2)
                values(b0, 1)
                probs(b0, 3)
                values(b0, 2)
                turn_slots(b1)
                values(b0, 3)
                turn_y(b0)
                if g:
                    gate_up1(MID[g])
                project(b0)
                if g == 0:
                    pe.wait_ge(s_w4in, 64)
                t = MID[g]
                if g == 0:
                    gate_up1(t)
                scores(b1)
                gate_up1(t + 1)
                turn_max(b1)
                down1(t)
                gate_up1(t + 2)
                probs(b1, 0)
                down1(t + 1)
                probs(b1, 1)
                values(b1, 0)
                down1(t + 2)
                probs(b1, 2)
                values(b1, 1)
                probs(b1, 3)
                gate_up1(t + 3)
                values(b1, 2)
                values(b1, 3)
                gate_up1(REST[g])
                turn_y(b1)
                down1(t + 3)
                project(b1)
                for t in range(REST[g] + 1, T1):
                    gate_up1(t)
                    if t >= REST[g] + 2:
                        down1(t - 2)
                    if g < G - 1 and t == LN_AT1:
                        ln_mean(G + g + 1)
                    if g < G - 1 and t == LN_AT1 + 1:
                        ln_var(G + g + 1)
                down1(T1 - 2)
                if g < G - 1:
                    normed(G + g + 1)
                    latents(b1 + 1)
                down1(T1 - 1)

        @block.scalar
        def _(a):
            def ln_square(n):
                a.wait_ge(s_xc, n + 1)
                a.activation(sq[:, :, :], xc[:, :, :], ACT.Square).then_inc(s_sq, 1)

            def ln_std(n):
                a.wait_ge(s_var, n + 1)
                a.activation(std[:, :], pm[:, :], ACT.Sqrt, bias=epsb[:, :]).then_inc(s_std, 1)

            def ln_hi(n):
                a.wait_ge(s_xn, n + 1)
                if n >= 1:
                    a.wait_ge(s_gu, T0 * n if n <= G else T0 * G + T1 * (n - G))
                a.activation(xh[:, :, :], xc[:, :, :], ACT.Copy).then_inc(s_xh, 1)

            def weights(*which):
                for n in which:
                    a.wait_ge(s_stage[n % NS], 16 * (n // NS + 1))
                    a.activation(pieces[n][1], staged(n), ACT.Copy).then_inc(s_whi, 1)

            def dequant(k):
                if 2 <= k < 2 * NQ + 2:
                    a.wait_ge(s_w, k - 1)
                    if k >= 4:
                        a.wait_ge(s_w4out[k % 2], 32 * (k // 2 - 1))
                    a.activation(w4h[:, k % 2, :], wf[:, :], ACT.Copy).then_inc(s_w4h, 1)
                if 0 <= k < 2 * NQ:
                    a.wait_ge(s_bits, 3 * (k + 1))
                    a.activation(gval[:, k % 2, :], fbits[:, :].bitcast(F32), ACT.Copy, bias=-1.0,
                                 scale=8.0).then_inc(s_val, 1)

            def activate(n, bank, rows, func):
                a.wait_ge(s_gu, n + 1)
                if n >= 2:
                    a.wait_ge(s_h, n - 1)
                a.activation(act[0:rows, n % 2, :], bank[0:rows, :], func).then_inc(s_act, 1)

            def split_h(n, rows, routed):
                if routed is None:
                    a.wait_ge(s_h, n + 1)
                else:
                    a.wait_ge(s_hw, routed + 1)
                if n >= HB:
                    a.wait_ge(s_dn, n - HB + 1)
                a.activation(hh[0:rows, n % HB, :], hf[0:rows, n % 2, :], ACT.Copy).then_inc(s_hh, 1)

            a.dma_start(gwf[:, :, :], gateT).then_inc(s_const, 16)
            a.dma_start(tie[:, :, :], tie_c).then_inc(s_const, 16)
            weights(0)
            ln_square(0)
            weights(1)
            a.wait_ge(s_const, 64)
            a.activation(gw[:, 0, :, :], gwf[:, :, :], ACT.Copy).then_inc(s_gwh, 1)
            a.wait_ge(s_prep, SETUP0)
            ln_std(0)
            weights(2, 3)
            ln_hi(0)
            for g in range(G):
                if g == 0:
                    weights(4)
                for m in range(KD):
                    a.wait_ge(s_v, 2 * g + m + 1)
                    a.activation(vs[:, m, :], ring[(0, 3)[m]][:, :], ACT.Copy, scale=DENOM).then_inc(s_vs, 1)
                    if g == 0 and m == 0:
                        weights(5)
                if g >= 1:
                    a.wait_ge(s_res, g)
                    a.dma_start(x1_at(g - 1), xg(g - 1)).then_inc(s_out, 16)
                if g == 0:
                    weights(6)
                a.wait_ge(s_lg, g + 1)
                a.activation(sig[:, :], pm[0:N_EXP, :], ACT.Sigmoid).then_inc(s_sig, 1)
                for m in range(KD):
                    a.wait_ge(s_vh, 2 * g + m + 1)
                    if g >= 1 and m == 0:
                        a.wait_ge(s_oproj, g)
                    a.activation(vhh[:, m, :], vfl[:, m, :], ACT.Copy).then_inc(s_vhh, 1)
                if g == 0:
                    weights(7)
                a.wait_ge(s_wt, g + 1)
                if g >= 1:
                    a.wait_ge(s_wbc, XT * g)
                a.activation(wT[0:N_EXP, :], pm[0:N_EXP, :], ACT.Copy).then_inc(s_wth, 1)
                if g >= 1:
                    a.wait_ge(s_out, 16 * g)
                    a.dma_start(xg(g + 1), xT[:, :, (g + 1) * NT:(g + 2) * NT] if g + 1 < G else x1_at(0)).then_inc(s_x, 16)
                for t in range(T0):
                    n = g * T0 + t
                    activate(n, ring[2 * (t % 2)], ST_M[t] if t < ST else P, ACT.Silu)
                    if g == 0 and t < ST:
                        weights(*((8, 9), (SEL_PIECE,), (SEL_PIECE + 1, SEL_PIECE + 2))[t])
                    if t >= 1:
                        u = t - 1
                        split_h(n - 1, ST_M[u] if u < ST else P, None if u < ST else g * XT + u - ST)
                    dequant(step_at(n))
                    if t == LN_AT + 2:
                        ln_square(g + 1)
                    if t == LN_AT + 4:
                        ln_std(g + 1)
                ln_hi(g + 1)
                split_h(g * T0 + T0 - 1, P, g * XT + XT - 1)

            def latents_std(nb):
                a.wait_ge(s_bn, 8 * (nb + 1))
                a.activation(cstd[:, :], mv[:, :, 1], ACT.Sqrt, bias=epsb[:, :]).then_inc(s_cstd, 1)

            def latents_hi(nb):
                for which in range(2):
                    a.wait_ge(s_ct, 2 * nb + which + 1)
                    rows = (D_Q, P)[which]
                    a.activation(cth[0:rows, which, :], ctf[0:rows, which, :], ACT.Copy).then_inc(s_cth, 1)

            def copy_slots(nb, which):
                for step, t, a0, b0 in which:
                    a.wait_ge(s_split, 8 * nb + step)
                    a.activation(t[:, :, :, b0 * DH:(b0 + 1) * DH], t[:, :, :, a0 * DH:(a0 + 1) * DH],
                                 ACT.Copy).then_inc(s_copy, 1)

            first_parts = ((1, qs, 0, 1), (2, ks, 0, 2), (1, qs, 0, 4), (2, ks, 0, 5))
            second_parts = ((5, qs, 2, 3), (6, ks, 1, 3))

            def turned(nb):
                for f in range(0, 8, 2):
                    a.wait_ge(s_tr, 8 * nb + f + 1)
                    a.activation(qbuf[f // 4][2][0:SLOT, 4 * (f % 4):4 * (f % 4) + 4, :].rearrange("p h t -> p (h t)"),
                                 ring[f % 3][0:SLOT, :].bitcast(BF16), ACT.Copy).then_inc(s_evA, 1)

            def place_max(nb):
                a.wait_ge(s_mtr, nb + 1)
                a.activation(mT[0:2 * H, :], ring[3][:, :].bitcast(BF16)[0:2 * H, 0:SEQ], ACT.Copy).then_inc(s_mT, 1)
                a.wait_ge(s_mT, nb + 1)
                for part in range(2):
                    a.dma_start(qT[SLOT + part:SLOT + part + 1, :, :], mT[part * H:(part + 1) * H, :]).then_inc(s_md, 16)

            def exponentials(nb, f):
                n = 12 * nb + f
                a.wait_ge(s_sT, n + 1)
                if n >= 2:
                    a.wait_ge(s_pls[n % 2], n // 2)
                a.activation(exps(n), ring[f % 3][:, :], ACT.Exp, scale=SCALE).then_inc(s_e, 1)
                if n % 2 == 0:
                    a.wait_ge(s_e, n + 1)
                    if n >= NP:
                        a.wait_ge(s_y, (n - NP) // 3 + 1)
                    a.activation(ph[:, n % NP, :], exps(n), ACT.Copy).then_inc(s_phs[0], 1)

            def y_hi(nb):
                a.wait_ge(s_ytr, nb + 1)
                if nb >= 1:
                    a.wait_ge(s_ao, nb)
                a.activation(yh[:, :, :], ring[3][:, :].rearrange("p (k t) -> p k t", k=KD), ACT.Copy).then_inc(s_yh, 1)

            for g in range(G):
                fill = MID[g]
                b0, b1 = 2 * g, 2 * g + 1

                tile = lambda t: T0 * G + g * T1 + t
                gelu = lambda t: activate(tile(t), bank_of(g, t, 0), P, ACT.Gelu_apprx_tanh) if t < T1 else None
                hi = lambda t: split_h(tile(t), P, None)

                latents_std(b0)
                if fill:
                    gelu(0)
                    hi(0)
                latents_hi(b0)
                for t in range(1, min(fill, 4)):
                    gelu(t)
                    hi(t)
                copy_slots(b0, first_parts)
                if fill:
                    gelu(4)
                    hi(4)
                copy_slots(b0, second_parts)
                for t in range(5, fill):
                    gelu(t)
                    hi(t)
                a.wait_ge(s_out, 16 * (G + g))
                turned(b0)
                latents_std(b1)
                place_max(b0)
                exponentials(b0, 0)
                latents_hi(b1)
                for f in range(1, 12):
                    exponentials(b0, f)
                    if f == COPY_AT:
                        copy_slots(b1, first_parts)
                copy_slots(b1, second_parts)
                turned(b1)
                y_hi(b0)
                t = MID[g]
                gelu(t)
                hi(t)
                gelu(t + 1)
                place_max(b1)
                hi(t + 1)
                gelu(t + 2)
                hi(t + 2)
                for f in range(12):
                    exponentials(b1, f)
                gelu(t + 3)
                hi(t + 3)
                gelu(REST[g])
                y_hi(b1)
                for t in range(REST[g] + 1, T1 + 1):
                    gelu(t)
                    if g < G - 1 and t == T1:
                        ln_hi(G + g + 1)
                    hi(t - 1)
                    if g < G - 1 and t == LN_AT1:
                        ln_square(G + g + 1)
                    if g < G - 1 and t == LN_AT1 + 2:
                        ln_std(G + g + 1)

        @block.gpsimd
        def _(pool):
            def low(dst, src, hi):
                return pool.tensor_tensor(dst, src, hi.bitcast(F32), ALU.subtract)

            def split_h(n, rows):
                pool.wait_ge(s_hh, n + 1)
                low(hl[0:rows, n % HB, :], hf[0:rows, n % 2, :], hh[0:rows, n % HB, :]).then_inc(s_hl, 1)

            def weights(*which):
                for n in which:
                    pool.wait_ge(s_whi, n + 1)
                    low(pieces[n][2], staged(n), pieces[n][1]).then_inc(s_wlo[1], 1)

            def dequant(k):
                if 2 <= k < 2 * NQ + 2:
                    pool.wait_ge(s_w4h, k - 1)
                    low(w4l[:, k % 2, :], wf[:, :], w4h[:, k % 2, :]).then_inc(s_w4l, 1)
                if 1 <= k < 2 * NQ + 1:
                    pool.wait_ge(s_sgn, 2 * k)
                    pool.wait_ge(s_scl, 16 * ((k - 1) // 2 + 1))
                    if k >= 2:
                        pool.wait_ge(s_w4l, k - 1)
                    pool.tensor_tensor(wf[:, :], gval[:, (k - 1) % 2, :], scl[:, :], ALU.mult).then_inc(s_w, 1)

            weights(1, 3, 5, 7)
            for g in range(G):
                for t in range(T0):
                    split_h(g * T0 + t, ST_M[t] if t < ST else P)
                    if g == 0 and t < 2:
                        weights((9, SEL_PIECE + 1)[t])
                    dequant(step_at(g * T0 + t))
            pool.wait_ge(s_res, G)
            for i in range(2):
                pool.wait_ge(s_w4out[i], 32 * NQ)
            pool.memset(v3[:, :, :, :, DH:], 0.0).then_inc(s_prep, 1)
            pool.wait_ge(s_prep, SETUP0 + 1)
            pool.memset(v3[:, :, :, 0, DH:], 1.0).then_inc(s_prep, 1)
            pool.wait_ge(s_prep, SETUP0 + 2)
            pool.memset(kT[SLOT:SLOT + 2, :, :], 1.0).then_inc(s_prep, 1)
            pool.wait_ge(s_prep, SETUP0 + SETUP1)
            def split_values(nb):
                if nb:
                    pool.wait_ge(s_y, 4 * nb)
                pool.wait_ge(s_qkvb, 3 * (nb + 1))
                n = 4 * nb
                part = lambda i: v3[:, :, :, i, 0:DH]
                pool.tensor_copy(part(0), vf).then_inc(s_vsp, 1)
                pool.wait_ge(s_vsp, n + 1)
                pool.tensor_tensor(vf, vf, part(0), ALU.subtract).then_inc(s_vsp, 1)
                pool.wait_ge(s_vsp, n + 2)
                pool.tensor_copy(part(1), vf).then_inc(s_vsp, 1)
                pool.wait_ge(s_vsp, n + 3)
                pool.tensor_tensor(part(2), vf, part(1), ALU.subtract).then_inc(s_vsp, 1)

            for g in range(G):
                fill = MID[g]
                n0 = T0 * G + g * T1

                def probs_lo(nb):
                    for n in range(12 * nb, 12 * nb + 12, 1 + nb % 2):
                        pool.wait_ge(s_phs[n % 2], n // 2 + 1)
                        pool.tensor_tensor(pl[:, n % NP, :], exps(n), ph[:, n % NP, :],
                                           ALU.subtract).then_inc(s_pls[n % 2], 1)

                for t in range(fill):
                    split_h(n0 + t, P)
                split_values(2 * g)
                probs_lo(2 * g)
                split_h(n0 + fill, P)
                split_values(2 * g + 1)
                split_h(n0 + fill + 1, P)
                split_h(n0 + fill + 2, P)
                probs_lo(2 * g + 1)
                for t in range(fill + 3, T1):
                    split_h(n0 + t, P)

        @block.vector
        def _(v):
            def sub(dst, src, hi):
                return v.tensor_tensor(dst, src, hi.bitcast(F32), ALU.subtract)

            def ln_centre(n):
                v.wait_ge(s_x, 16 * (n + 1))
                v.wait_ge(s_mean, n + 1)
                mean = pm[:, :].unsqueeze(1).to_broadcast([P, KD, NT])
                v.tensor_tensor(xc[:, :, :], xg(n), mean, ALU.subtract).then_inc(s_xc, 1)

            def ln_inverse(n, *quarters):
                for i in quarters:
                    v.wait_ge(s_std, n + 1)
                    cols = slice(i * P, (i + 1) * P)
                    v.reciprocal(rstd[:, cols], std[:, cols]).then_inc(s_rstd, 1)

            def ln_scale(n):
                v.wait_ge(s_rstd, 4 * (n + 1))
                v.tensor_tensor(xc[:, :, :], xc[:, :, :], rstd[:, :].unsqueeze(1).to_broadcast([P, KD, NT]),
                                ALU.mult).then_inc(s_xn, 1)

            def ln_lo(n):
                v.wait_ge(s_xh, n + 1)
                sub(xl[:, :, :], xc[:, :, :], xh[:, :, :]).then_inc(s_xl, 1)

            def weights(*which):
                for n in which:
                    v.wait_ge(s_whi, n + 1)
                    sub(pieces[n][2], staged(n), pieces[n][1]).then_inc(s_wlo[0], 1)

            u32 = mybir.dt.uint32

            def dequant(k):
                if 1 <= k < 2 * NQ + 1:
                    v.wait_ge(s_val, k)
                    val = gval[:, (k - 1) % 2, :]
                    v.scalar_tensor_tensor(out=val, in0=fbits[:, :].bitcast(F32), scalar=4.0, in1=val, op0=ALU.mult,
                                           op1=ALU.min).then_inc(s_sgn, 1)
                    v.wait_ge(s_sgn, 2 * k - 1)
                    v.tensor_tensor(val.bitcast(u32), val.bitcast(u32), sbits[:, :].bitcast(u32),
                                    ALU.bitwise_or).then_inc(s_sgn, 1)
                if 0 <= k < 2 * NQ:
                    j = k % 2
                    v.wait_ge(s_words[k // 2 % 2], 16 * (k // 4 + 1))
                    if k:
                        v.wait_ge(s_sgn, 2 * k)
                    w32, f32 = words[:, k // 2 % 2, :].bitcast(u32), fbits[:, :].bitcast(u32)
                    v.tensor_scalar(f32, w32, 22 - 4 * j, 7 << 22, ALU.logical_shift_left,
                                    ALU.bitwise_and).then_inc(s_bits, 1)
                    v.tensor_scalar(sbits[:, :].bitcast(u32), w32, 28 - 4 * j, 1 << 31, ALU.logical_shift_left,
                                    ALU.bitwise_and).then_inc(s_bits, 1)
                    v.wait_ge(s_bits, 3 * k + 2)
                    v.tensor_scalar(f32, f32, 124 << 23, None, ALU.bitwise_or).then_inc(s_bits, 1)

            def gated(n, bank, rows):
                v.wait_ge(s_act, n + 1)
                if n >= 2:
                    v.wait_ge(s_hl, n - 1)
                v.tensor_tensor(hf[0:rows, n % 2, :], act[0:rows, n % 2, :], bank[0:rows, :],
                                ALU.mult).then_inc(s_h, 1)

            v.wait_ge(s_const, 64)
            ln_centre(0)
            weights(0)
            v.memset(epsb[:, :], EPS).then_inc(s_prep, 1)
            v.memset(unit[:, :], 1.0).then_inc(s_prep, 1)
            v.memset(wT[:, :].bitcast(F32), 0.0).then_inc(s_prep, 1)
            v.wait_ge(s_gwh, 1)
            sub(gw[:, 1, :, :], gwf[:, :, :], gw[:, 0, :, :]).then_inc(s_prep, 1)
            v.wait_ge(s_prep, SETUP0)
            ln_inverse(0, 0, 1, 2, 3)
            ln_scale(0)
            ln_lo(0)
            for g in range(G):
                if g == 0:
                    weights(2)
                for m in range(KD):
                    n = 2 * g + m
                    v.wait_ge(s_k, n + 1)
                    v.wait_ge(s_vs, n + 1)
                    v.tensor_tensor(kv0[:, m, :], ring[(1, 0)[m]][:, :], vs[:, m, :], ALU.mult).then_inc(s_kv, 1)
                    v.wait_ge(s_kv, n + 1)
                    for b in range(NT // SEQ):
                        cols = slice(b * SEQ, (b + 1) * SEQ)
                        v.tensor_tensor_scan(kvt[:, m, cols], unit[:, :].to_broadcast([P, SEQ]), kv0[:, m, cols], 0.0, ALU.mult,
                                             ALU.add).then_inc(s_scan, 1)
                    v.wait_ge(s_scan, 2 * n + 2)
                    v.wait_ge(s_q, n + 1)
                    if m == 0 and g >= 1:
                        v.wait_ge(s_hl, T0 * g)
                    v.tensor_tensor(vfl[:, m, :], ring[(2, 1)[m]][:, :], kvt[:, m, :], ALU.mult).then_inc(s_vh, 1)
                for m in range(KD):
                    v.wait_ge(s_vh, 2 * g + m + 1)
                    v.wait_ge(s_vhh, 2 * g + m + 1)
                    sub(vhl[:, m, :], vfl[:, m, :], vhh[:, m, :]).then_inc(s_vhl, 1)
                if g == 0:
                    weights(4)
                r = 11 * g
                v.wait_ge(s_st, g + 1)
                v.tensor_copy(sc[:, :, :].rearrange("p t e -> p (t e)"), pv[:, 0:4 * N_EXP]).then_inc(s_rk, 1)
                v.wait_ge(s_rk, r + 1)
                other = sc[:, :, :].unsqueeze(2).to_broadcast([P, 4, N_EXP, N_EXP])
                own = sc[:, :, :].unsqueeze(3).to_broadcast([P, 4, N_EXP, N_EXP])
                v.tensor_tensor(gt[:, :, :, :], other, own, ALU.is_gt).then_inc(s_rk, 1)
                v.tensor_tensor(ge[:, :, :, :], other, own, ALU.is_ge).then_inc(s_rk, 1)
                v.wait_ge(s_rk, r + 3)
                v.tensor_tensor(ge[:, :, :, :], ge[:, :, :, :],
                                tie[:, :, :].unsqueeze(1).to_broadcast([P, 4, N_EXP, N_EXP]),
                                ALU.mult).then_inc(s_rk, 1)
                v.wait_ge(s_rk, r + 4)
                v.tensor_tensor(gt[:, :, :, :], gt[:, :, :, :], ge[:, :, :, :], ALU.max).then_inc(s_rk, 1)
                v.wait_ge(s_rk, r + 5)
                v.tensor_reduce(rank[:, :, :], gt[:, :, :, :], AX.X, ALU.add).then_inc(s_rk, 1)
                v.wait_ge(s_rk, r + 6)
                v.scalar_tensor_tensor(out=rw[:, :, :], in0=rank[:, :, :], scalar=1.5, in1=sc[:, :, :],
                                       op0=ALU.is_lt, op1=ALU.mult).then_inc(s_rk, 1)
                v.wait_ge(s_rk, r + 7)
                v.tensor_reduce(rsum[:, :], rw[:, :, :], AX.X, ALU.add).then_inc(s_rk, 1)
                v.wait_ge(s_rk, r + 8)
                v.tensor_scalar(rsum[:, :], rsum[:, :], 1e-20, None, ALU.add).then_inc(s_rk, 1)
                v.wait_ge(s_rk, r + 9)
                v.reciprocal(rrec[:, :], rsum[:, :]).then_inc(s_rk, 1)
                v.wait_ge(s_rk, r + 10)
                v.scalar_tensor_tensor(out=rwn[:, :, :], in0=rw[:, :, :], scalar=ROUTE_SCALE,
                                       in1=rrec[:, :].unsqueeze(2).to_broadcast([P, 4, N_EXP]),
                                       op0=ALU.mult, op1=ALU.mult).then_inc(s_rk, 1)
                if g == 0:
                    weights(6)
                v.wait_ge(s_wth, g + 1)
                sub(wT[32:32 + N_EXP, :], pm[0:N_EXP, :], wT[0:N_EXP, :]).then_inc(s_wtl, 1)
                for t in range(T0):
                    n = g * T0 + t
                    gated(n, ring[2 * (t % 2) + 1], ST_M[t] if t < ST else P)
                    if g == 0 and t in (0, 2):
                        weights(8 if t == 0 else SEL_PIECE + 2)
                    if t >= ST:
                        e = g * XT + t - ST
                        v.wait_ge(s_h, n + 1)
                        v.wait_ge(s_wbc, e + 1)
                        v.tensor_tensor(hf[:, n % 2, :], hf[:, n % 2, :], pv[:, :], ALU.mult).then_inc(s_hw, 1)
                    dequant(step_at(n))
                    if t == LN_AT + 1:
                        ln_centre(g + 1)
                    if LN_AT + 5 <= t < LN_AT + 9:
                        ln_inverse(g + 1, t - LN_AT - 5)
                    if t == LN_AT + 8:
                        ln_scale(g + 1)
                ln_lo(g + 1)
                v.wait_ge(s_dn, T0 * (g + 1))
                v.tensor_tensor(xg(g), xg(g), acc[:, :, :], ALU.add).then_inc(s_res, 1)

            for i in range(2):
                v.wait_ge(s_w4out[i], 32 * NQ)
            v.wait_ge(s_res, G)

            def bias_latents(nb):
                v.wait_ge(s_cps, nb + 1)
                if nb == 0:
                    v.wait_ge(s_bc, 16)
                both = lambda ap: ap.unsqueeze(1).to_broadcast([P, 2, ap.shape[1]])
                v.tensor_tensor(c[:, :, :], pm[:, :].rearrange("p (t n) -> p t n", t=2)[:, :, 0:C_W], both(bc[:, :]),
                                ALU.add).then_inc(s_c, 1)
                v.wait_ge(s_c, nb + 1)
                for t in range(2):
                    for w in range(2):
                        v.bn_stats(bst[:, 2 * t + w, :], c[:, t, seg[w]]).then_inc(s_bn, 1)
                v.wait_ge(s_bn, 8 * nb + 4)
                for i in range(4):
                    v.bn_aggr(mv[:, i, :], bst[:, i, :]).then_inc(s_bn, 1)

            def norm_latents(nb):
                v.wait_ge(s_cstd, nb + 1)
                v.wait_ge(s_bn, 8 * nb + 8)
                v.reciprocal(crs[:, :], cstd[:, :]).then_inc(s_crs, 1)
                v.wait_ge(s_crs, nb + 1)
                for t in range(2):
                    for w in range(2):
                        i = 2 * t + w
                        v.tensor_scalar(cn[:, t, seg[w]], c[:, t, seg[w]], mv[:, i, 0:1], crs[:, i:i + 1],
                                        ALU.subtract, ALU.mult).then_inc(s_cn, 1)

            def affine_latents(nb):
                if nb == 0:
                    v.wait_ge(s_const, 16 * 12)
                v.wait_ge(s_ctr, nb + 1)
                for w, rows in ((0, D_Q), (1, P)):
                    v.tensor_scalar(ctf[0:rows, w, :], pv[0:rows, w * SEQ:(w + 1) * SEQ], gb[0:rows, 2 * w:2 * w + 1],
                                    gb[0:rows, 2 * w + 1:2 * w + 2], ALU.mult, ALU.add).then_inc(s_ct, 1)
                for w, rows in ((0, D_Q), (1, P)):
                    v.wait_ge(s_cth, 2 * nb + w + 1)
                    sub(ctl[0:rows, w, :], ctf[0:rows, w, :], cth[0:rows, w, :]).then_inc(s_ctl, 1)

            heads = lambda ap, n: ap.rearrange("p t (h d) -> p t h d", h=n)
            tiles = lambda bank: bank[:, :].rearrange("p (t n) -> p t n", t=2)
            both = lambda ap: ap.unsqueeze(1).to_broadcast([P, 2, ap.shape[1]])

            def bias_qk(nb):
                v.wait_ge(s_qkv, 3 * nb + 1)
                v.tensor_tensor(qf.rearrange("p t h d -> p t (h d)"), tiles(pm), both(bq[:, :]),
                                ALU.add).then_inc(s_qkvb, 1)
                v.wait_ge(s_qkv, 3 * nb + 2)
                for t in range(2):
                    kb = v.tensor_tensor(kf[:, t, :, 0:DN], tiles(pv)[:, t, 0:P].rearrange("p (h d) -> p h d", h=H),
                                         bkv[:, 0:P].rearrange("p (h d) -> p h d", h=H), ALU.add)
                kb.then_inc(s_qkvb, 1)

            def bias_v(nb):
                v.wait_ge(s_qkv, 3 * nb + 3)
                if nb:
                    v.wait_ge(s_vsp, 4 * nb)
                v.tensor_tensor(vf.rearrange("p t h d -> p t (h d)"), tiles(pm), both(bkv[:, P:]),
                                ALU.add).then_inc(s_qkvb, 1)

            def rotate(nb):
                v.wait_ge(s_qkvb, 3 * nb + 2)
                x1, x2 = qf[:, :, :, DN:DN + 4], qf[:, :, :, DN + 4:]
                cos, sin = (rot[:, i, :, :].unsqueeze(1).to_broadcast([P, 2, H, 4]) for i in range(2))
                for i, (xx, tt) in enumerate(((x1, cos), (x2, sin), (x1, sin), (x2, cos))):
                    v.tensor_tensor(rt[:, i, :, :, :], xx, tt, ALU.mult).then_inc(s_rope, 1)
                v.wait_ge(s_rope, 7 * nb + 4)
                v.tensor_tensor(x1, rt[:, 0, :, :, :], rt[:, 1, :, :, :], ALU.add).then_inc(s_rope, 1)
                v.tensor_tensor(x2, rt[:, 3, :, :, :], rt[:, 2, :, :, :], ALU.subtract).then_inc(s_rope, 1)
                for t in range(2):
                    kr = v.tensor_copy(kf[:, t, :, DN:], c[:, t, D_Q + D_KV:].unsqueeze(1).to_broadcast([P, H, DR]))
                kr.then_inc(s_rope, 1)

            slot = lambda t, i: t[:, :, :, i * DH:(i + 1) * DH]
            q_and_k = ((qf, slot(qs, 0), slot(qs, 2), slot(qs, 5)), (kf, slot(ks, 0), slot(ks, 1), slot(ks, 4)))

            def split_first(nb):
                v.wait_ge(s_rope, 7 * nb + 7)
                v.wait_ge(s_qkv, 3 * nb + 3)
                for full, p0, p1, p2 in q_and_k:
                    v.tensor_copy(p0, full).then_inc(s_split, 1)
                v.wait_ge(s_split, 8 * nb + 2)
                for full, p0, p1, p2 in q_and_k:
                    v.tensor_tensor(full, full, p0, ALU.subtract).then_inc(s_split, 1)

            def split_second(nb):
                v.wait_ge(s_split, 8 * nb + 4)
                for full, p0, p1, p2 in q_and_k:
                    v.tensor_copy(p1, full).then_inc(s_split, 1)
                v.wait_ge(s_split, 8 * nb + 6)
                for full, p0, p1, p2 in q_and_k:
                    v.tensor_tensor(p2, full, p1, ALU.subtract).then_inc(s_split, 1)

            def turned(nb):
                for f in range(1, 8, 2):
                    v.wait_ge(s_tr, 8 * nb + f + 1)
                    v.tensor_copy(qbuf[f // 4][2][0:SLOT, 4 * (f % 4):4 * (f % 4) + 4, :].rearrange("p h t -> p (h t)"),
                                  ring[f % 3][0:SLOT, :].bitcast(BF16)).then_inc(s_evD, 1)

            def maxima(nb):
                for f in range(12):
                    v.wait_ge(s_s, 12 * nb + f + 1)
                    i = 0 if f < 4 else 1
                    nh = 4 if i == 0 else 2
                    h0 = 4 * f if i == 0 else 2 * (f - 4)
                    v.tensor_reduce(mx[:, i, h0:h0 + nh], ring[f % 3][:, :].rearrange("p (n k) -> p n k", n=nh),
                                    AX.X, ALU.max).then_inc(s_mx, 1)
                v.wait_ge(s_mx, 12 * (nb + 1))
                v.tensor_scalar(nm[:, :, 0, :], mx[:, :, :], -1.0, None, ALU.mult).then_inc(s_nm, 1)
                v.wait_ge(s_nm, 2 * nb + 1)
                v.scalar_tensor_tensor(out=nm[:, :, 1, :], in0=mx[:, :, :], scalar=-1.0, in1=nm[:, :, 0, :],
                                       op0=ALU.mult, op1=ALU.subtract).then_inc(s_nm, 1)

            def normalize(nb, hg):
                n = 4 * nb + hg
                v.wait_ge(s_y, n + 1)
                if n >= 1:
                    v.wait_ge(s_yn, n)
                bank = ring[3][:, 0:8 * 51].rearrange("p (x s d) -> p x d s", x=8, s=3)
                v.tensor_reduce(ys[:, :, :], bank, AX.X, ALU.add).then_inc(s_yst, 1)
                v.wait_ge(s_yst, 2 * n + 1)
                v.reciprocal(yr[:, :], ys[:, :, DH]).then_inc(s_yst, 1)
                v.wait_ge(s_yst, 2 * n + 2)
                for i in range(2):
                    last = v.tensor_tensor(y[:, i, 4 * hg:4 * hg + 4, :], ys[:, 4 * i:4 * i + 4, 0:DH],
                                           yr[:, 4 * i:4 * i + 4].unsqueeze(2).to_broadcast([P, 4, DH]),
                                           ALU.mult)
                last.then_inc(s_yn, 1)

            def split_probs(nb, *odd):
                for f in odd:
                    n = 12 * nb + f
                    v.wait_ge(s_e, n + 1)
                    if n >= NP:
                        v.wait_ge(s_y, (n - NP) // 3 + 1)
                    v.tensor_copy(ph[:, n % NP, :], exps(n)).then_inc(s_phs[1], 1)
                    if nb % 2:
                        v.wait_ge(s_phs[1], n // 2 + 1)
                        v.tensor_tensor(pl[:, n % NP, :], exps(n), ph[:, n % NP, :],
                                        ALU.subtract).then_inc(s_pls[1], 1)

            def y_lo(nb):
                v.wait_ge(s_yh, nb + 1)
                if nb >= 1:
                    v.wait_ge(s_ao, nb)
                sub(yl[:, :, :], ring[3][:, :].rearrange("p (k t) -> p k t", k=KD), yh[:, :, :]).then_inc(s_yl, 1)

            seg = (slice(0, D_Q), slice(D_Q, D_Q + D_KV))
            for g in range(G):
                fill = MID[g]
                b0, b1 = 2 * g, 2 * g + 1
                tile1 = lambda t: gated(T0 * G + g * T1 + t, bank_of(g, t, 1), P)
                fill1 = lambda t: tile1(t) if t < fill else None
                if g == 0:
                    bias_latents(0)
                norm_latents(b0)
                fill1(0)
                affine_latents(b0)
                fill1(1)
                bias_qk(b0)
                fill1(2)
                bias_v(b0)
                rotate(b0)
                fill1(3)
                split_first(b0)
                fill1(4)
                split_second(b0)
                for t in range(5, fill):
                    fill1(t)
                turned(b0)
                bias_latents(b1)
                maxima(b0)
                norm_latents(b1)
                affine_latents(b1)
                split_probs(b0, 1)
                bias_qk(b1)
                split_probs(b0, 3)
                normalize(b0, 0)
                split_probs(b0, 5)
                bias_v(b1)
                rotate(b1)
                split_probs(b0, 7)
                split_first(b1)
                split_probs(b0, 9)
                normalize(b0, 1)
                split_second(b1)
                split_probs(b0, 11)
                normalize(b0, 2)
                turned(b1)
                normalize(b0, 3)
                y_lo(b0)
                t = MID[g]
                tile1(t)
                maxima(b1)
                tile1(t + 1)
                tile1(t + 2)
                split_probs(b1, 1, 3)
                normalize(b1, 0)
                split_probs(b1, 5, 7)
                normalize(b1, 1)
                split_probs(b1, 9, 11)
                normalize(b1, 2)
                tile1(t + 3)
                normalize(b1, 3)
                tile1(REST[g])
                y_lo(b1)
                for t in range(REST[g] + 1, T1):
                    tile1(t)
                    if g < G - 1 and t == LN_AT1:
                        v.wait_ge(s_vsp, 8 * (g + 1))
                        v.wait_ge(s_ao, 2 * (g + 1))
                        ln_centre(G + g + 1)
                    if g < G - 1 and t in (LN_AT1 + 2, LN_AT1 + 3):
                        i = 2 * (t - LN_AT1 - 2)
                        ln_inverse(G + g + 1, i, i + 1)
                        if i:
                            ln_scale(G + g + 1)
                if g < G - 1:
                    ln_lo(G + g + 1)
                    bias_latents(b1 + 1)
                v.wait_ge(s_dn, T0 * G + T1 * (g + 1))
                for j in range(KD):
                    last = v.scalar_tensor_tensor(out=xg(g)[:, j, :], in0=acc[:, j, :], scalar=bout[:, j:j + 1],
                                                  in1=xg(g)[:, j, :], op0=ALU.add, op1=ALU.add)
                last.then_inc(s_res, 1)


def _layouts(i):
    import numpy as np

    a = {k: np.asarray(v) for k, v in i.items()}
    f = np.float32
    perm = np.concatenate([np.arange(0, D, 2), np.arange(1, D, 2)])

    def rows2(w):
        return w.reshape(P, KD, -1)

    def tiles(w, n):
        full = np.zeros((n * P, w.shape[1]), f)
        full[:w.shape[0]] = w
        return full.reshape(n, P, -1).transpose(1, 0, 2)

    flat = lambda parts: np.ascontiguousarray(np.concatenate([p.reshape(P, -1) for p in parts], 1))
    ew = lambda w: w.reshape(N_EXP * E_FF, D).T
    w0 = flat([rows2(a["L0_attn_Wq"].T), rows2(a["L0_attn_Wk"].T), rows2(a["L0_attn_Wv"].T),
               tiles(a["L0_attn_Wo"].T[:, perm], KD),
               rows2(a["L0_ffn_shared_wg"].T), rows2(a["L0_ffn_shared_wu"].T),
               tiles(a["L0_ffn_shared_wd"].T[:, perm], ST),
               rows2(ew(a["L0_ffn_exp_wg"])), rows2(ew(a["L0_ffn_exp_wu"])),
               tiles(a["L0_ffn_exp_wd"].transpose(0, 2, 1).reshape(N_EXP * E_FF, D)[:, perm], XT)])
    dn = np.zeros((D, 256), f)
    dn[:, :D_Q] = a["L1_attn_W_d_q"].T
    dn[:, D_Q:C_W] = a["L1_attn_W_d_kv"].T
    kv = np.arange(D + H * DN).reshape(H, DN + DH)
    kv = np.concatenate([kv[:, :DN].ravel(), kv[:, DN:].ravel()])
    wa = flat([rows2(dn), tiles(a["L1_attn_W_u_q"].T, 1), tiles(a["L1_attn_W_u_kv"][kv].T, 1),
               tiles(a["L1_attn_W_o"].T[:, perm], KD)])
    lng = np.zeros((P, 4), f)
    lng[:D_Q, 0], lng[:D_Q, 1] = a["L1_attn_q_norm_g"], a["L1_attn_q_norm_b"]
    lng[:, 2], lng[:, 3] = a["L1_attn_kv_norm_g"], a["L1_attn_kv_norm_b"]
    order = np.array([2 * ((t // 2) * P + p) + t % 2 for t in range(T1) for p in range(P)])
    up = lambda w: w[order].T.reshape(P, 4, QW)
    down = a["L1_ffn_down_W_packed"].T[:, perm].reshape(8, P, D).transpose(1, 0, 2).reshape(P, 4, QW)
    q4 = np.concatenate([up(a["L1_ffn_gate_W_packed"]), up(a["L1_ffn_up_W_packed"]), down], 1)
    ups = lambda w: np.repeat(w[order].T, 16, 0).reshape(P, 4, QW)
    downs = np.repeat(a["L1_ffn_down_scales"].T[:, perm], 16, 0).reshape(8, P, D).transpose(1, 0, 2).reshape(P, 4, QW)
    s4 = np.concatenate([ups(a["L1_ffn_gate_scales"]), ups(a["L1_ffn_up_scales"]), downs], 1)

    bf16 = lambda c: (c.view(np.uint32) >> 16).astype(np.uint16)
    sel = np.zeros((P, N_EXP * E_FF), f)
    for e in range(N_EXP):
        sel[[e, 32 + e], e * E_FF:(e + 1) * E_FF] = 1
    masks = np.zeros((2, P, P), f)
    masks[0][np.triu_indices(P, 1)] = MASKED
    masks[1][np.tril_indices(P, -1)] = MASKED
    inv = ((1.0 / 10000.0) ** (np.arange(0, DR, 2, dtype=f) / DR)).astype(f)
    angle = np.arange(H, dtype=f)[:, None] * inv[None, :]
    rot = np.broadcast_to(np.stack([np.cos(angle), np.sin(angle)]).astype(f), (P, 2, H, 4))
    tie = np.broadcast_to((np.arange(N_EXP)[None, :] < np.arange(N_EXP)[:, None]).astype(f), (P, N_EXP, N_EXP))
    return {
        "xT": a["L0_attn_x"].reshape(TOKENS, P, KD).transpose(1, 2, 0), "w0": w0, "gateT": rows2(a["L0_ffn_gate_w"].T),
        "wa": wa, "biasc": np.concatenate([a["L1_attn_b_d_q"], a["L1_attn_b_d_kv"]]), "biasq": a["L1_attn_b_u_q"],
        "biaskv": a["L1_attn_b_u_kv"][kv], "lng": lng, "bo": a["L1_attn_b_o"].reshape(P, KD),
        "ones_c": np.full((P, P), 1.0 / D, f), "sel_c": sel, "ident_c": np.eye(P, dtype=f),
        "identb_c": bf16(np.eye(P, dtype=f)), "mask_c": bf16(masks), "rot_c": rot, "tie_c": tie, "q4": q4, "s4": s4,
    }


def kernel(**inputs):
    import numpy as np
    import concourse.bacc as bacc
    from concourse.bass_utils import run_bass_kernel_spmd

    nc = bacc.Bacc("TRN2", target_bir_lowering=False, num_devices=1)
    arrays, args = {}, {}
    for name, a in _layouts(inputs).items():
        a = np.ascontiguousarray(a)
        arrays[name] = a
        args[name] = nc.dram_tensor(name, a.shape, mybir.dt.from_np(a.dtype), kind="ExternalInput").ap()
    args["out"] = nc.dram_tensor("out", (P, KD, TOKENS), F32, kind="ExternalOutput").ap()
    args["x1s"] = nc.dram_tensor("x1s", (P, KD, TOKENS), F32, kind="Internal").ap()
    args["w4s"] = nc.dram_tensor("w4s", (2, P, 3 * KD * MLP), F32, kind="Internal").ap()
    transformer_blocks(nc, **args)
    r = run_bass_kernel_spmd(nc, [arrays], core_ids=[0])
    o = r.results[0]["out"]
    return np.ascontiguousarray(o.transpose(2, 0, 1)).reshape(BATCHES, SEQ, D)
```
